# Optimizing a Trainium2 kernel written in Bass

```python
import numpy as np
import jax
import jax.numpy as jnp

def _softmax(x, axis=-1):
    return jax.nn.softmax(x, axis=axis)

def _gelu(x):
    return jax.nn.gelu(x, approximate=True)

def _silu(x):
    return jax.nn.silu(x)

def _sigmoid(x):
    return jax.nn.sigmoid(x)

def _layernorm(x, axis=-1, eps=1e-05):
    m = jnp.mean(x, axis=axis, keepdims=True)
    v = jnp.var(x, axis=axis, keepdims=True)
    return (x - m) / jnp.sqrt(v + eps)

def _scatter_add(tgt, idx, src, axis=0):
    return tgt.at[idx].add(src)

def _segment_sum(src, seg, n):
    return jax.ops.segment_sum(src, seg, n)
kernel_name = 'mk_gnn_ffn_d2_gnn_r8_f6a076'

def setup_inputs(seed: int=0):
    np.random.seed(seed)
    _w = jnp.asarray

    def _rec_inputs():
        import jax
        import jax.numpy as jnp
        _gk = jax.random.key(seed)
        x = -0.0002117 + 1 * jax.random.normal(jax.random.fold_in(_gk, 1), (1250, 512), jnp.float32)
        src = jax.random.randint(jax.random.fold_in(_gk, 2), (40000,), 0, 1250, jnp.int32)
        dst = jnp.minimum((1250 * jax.random.uniform(jax.random.fold_in(_gk, 3), (40000,)) ** 2.0).astype(jnp.int32), 9999)
        _o = jnp.argsort(dst, stable=True)
        src = src[_o]
        dst = dst[_o]
        return (x, src, dst)
    x, src, dst = _rec_inputs()

    def _L0_gnn_setup():
        import jax, jax.numpy as jnp
        import numpy as np
        N, E, H, D_IN, D_PRIME = (6250, 100000, 8, 512, 64)

        def _segment_softmax(scores, seg, num_segments):
            smax = jax.ops.segment_max(scores, seg, num_segments=num_segments)
            ex = jnp.exp(scores - smax[seg])
            denom = jax.ops.segment_sum(ex, seg, num_segments=num_segments)
            return ex / denom[seg]
        key = jax.random.key(seed)
        ks = jax.random.split(key, 6)
        x = jax.random.normal(ks[0], (N, D_IN), dtype=jnp.float32)
        edge_index = jax.random.randint(ks[1], (2, E), 0, N)
        Ws = jax.random.normal(ks[2], (H, D_IN, D_PRIME), dtype=jnp.float32) * 0.05
        Wb = jax.random.normal(ks[3], (H, D_PRIME), dtype=jnp.float32) * 0.05
        a_w = jax.random.normal(ks[4], (H, 2 * D_PRIME), dtype=jnp.float32) * 0.05
        a_b = jax.random.normal(ks[5], (H,), dtype=jnp.float32) * 0.05
        return dict(x=x, edge_index=edge_index, Ws=Ws, Wb=Wb, a_w=a_w, a_b=a_b)
    _L0_gnn_all = _L0_gnn_setup()
    _L0_gnn_in = {k: v for k, v in _L0_gnn_all.items() if k in ('Ws', 'Wb', 'a_w', 'a_b')}
    del _L0_gnn_all

    def _L0_ffn_setup():
        import jax, jax.numpy as jnp
        import numpy as np
        B, S, D, E, O = (1024, 256, 512, 16, 512)
        key = jax.random.key(seed)
        k_x, k_wg, k_bg, k_we, k_be = jax.random.split(key, 5)
        scale_g = 1.0 / np.sqrt(D)
        scale_e = 1.0 / np.sqrt(D)
        return {'x': jax.random.normal(k_x, (B, S, D), dtype=jnp.float32), 'Wg': jax.random.uniform(k_wg, (D, E), jnp.float32, -scale_g, scale_g), 'bg': jax.random.uniform(k_bg, (E,), jnp.float32, -scale_g, scale_g), 'We': jax.random.uniform(k_we, (E, D, O), jnp.float32, -scale_e, scale_e), 'be': jax.random.uniform(k_be, (E, O), jnp.float32, -scale_e, scale_e)}
    _L0_ffn_all = _L0_ffn_setup()
    _L0_ffn_in = {k: v for k, v in _L0_ffn_all.items() if k in ('Wg', 'bg', 'We', 'be')}
    del _L0_ffn_all

    def _L1_gnn_setup():
        import jax, jax.numpy as jnp
        import numpy as np
        N_NODES = 6250
        N_EDGES = 50000
        IN_DIM = 512
        OUT_DIM = 512
        key = jax.random.key(seed)
        k1, k2, k3, k4 = jax.random.split(key, 4)
        x = jax.random.normal(k1, (N_NODES, IN_DIM), dtype=jnp.float32)
        edge_index = jax.random.randint(k2, (2, N_EDGES), 0, N_NODES, dtype=jnp.int64)
        W = jax.random.normal(k3, (OUT_DIM, IN_DIM), dtype=jnp.float32) / np.sqrt(IN_DIM)
        b = jax.random.normal(k4, (OUT_DIM,), dtype=jnp.float32) * 0.01
        return {'x': x, 'edge_index': edge_index, 'W': W, 'b': b}
    _L1_gnn_all = _L1_gnn_setup()
    _L1_gnn_in = {k: v for k, v in _L1_gnn_all.items() if k in ('W', 'b')}
    del _L1_gnn_all

    def _L1_ffn_setup():
        import jax, jax.numpy as jnp
        import numpy as np
        B, S, H, E, F = (4, 256, 512, 8, 512)
        key = jax.random.key(seed)
        k = jax.random.split(key, 7)
        x = jax.random.normal(k[0], (B, S, H), dtype=jnp.float32)
        Wr = jax.random.normal(k[1], (H, E), dtype=jnp.float32) / np.sqrt(H)
        br = jnp.zeros((E,), dtype=jnp.float32)
        W1 = jax.random.normal(k[2], (E, H, F), dtype=jnp.float32) / np.sqrt(H)
        b1 = jnp.zeros((E, F), dtype=jnp.float32)
        W2 = jax.random.normal(k[3], (E, F, H), dtype=jnp.float32) / np.sqrt(F)
        b2 = jnp.zeros((E, H), dtype=jnp.float32)
        return {'x': x, 'Wr': Wr, 'br': br, 'W1': W1, 'b1': b1, 'W2': W2, 'b2': b2}
    _L1_ffn_all = _L1_ffn_setup()
    _L1_ffn_in = {k: v for k, v in _L1_ffn_all.items() if k in ('Wr', 'br', 'W1', 'b1', 'W2', 'b2')}
    del _L1_ffn_all
    return {'x': x, 'src': src, 'dst': dst, 'L0_gnn_Ws': _L0_gnn_in['Ws'], 'L0_gnn_Wb': _L0_gnn_in['Wb'], 'L0_gnn_a_w': _L0_gnn_in['a_w'], 'L0_gnn_a_b': _L0_gnn_in['a_b'], 'L0_ffn_Wg': _L0_ffn_in['Wg'], 'L0_ffn_bg': _L0_ffn_in['bg'], 'L0_ffn_We': _L0_ffn_in['We'], 'L0_ffn_be': _L0_ffn_in['be'], 'L1_gnn_W': _L1_gnn_in['W'], 'L1_gnn_b': _L1_gnn_in['b'], 'L1_ffn_Wr': _L1_ffn_in['Wr'], 'L1_ffn_br': _L1_ffn_in['br'], 'L1_ffn_W1': _L1_ffn_in['W1'], 'L1_ffn_b1': _L1_ffn_in['b1'], 'L1_ffn_W2': _L1_ffn_in['W2'], 'L1_ffn_b2': _L1_ffn_in['b2']}

def reference(x, src, dst, L0_gnn_Ws, L0_gnn_Wb, L0_gnn_a_w, L0_gnn_a_b, L0_ffn_Wg, L0_ffn_bg, L0_ffn_We, L0_ffn_be, L1_gnn_W, L1_gnn_b, L1_ffn_Wr, L1_ffn_br, L1_ffn_W1, L1_ffn_b1, L1_ffn_W2, L1_ffn_b2):
    import jax
    import jax.numpy as jnp

    def _L0_gnn_ref(x, edge_index, Ws, Wb, a_w, a_b):
        import jax, jax.numpy as jnp
        import numpy as np
        N, E, H, D_IN, D_PRIME = (6250, 100000, 8, 512, 64)

        def _segment_softmax(scores, seg, num_segments):
            smax = jax.ops.segment_max(scores, seg, num_segments=num_segments)
            ex = jnp.exp(scores - smax[seg])
            denom = jax.ops.segment_sum(ex, seg, num_segments=num_segments)
            return ex / denom[seg]
        v_src, v_tgt = (edge_index[0], edge_index[1])
        n = x.shape[0]
        outs = []
        for h in range(Ws.shape[0]):
            Wx = x @ Ws[h] + Wb[h]
            d = Wx.shape[-1]
            s = Wx[v_tgt] @ a_w[h, :d] + Wx[v_src] @ a_w[h, d:] + a_b[h]
            s = jax.nn.leaky_relu(s, negative_slope=0.2)
            alpha = _segment_softmax(s, v_tgt, n)
            outs.append(jax.ops.segment_sum(alpha[:, None] * Wx[v_src], v_tgt, num_segments=n))
        return jnp.stack(outs, axis=1).reshape(n, -1)

    def _L0_ffn_ref(x, Wg, bg, We, be):
        import jax, jax.numpy as jnp
        import numpy as np
        B, S, D, E, O = (1024, 256, 512, 16, 512)
        scores = jax.nn.softmax(jnp.mean(x, axis=1) @ Wg + bg, axis=-1)
        idx = jnp.argmax(scores, axis=-1)
        gate = jnp.take_along_axis(scores, idx[:, None], axis=-1)
        W_sel = We[idx]
        b_sel = be[idx]
        y = jnp.einsum('bsd,bdo->bso', x, W_sel) + b_sel[:, None, :]
        return gate[:, :, None] * y

    def _L1_gnn_ref(x, edge_index, W, b):
        import jax, jax.numpy as jnp
        import numpy as np
        N_NODES = 6250
        N_EDGES = 50000
        IN_DIM = 512
        OUT_DIM = 512
        n = x.shape[0]
        loops = jnp.arange(n, dtype=edge_index.dtype)
        row = jnp.concatenate([edge_index[0], loops])
        col = jnp.concatenate([edge_index[1], loops])
        deg = jax.ops.segment_sum(jnp.ones(row.shape[0], dtype=x.dtype), row, num_segments=n)
        dis = jax.lax.rsqrt(deg)
        norm = dis[row] * dis[col]
        h = x @ W.T + b
        out = jax.ops.segment_sum(norm[:, None] * h[row], col, num_segments=n)
        return jax.nn.relu(out)

    def _L1_ffn_ref(x, Wr, br, W1, b1, W2, b2):
        import jax, jax.numpy as jnp
        import numpy as np
        B, S, H, E, F = (4, 256, 512, 8, 512)
        b, s, h = x.shape
        xt = x.reshape(-1, h)
        logits = xt @ Wr + br
        probs = jax.nn.softmax(logits, axis=-1)
        G = jnp.max(probs, axis=-1)
        idx = jnp.argmax(probs, axis=-1)
        h1 = jax.nn.relu(jnp.einsum('nh,ehf->nef', xt, W1) + b1)
        eo = jnp.einsum('nef,efh->neh', h1, W2) + b2
        Eout = jnp.take_along_axis(eo, idx[:, None, None], axis=1)[:, 0, :]
        y = G[:, None] * Eout
        return y.reshape(b, s, h)
    edge_index = jnp.stack([src, dst])
    x = x + _L0_gnn_ref(_layernorm(x, axis=-1), edge_index, L0_gnn_Ws, L0_gnn_Wb, L0_gnn_a_w, L0_gnn_a_b)
    x = x + _L0_ffn_ref(_layernorm(x, axis=-1)[None], L0_ffn_Wg, L0_ffn_bg, L0_ffn_We, L0_ffn_be)[0]
    x = x + _L1_gnn_ref(_layernorm(x, axis=-1), edge_index, L1_gnn_W, L1_gnn_b)
    x = x + _L1_ffn_ref(_layernorm(x, axis=-1)[None], L1_ffn_Wr, L1_ffn_br, L1_ffn_W1, L1_ffn_b1, L1_ffn_W2, L1_ffn_b2)[0]
    return x

_drawn_inputs = setup_inputs


def setup_inputs(seed=0):
    import zlib

    import numpy as np

    out = dict(_drawn_inputs(seed))
    spreads = {'L1_ffn_br': (0.0, 0.1), 'L1_ffn_b1': (0.0, 0.311), 'L1_ffn_b2': (0.0, 0.1)}
    factors = {'L0_gnn_a_b': 4.349, 'L0_ffn_be': 6.353, 'L1_gnn_b': 2.976}
    for name, (base, spread) in spreads.items():
        noise = np.random.default_rng([zlib.crc32(name.encode()), seed]).standard_normal(out[name].shape)
        drawn = base * np.exp(spread * noise) if base else spread * noise
        out[name] = jnp.asarray(drawn.astype(out[name].dtype))
    for name, factor in factors.items():
        out[name] = (out[name] * factor).astype(out[name].dtype)
    return out
```

```python
import numpy as np
import concourse.bass as bass
from concourse import mybir
from contextlib import ExitStack

F32 = mybir.dt.float32
F16 = mybir.dt.float16
I32 = mybir.dt.int32
ALU = mybir.AluOpType
ACT = mybir.ActivationFunctionType
AX = mybir.AxisListType

P = 128
NODES, D = 1250, 512
T = (NODES + P - 1) // P
NP = T * P
LAST = NODES - (T - 1) * P
K = D // P

EDGES = 40000
CH = 3
GE = CH * P
NG = (EDGES + GE - 1) // GE
GLAST = EDGES - (NG - 1) * GE
WN = 32
NW = NP // WN
RW = WN * T
NPAIR = NG + NW - 1
LB = 8
LC = LB * CH
NB = NPAIR // LB
MAXPASS = (NG * NW + NPAIR - 1) // NPAIR
RR, RS = 4, 4

H, F = 8, 64
FE = F + 1
E0, E1 = 16, 8
NT = (NP + E1 * (P - 1)) // P
RZ = 4
EPS = 1e-5
SLOPE = 0.2


def gnn_ffn_kernel(nc, x_d, src_d, dst_d, Ws_d, Wb_d, aw_d, ab_d, Wg_d, bg_d, We_d, be_d, gW_d, gb_d,
                   Wr_d, br_d, W1_d, b1_d, W2_d, b2_d, out_d):
    ctx = ExitStack()
    with ctx:
        def sb(name, shape, dt=F32):
            return ctx.enter_context(nc.sbuf_tensor(name, shape, dt))

        sems = {}

        def sem(name):
            if name not in sems:
                sems[name] = ctx.enter_context(nc.semaphore(name))
            return sems[name]

        def carve(region, at, shape, dt=F32):
            n = int(np.prod(shape))
            words = n if dt in (F32, I32) else (n + 1) // 2
            v = region[:, at:at + words]
            if dt != F32:
                v = v.bitcast(dt)
            if len(shape) > 1:
                names = " ".join(f"a{i}" for i in range(len(shape)))
                v = v.rearrange(f"p ({names}) -> p {names}", **{f"a{i}": s for i, s in enumerate(shape)})
            return v, at + words

        x = sb("x", [P, T, D])
        ident = sb("ident", [P, P])
        ident16 = sb("ident16", [P, P], F16)
        tri = sb("tri", [P, P])
        ones = sb("ones", [P, P])
        zero16 = sb("zero16", [P, 400], F16)
        xh_ring = sb("xh_ring", [P, 2, D])
        xT_ring = sb("xT_ring", [P, 2, K, P])
        gb_bc = sb("gb_bc", [P, D])
        be_bc = sb("be_bc", [P, D])
        num = sb("num", [P, H, FE])
        Wg = sb("Wg", [P, K, E0])
        Wr = sb("Wr", [P, K, E1])
        bg = sb("bg", [1, E0])
        br_bc = sb("br_bc", [P, E1])
        st = sb("st", [P, 2, 6])
        mv = sb("mv", [P, 2, 2])
        ve = sb("ve", [P, 2])
        sd = sb("sd", [P, 2])
        rs = sb("rs", [P, 2])
        deg = sb("deg", [P, T])
        dis = sb("dis", [P, T])
        iota8 = sb("iota8", [P, E1])
        iota16 = sb("iota16", [P, E0])
        small = sb("small", [P, 1536])

        mid = sb("mid", [P, E1 * K * D])
        C, o = carve(mid, 0, [T, NP], F16)
        gWT, o = carve(mid, o, [K, D])
        free0 = o
        hp, o = carve(mid, o, [T, 2, D], F16)
        We, o = carve(mid, o, [K, D])
        Wx, o = carve(mid, free0, [T, H, FE])
        raw0, o = carve(mid, o, [T, 2, FE])
        W2, _ = carve(mid, 0, [E1, K, D])

        big = sb("big", [P, E1 * K * D])
        src_i, o = carve(big, 0, [GE], I32)
        dst_i, o = carve(big, o, [GE], I32)
        lo_i, o = carve(big, o, [GE], I32)
        hi_i, o = carve(big, o, [GE], I32)
        w_i, o = carve(big, o, [GE], I32)
        lo_f, o = carve(big, o, [GE])
        q_f, o = carve(big, o, [GE])
        iotaL, o = carve(big, o, [P, LC], F16)
        iotaR, o = carve(big, o, [RW], F16)
        L_ring, o = carve(big, o, [2, P, LC], F16)
        R_ring, o = carve(big, o, [RR, CH, RW], F16)
        stage, o = carve(big, o, [RS, T, WN], F16)
        loT, o = carve(big, o, [NPAIR * CH], F16)
        qT, o = carve(big, o, [NPAIR * CH])
        iotaK, o = carve(big, o, [NPAIR])
        from_, o = carve(big, o, [NPAIR])
        inside, o = carve(big, o, [NPAIR])
        tv, o = carve(big, o, [NPAIR])
        wneg, o = carve(big, o, [NPAIR])
        wk, o = carve(big, o, [NPAIR], I32)
        W0, o = carve(big, o, [K, H, F])
        a_bc, o = carve(big, o, [H, 2 * F])
        Wb_bc, o = carve(big, o, [H, F])
        watmp, o = carve(big, o, [H, F])
        VP, o = carve(big, 0, [T, 2, H, 2, FE], F16)
        nacc, o = carve(big, o, [T, H, FE])
        W1, _ = carve(big, 0, [E1, K, D])
        yg, _ = carve(big, 0, [T, D])

        aux = sb("aux", [P, T * D])
        thr_bc, _ = carve(aux, 0, [2, NP])
        x2T, _ = carve(aux, 0, [T, K, P])
        xh4, _ = carve(aux, 0, [T, D])
        xp, o = carve(aux, 0, [2, D])
        b1_bc, o = carve(aux, o, [2, D])
        b2_bc, o = carve(aux, o, [2, D])
        h_sb, o = carve(aux, o, [2, D])
        y_sb, o = carve(aux, o, [2, D])
        hT = xh_ring[:, :, :].rearrange("p a (k m) -> p a k m", k=K)

        raw1, o = carve(aux, 2 * NP, [T, 2, FE])
        junk, o = carve(aux, o, [NP], F16)
        work = sb("work", [P, 2 * T * FE + RZ * NP // 2])
        vtmp, o = carve(work, 0, [2, T, FE])
        cz, o = carve(work, o, [RZ, NP], F16)
        thrT, _ = carve(work, 0, [NP])
        hs, o = carve(work, 0, [2, D])
        rtmp, o = carve(work, o, [2, D])
        gW, _ = carve(work, 1812, [K, D])
        zero, _ = carve(work, NP, [1, D])
        raw = [raw0, raw1]

        at = 0
        Wa, at = carve(small, at, [K, 2 * H])
        cb, at = carve(small, at, [2 * H])
        ab_bc, at = carve(small, at, [H])
        sc, at = carve(small, at, [T, 2 * H])
        atb, at = carve(small, at, [T, H])
        thr, at = carve(small, at, [T, H])
        asmax, at = carve(small, at, [H])
        cs, at = carve(small, at, [H])
        zz, at = carve(small, at, [T, H])
        ll, at = carve(small, at, [T, H])
        e1t, at = carve(small, at, [T, H])
        e2t, at = carve(small, at, [T, H])
        d1t, at = carve(small, at, [T, H])
        A1, at = carve(small, at, [T, H])
        A2, at = carve(small, at, [T, H])
        B1, at = carve(small, at, [T, H])
        B2, at = carve(small, at, [T, H])
        grp, at = carve(small, at, [8])
        kt, at = carve(small, at, [MAXPASS])
        npass, at = carve(small, at, [1], I32)
        rden, at = carve(small, at, [H])
        msum, at = carve(small, at, [T, K])
        mean, at = carve(small, at, [K])
        gt, at = carve(small, at, [4, E0])
        gs, at = carve(small, at, [8])
        gidx, at = carve(small, at, [1], I32)
        at = 0
        lg, at = carve(small, at, [T, E1])
        ex, at = carve(small, at, [T, E1])
        mx10, at = carve(small, at, [T])
        G, at = carve(small, at, [T])
        em, at = carve(small, at, [T])
        oh, at = carve(small, at, [T, E1])
        eq, at = carve(small, at, [T, E1])
        tot, at = carve(small, at, [T, E1])
        pre, at = carve(small, at, [T + 1, E1])
        cmp_, at = carve(small, at, [E1, T])
        tl, at = carve(small, at, [E1])
        cum, at = carve(small, at, [E1])
        base, at = carve(small, at, [E1])
        slot, at = carve(small, at, [T, E1])
        pos_f, at = carve(small, at, [T])
        pos, at = carve(small, at, [T], I32)
        tcmp, at = carve(small, at, [NT, E1 - 1])
        te_f, at = carve(small, at, [NT])
        te, at = carve(small, at, [NT], I32)
        iotaM = sb("iotaM", [P, T])
        iotaJ = sb("iotaJ", [P, NT])

        bank = [ctx.enter_context(nc.psum_tensor(f"bank{i}", [P, 512], F32)) for i in range(8)]

        thr_d = nc.dram_tensor("thr_scratch", [H, NP], F32, kind="Internal").ap()
        xp_d = nc.dram_tensor("xperm_scratch", [NT * P, D], F32, kind="Internal").ap()
        yp_d = nc.dram_tensor("yperm_scratch", [NT * P, D], F32, kind="Internal").ap()

        block = ctx.enter_context(nc.Block())

        def at_least(eng, name, value):
            if isinstance(value, int) and value <= 0:
                return
            eng.wait_ge(sem(name), value)

        def bc(ap, shape):
            return ap.unsqueeze(len(ap.shape)).to_broadcast(shape)

        def acc_region(t):
            return bank[t // 3][:, (t % 3) * 2 * FE:(t % 3 + 1) * 2 * FE]

        @block.sync
        def _(sp):
            sp.wait_ge(sem("edge_pads"), 2)
            full = (NG - 1) * GE
            for i_d, i_sb in ((src_d, src_i), (dst_d, dst_i)):
                sp.dma_start(i_sb[0:NG - 1, :], i_d[0:full].rearrange("(g e) -> g e", e=GE)).then_inc(sem("ld_edges"), 16)
                sp.dma_start(i_sb[NG - 1:NG, 0:GLAST], i_d[full:EDGES].rearrange("(g e) -> g e", g=1)).then_inc(sem("ld_edges"), 16)
            for k in range(K):
                sp.dma_start(W0[:, k, :, :], Ws_d[:, k * P:(k + 1) * P, :].rearrange("h p f -> p h f")).then_inc(sem("ld_w0"), 16)
            sp.dma_start(a_bc, aw_d.partition_broadcast(P)).then_inc(sem("ld_w0"), 16)
            sp.dma_start(Wb_bc, Wb_d.partition_broadcast(P)).then_inc(sem("ld_w0"), 16)
            sp.dma_start(ab_bc, ab_d.partition_broadcast(P)).then_inc(sem("ld_w0"), 16)
            sp.wait_ge(sem("x_pad"), 1)
            sp.dma_start(x[:, 0:T - 1, :], x_d[0:(T - 1) * P, :].rearrange("(t p) d -> p t d", p=P)).then_inc(sem("ld_x"), 16)
            sp.dma_start(x[0:LAST, T - 1, :], x_d[(T - 1) * P:NODES, :]).then_inc(sem("ld_x"), 16)
            sp.dma_start(gW, gW_d.rearrange("(k p) i -> p k i", p=P)).then_inc(sem("ld_gw"), 16)
            for dst, src in ((gb_bc[:, :], gb_d.partition_broadcast(P)),
                             (Wg[:, :, :], Wg_d.rearrange("(k p) e -> p k e", p=P)),
                             (Wr[:, :, :], Wr_d.rearrange("(k p) e -> p k e", p=P)),
                             (bg[:, :], bg_d.rearrange("(a e) -> a e", a=1)),
                             (br_bc[:, :], br_d.partition_broadcast(P))):
                sp.dma_start(dst, src).then_inc(sem("ld_w1"), 16)
            sp.wait_ge(sem("zero_set"), 1)
            sp.dma_start(xp_d.rearrange("(j p) d -> p j d", p=P),
                         zero[:, 0:1, :].to_broadcast([P, NT, D])).then_inc(sem("xp_zeroed"), 16)
            sp.wait_ge(sem("thrT_ready"), 3)
            sp.dma_start(thr_d, thrT[0:H, :]).then_inc(sem("thr_out"), 16)
            sp.wait_ge(sem("thr_out"), 16)
            for h in range(H):
                if h >= 2:
                    sp.wait_ge(sem("cz_made"), T * (h - 1))
                sp.dma_start(thr_bc[:, h % 2, :], thr_d[h, :].partition_broadcast(P)).then_inc(sem(f"thr_ld{h % 2}"), 16)
            sp.wait_ge(sem("gate_idx"), 1)
            e = sp.value_load(gidx[0:1, 0:1], min_val=0, max_val=E0 - 1)
            sp.dma_start(We, We_d[bass.ds(e, 1), :, :].rearrange("a (k p) o -> p (a k) o", p=P)).then_inc(sem("ld_we"), 16)
            sp.dma_start(be_bc[:, :], be_d[bass.ds(e, 1), :].rearrange("a o -> (a o)").partition_broadcast(P)).then_inc(sem("ld_we"), 16)
            sp.wait_ge(sem("x2_made"), T)
            for i in range(E1):
                sp.dma_start(W1[:, i, :, :], W1_d[i].rearrange("(k p) f -> p k f", p=P)).then_inc(sem(f"ld_W1"), 16)
            sp.wait_ge(sem("agg_done"), T)
            for i in range(E1):
                sp.dma_start(W2[:, i, :, :], W2_d[i].rearrange("(k p) f -> p k f", p=P)).then_inc(sem(f"ld_W2"), 16)
            sp.wait_ge(sem("te_ready"), 1)
            sp.wait_ge(sem("scattered"), 16 * T)
            for j in range(NT):
                e = sp.value_load(te[0:1, j:j + 1], min_val=0, max_val=E1 - 1)
                if j >= 2:
                    sp.wait_ge(sem("xpT_psum"), j - 1)
                    sp.wait_ge(sem("y_made"), j - 1)
                s = sem(f"ld_xp{j % 2}")
                sp.dma_start(xp[:, j % 2, :], xp_d[j * P:(j + 1) * P, :]).then_inc(s, 16)
                sp.dma_start(b1_bc[:, j % 2, :], b1_d[bass.ds(e, 1), :].rearrange("a o -> (a o)").partition_broadcast(P)).then_inc(s, 16)
                sp.dma_start(b2_bc[:, j % 2, :], b2_d[bass.ds(e, 1), :].rearrange("a o -> (a o)").partition_broadcast(P)).then_inc(s, 16)
            sp.wait_ge(sem("out_done"), 16 * (T + 1))

        @block.gpsimd
        def _(g):
            nc.gpsimd.memset(src_i[96:NG, :], 0).then_inc(sem("edge_pads"), 1)
            nc.gpsimd.memset(dst_i[96:NG, :], NP).then_inc(sem("edge_pads"), 1)
            nc.gpsimd.memset(x[96:P, T - 1, :], 0.0).then_inc(sem("x_pad"), 1)
            g.wait_ge(sem("x_pad"), 1)
            nc.gpsimd.memset(zero[:, 0, :], 0.0).then_inc(sem("zero_set"), 1)
            nc.gpsimd.memset(zero16[:, :], 0.0)
            nc.gpsimd.memset(ident[:, :], 0.0).then_inc(sem("pc"), 1)
            nc.gpsimd.memset(ones[:, :], 1.0).then_inc(sem("pc"), 1)
            g.wait_ge(sem("pc"), 2)
            nc.gpsimd.affine_select(out=ident[:, :], in_=ident[:, :], compare_op=ALU.not_equal, fill=1.0,
                                    base=0, pattern=[[-1, P]], channel_multiplier=1).then_inc(sem("pc"), 1)
            nc.gpsimd.affine_select(out=tri[:, :], in_=ones[:, :], compare_op=ALU.is_gt, fill=0.0,
                                    base=0, pattern=[[1, P]], channel_multiplier=-1)
            kw = dict(allow_small_or_imprecise_dtypes=True, channel_multiplier=0)
            nc.gpsimd.iota(iotaK, [[1, NPAIR]], base=0, **kw)
            nc.gpsimd.iota(iotaR, [[1, RW]], base=1, **kw)
            nc.gpsimd.iota(iotaL, [[1, P], [0, LC]], base=0, **kw)
            nc.gpsimd.iota(iota8[:, :], [[1, E1]], base=-99, **kw)
            nc.gpsimd.iota(iota16[:, :], [[1, E0]], base=-99, **kw)
            nc.gpsimd.iota(iotaM[:, :], [[P, T]], base=0, **kw)
            nc.gpsimd.iota(iotaJ[:, :], [[1, NT]], base=0, **kw)
            nc.gpsimd.memset(Wx[:, :, :, F:FE], 1.0)
            nc.gpsimd.memset(C.bitcast(F32), 0.0)
            g.wait_ge(sem("pc"), 3)
            nc.gpsimd.tensor_copy(ident16[:, :], ident[:, :]).then_inc(sem("consts"), 1)

            g.wait_ge(sem("asmax"), 1)
            nc.gpsimd.partition_all_reduce(cs, asmax, P, bass.bass_isa.ReduceOp.max).then_inc(sem("cs_ready"), 1)

            g.wait_ge(sem("npass_ready"), 1)
            n = g.value_load(npass[0:1, 0:1], min_val=1, max_val=MAXPASS)

            def add_pairs(base, off):
                for k in range(2 * LB):
                    w = g.value_load(wk[0:1, bass.ds(off + k, 1)], min_val=0, max_val=NW - 1)
                    g.wait_ge(sem("staged"), base + (k + 1))
                    at_least(g, "added", base + k)
                    if not isinstance(base, int):
                        g.sem_inc(sem("pool_step"), 1)
                    dst = C[:, :, bass.ds(w * WN, WN)]
                    nc.gpsimd.tensor_tensor(dst, dst, stage[:, k % RS, :, :], ALU.add).then_inc(sem("added"), 1)

            g.wait_ge(sem("tables"), 1)
            for i in range(NB // 2):
                add_pairs(i * 2 * LB, i * 2 * LB)
            with g.If(n > 1):
                with g.Fori(1, n) as p:
                    g.wait_ge(sem("tables"), p + 1)
                    g.sem_inc(sem("pool_step"), 1)
                    with g.Fori(0, NB // 2) as i:
                        add_pairs(p * NPAIR + i * 2 * LB, i * 2 * LB)
                g.wait_ge(sem("added"), 2 * NPAIR)
            g.wait_ge(sem("added"), NPAIR)
            g.sem_inc(sem("hist_done"), 1)

            g.wait_ge(sem("exps"), 1)
            g.wait_ge(sem("evacA"), T)

            def value(i):
                h, b = divmod(i, 2)
                if i >= 2:
                    g.wait_ge(sem("v_lo"), i - 1)
                nc.gpsimd.tensor_tensor(vtmp[:, i % 2, :, :], Wx[:, :, h, :],
                                        bc((B1, B2)[b][:, :, h], [P, T, FE]), ALU.mult).then_inc(sem("v_made"), 1)

            def low(i):
                h, b = divmod(i, 2)
                g.wait_ge(sem("v_hi"), i + 1)
                nc.gpsimd.tensor_tensor(VP[:, :, 1, h, b, :], vtmp[:, i % 2, :, :], VP[:, :, 0, h, b, :],
                                        ALU.subtract).then_inc(sem("v_lo"), 1)

            def numer(h):
                g.wait_ge(sem("raw_made"), 4 * (h + 1))
                r = raw[h % 2]
                nc.gpsimd.tensor_tensor(r[:, :, 0, :], r[:, :, 0, :], bc(A1[:, :, h], [P, T, FE]), ALU.mult).then_inc(sem("pn"), 1)
                nc.gpsimd.tensor_tensor(r[:, :, 1, :], r[:, :, 1, :], bc(A2[:, :, h], [P, T, FE]), ALU.mult).then_inc(sem("pn"), 1)
                g.wait_ge(sem("pn"), 2 * (h + 1))
                nc.gpsimd.tensor_tensor(nacc[:, :, h, :], r[:, :, 0, :], r[:, :, 1, :], ALU.subtract).then_inc(sem("nacc_made"), 1)

            g.wait_ge(sem("thr_out"), 16)
            g.wait_ge(sem("xp_zeroed"), 16)
            value(0)
            for i in range(2 * H):
                if i + 1 < 2 * H:
                    value(i + 1)
                low(i)
                if i >= 7 and i % 2:
                    numer(i // 2 - 3)
            for h in range(H - 3, H):
                numer(h)

            g.wait_ge(sem("U_done"), T)
            g.wait_ge(sem("deg_made"), T)
            for s in range(T):
                d = C[:, s, s * P:(s + 1) * P]
                last = nc.gpsimd.tensor_tensor(d, d, ident16[:, :], ALU.add)
            last.then_inc(sem("loops"), 1)
            for t in range(T):
                g.wait_ge(sem("h_hi"), t + 1)
                nc.gpsimd.tensor_tensor(hp[:, t, 1, :], hs[:, t % 2, :], hp[:, t, 0, :], ALU.subtract).then_inc(sem("h_lo"), 1)
            for t in range(T):
                g.wait_ge(sem("relu_made"), t + 1)
                nc.gpsimd.tensor_tensor(x[:, t, :], x[:, t, :], rtmp[:, t % 2, :], ALU.add).then_inc(sem("x4_made"), 1)
            g.wait_ge(sem("pos_ready"), 1)
            g.wait_ge(sem("xp_zeroed"), 16)
            for t in range(T):
                nc.gpsimd.indirect_dma_start(xp_d, bass.IndirectOffsetOnAxis(ap=pos[:, t:t + 1], axis=0),
                                             xh4[:, t, :], None).then_inc(sem("scattered"), 16)
            g.wait_ge(sem("y_stored"), 16 * NT)
            for t in range(T):
                nc.gpsimd.indirect_dma_start(yg[:, t, :], None, yp_d,
                                             bass.IndirectOffsetOnAxis(ap=pos[:, t:t + 1], axis=0)).then_inc(sem(f"gathered{t}"), 16)

        @block.scalar
        def _(a):
            act = nc.scalar.activation

            def ln_sqrt(n):
                a.wait_ge(sem("ln_var"), n + 1)
                act(sd[:, n % 2:n % 2 + 1], ve[:, n % 2:n % 2 + 1], ACT.Sqrt).then_inc(sem("ln_sd"), 1)

            def ln_copy(n, b, dst):
                a.wait_ge(sem("xt_psum"), n + 1)
                act(dst, b[:, :].rearrange("p (k m) -> p k m", k=K), ACT.Copy).then_inc(sem("xT_ready"), 1)

            ln_sqrt(0)
            ln_sqrt(1)
            for t in range(T):
                if t >= 2:
                    a.wait_ge(sem("linA"), t - 1)
                ln_copy(t, bank[6 + t % 2], xT_ring[:, t % 2, :, :])
                if t + 2 < T:
                    ln_sqrt(t + 2)
            for k in range(K):
                a.wait_ge(sem("gwT_psum"), k + 1)
                act(gWT[:, k, :], bank[6 + k % 2][:, :], ACT.Copy).then_inc(sem("gwT_ready"), 1)
            for i, n in enumerate((4, 4, 2)):
                a.wait_ge(sem("thrT_psum"), i + 1)
                act(thrT[0:H, i * 512:i * 512 + n * P], bank[5 + i][0:H, 0:n * P], ACT.Copy).then_inc(sem("thrT_ready"), 1)
            a.wait_ge(sem("exp_in"), 1)
            act(A1, e1t, ACT.Exp)
            act(A2, e2t, ACT.Exp)
            act(B1, d1t, ACT.Exp)
            act(B2, d1t, ACT.Exp, scale=SLOPE).then_inc(sem("exps"), 1)

            a.wait_ge(sem("npass_ready"), 1)
            n = a.value_load(npass[0:1, 0:1], min_val=1, max_val=MAXPASS)

            def stage_pairs(base):
                for k in range(2 * LB):
                    a.wait_ge(sem("counted"), base + (k + 1))
                    at_least(a, "added", base + (k + 1 - RS))
                    act(stage[:, k % RS, :, :], bank[k % 2][:, 0:RW].rearrange("p (d s) -> p s d", s=T),
                        ACT.Copy).then_inc(sem("staged"), 1)

            for i in range(NB // 2):
                stage_pairs(i * 2 * LB)
            with a.If(n > 1):
                with a.Fori(1, n) as p:
                    with a.Fori(0, NB // 2) as i:
                        stage_pairs(p * NPAIR + i * 2 * LB)

            def hi(i):
                h, b = divmod(i, 2)
                a.wait_ge(sem("v_made"), i + 1)
                act(VP[:, :, 0, h, b, :], vtmp[:, i % 2, :, :], ACT.Copy).then_inc(sem("v_hi"), 1)

            def raw_copy(h):
                if h >= 2:
                    a.wait_ge(sem("nacc_made"), h - 1)
                for b in range(4):
                    n3 = min(3, T - 3 * b)
                    a.wait_ge(sem("acc_done"), h + 1)
                    act(raw[h % 2][:, 3 * b:3 * b + n3, :, :],
                        bank[b][:, 0:n3 * 2 * FE].rearrange("p (t b f) -> p t b f", b=2, f=FE),
                        ACT.Copy).then_inc(sem("raw_made"), 1)

            def degree(s):
                if s:
                    a.wait_ge(sem("deg_made"), s)
                act(junk, C[:, s, :], ACT.Copy, accum_out=deg[:, s:s + 1]).then_inc(sem("deg_made"), 1)

            a.wait_ge(sem("hist_done"), 1)
            for i in range(2 * H):
                hi(i)
                if i >= 7 and i % 2:
                    raw_copy(i // 2 - 3)
            for h in range(H - 3, H):
                raw_copy(h)
                degree(h - (H - 3))
            for s in range(3, T):
                degree(s)
            for t in range(T):
                ln_sqrt(T + t)
                ln_copy(T + t, bank[t % 2], x2T[:, t, :, :])
            a.wait_ge(sem("dis_in"), 1)
            act(dis[:, :], deg[:, :], ACT.Sqrt).then_inc(sem("dis_sqrt"), 1)
            a.wait_ge(sem("gate_in"), 1)
            act(gt[0:1, 1, :], gt[0:1, 0, :], ACT.Exp, bias=gs[0:1, 0:1], accum_out=gs[0:1, 1:2]).then_inc(sem("gate_exp"), 1)
            for t in range(T + 1):
                if t < T:
                    ln_sqrt(2 * T + t)
                    if t >= 2:
                        a.wait_ge(sem("linC"), t - 1)
                    ln_copy(2 * T + t, bank[t % 2], xT_ring[:, t % 2, :, :])
                if t >= 1:
                    a.wait_ge(sem("hs_made"), t)
                    act(hp[:, t - 1, 0, :], hs[:, (t - 1) % 2, :], ACT.Copy).then_inc(sem("h_hi"), 1)
            for t in range(T + 1):
                if t < T:
                    a.wait_ge(sem("agg_done"), t + 1)
                    if t >= 2:
                        a.wait_ge(sem("x4_made"), t - 1)
                    act(rtmp[:, t % 2, :], bank[6 + t % 2][:, :], ACT.Relu, scale=dis[:, t:t + 1]).then_inc(sem("relu_made"), 1)
                    ln_sqrt(3 * T + t)
                if t >= 1:
                    if t >= 3:
                        a.wait_ge(sem("linD"), t - 2)
                    ln_copy(3 * T + t - 1, bank[(t - 1) % 2], xT_ring[:, (t - 1) % 2, :, :])
            a.wait_ge(sem("rt_in"), 1)
            act(ex, ex, ACT.Exp).then_inc(sem("rt_exp"), 1)

            def xp_copy(j):
                a.wait_ge(sem("xpT_psum"), j + 1)
                if j >= 2:
                    a.wait_ge(sem("m1_done"), j - 1)
                act(xT_ring[:, j % 2, :, :], bank[4 + j % 2][:, :].rearrange("p (k m) -> p k m", k=K),
                    ACT.Copy).then_inc(sem("xpT"), 1)

            def store(j):
                a.wait_ge(sem("y_made"), j + 1)
                a.dma_start(yp_d[j * P:(j + 1) * P, :], y_sb[:, j % 2, :]).then_inc(sem(f"y_st{j % 2}"), 16)

            xp_copy(0)
            for j in range(NT):
                if j + 1 < NT:
                    xp_copy(j + 1)
                a.wait_ge(sem("hT_psum"), j + 1)
                if j >= 2:
                    a.wait_ge(sem("m2_done"), j - 1)
                act(hT[:, j % 2, :, :], bank[j % 2][:, :].rearrange("p (k m) -> p k m", k=K),
                    ACT.Relu).then_inc(sem("hT_ready"), 1)
                if j:
                    store(j - 1)
            store(NT - 1)
            a.wait_ge(sem("y_st0"), 16 * ((NT + 1) // 2))
            a.wait_ge(sem("y_st1"), 16 * (NT // 2))
            a.sem_inc(sem("y_stored"), 16 * NT)
            for t in range(T):
                a.wait_ge(sem("final"), t + 1)
                if t < T - 1:
                    a.dma_start(out_d[t * P:(t + 1) * P, :], yg[:, t, :]).then_inc(sem("out_done"), 16)
                else:
                    a.dma_start(out_d[t * P:NODES, :], yg[0:LAST, t, :]).then_inc(sem("out_done"), 16)
            a.sem_inc(sem("out_done"), 16)

        @block.vector
        def _(v):
            V = nc.vector
            count = [0]

            def link(ins):
                count[0] += 1
                ins.then_inc(sem("dve"), 1)
                v.wait_ge(sem("dve"), count[0])

            def ln_stats(n, xt):
                i = n % 2
                link(V.bn_stats(st[:, i, :], xt))
                link(V.bn_aggr(mv[:, i, :], st[:, i, :]))
                V.tensor_scalar(ve[:, i:i + 1], mv[:, i, 1:2], EPS, None, ALU.add).then_inc(sem("ln_var"), 1)

            def ln_norm(n, xt, dst):
                i = n % 2
                v.wait_ge(sem("ln_sd"), n + 1)
                link(V.reciprocal(rs[:, i:i + 1], sd[:, i:i + 1]))
                if n >= 2:
                    v.wait_ge(sem("xt_psum"), n - 1)
                V.tensor_scalar(dst, xt, mv[:, i, 0:1], rs[:, i:i + 1], ALU.subtract, ALU.mult).then_inc(sem("xh_made"), 1)

            v.wait_ge(sem("consts"), 1)
            v.wait_ge(sem("ld_edges"), 64)
            gp = slice(0, NG)
            V.tensor_scalar(lo_i[gp, :], src_i[gp, :], P - 1, None, ALU.bitwise_and)
            V.tensor_scalar(hi_i[gp, :], src_i[gp, :], 7, None, ALU.logical_shift_right)
            V.tensor_scalar(w_i[gp, :], dst_i[gp, :], 5, None, ALU.logical_shift_right)
            link(V.tensor_scalar(q_f[gp, :], dst_i[gp, :], float(T), 1.0, ALU.mult, ALU.add))
            V.tensor_copy(lo_f[gp, :], lo_i[gp, :])
            V.tensor_tensor(q_f[gp, :], q_f[gp, :], hi_i[gp, :], ALU.add)
            V.tensor_reduce(grp[gp, 0:1], w_i[gp, :], AX.X, ALU.min)
            link(V.tensor_reduce(grp[gp, 1:2], w_i[gp, :], AX.X, ALU.max))
            link(V.tensor_scalar(grp[gp, 2:3], grp[gp, 1:2], float(NW - 1), 1.0, ALU.min, ALU.add))
            V.tensor_tensor(grp[gp, 2:3], grp[gp, 2:3], grp[gp, 0:1], ALU.subtract).then_inc(sem("n_ready"), 1)

            v.wait_ge(sem("ld_w0"), 16 * (K + 3))
            for k in range(K + 1):
                w, dst = (W0[:, k, :, :], Wa[:, k, :]) if k < K else (Wb_bc, cb)
                for i in range(2):
                    link(V.tensor_tensor(watmp, w, a_bc[:, :, i * F:(i + 1) * F], ALU.mult))
                    ins = V.tensor_reduce(dst[:, i * H:(i + 1) * H], watmp, AX.X, ALU.add)
                    link(ins)
            V.tensor_copy(small[0:1, 1501:1502], ones[0:1, 0:1]).then_inc(sem("wa_ready"), 1)

            v.wait_ge(sem("ld_x"), 32)

            def evac_a(t):
                v.wait_ge(sem("linA"), t + 1)
                V.tensor_tensor(Wx[:, t, :, 0:F], bank[2 + t % 2][:, :].rearrange("p (h f) -> p h f", h=H), Wb_bc, ALU.add)
                V.tensor_tensor(sc[:, t, :], bank[4 + t % 2][:, 0:2 * H], cb, ALU.add).then_inc(sem("evacA"), 1)

            for t in range(T + 2):
                if t < T:
                    ln_stats(t, x[:, t, :])
                    ln_norm(t, x[:, t, :], xh_ring[:, t % 2, :])
                if t >= 2:
                    evac_a(t - 2)
            v.wait_ge(sem("evacA"), T)
            link(V.tensor_tensor(atb, sc[:, :, 0:H], ab_bc.unsqueeze(1).to_broadcast([P, T, H]), ALU.add))
            V.tensor_scalar(thr, atb, -1.0, None, ALU.mult).then_inc(sem("thr_made"), 1)
            V.tensor_reduce(asmax, sc[:, :, H:2 * H].rearrange("p t h -> p h t"), AX.X, ALU.max).then_inc(sem("asmax"), 1)
            v.wait_ge(sem("cs_ready"), 1)
            csb = cs.unsqueeze(1).to_broadcast([P, T, H])
            V.tensor_tensor(d1t, sc[:, :, H:2 * H], csb, ALU.subtract)
            link(V.tensor_tensor(zz, atb, csb, ALU.add))
            link(V.scalar_tensor_tensor(ll, zz, SLOPE, zz, ALU.mult, ALU.max))
            V.tensor_tensor(e1t, zz, ll, ALU.subtract)
            V.scalar_tensor_tensor(e2t, zz, SLOPE, ll, ALU.mult, ALU.subtract).then_inc(sem("exp_in"), 1)

            v.wait_ge(sem("rb_psum"), 1)
            V.tensor_copy(grp[gp, 3:4], bank[5][gp, 0:1])
            link(V.tensor_scalar(kt[0:1, :], iotaK[0:1, 0:MAXPASS], float(NPAIR), None, ALU.mult))
            link(V.tensor_scalar(kt[0:1, :], kt[0:1, :], bank[4][0:1, 32:33], None, ALU.is_lt))
            link(V.tensor_reduce(grp[0:1, 6:7], kt[0:1, :], AX.X, ALU.add))
            V.tensor_copy(npass[0:1, :], grp[0:1, 6:7]).then_inc(sem("npass_ready"), 1)
            v.wait_ge(sem("npass_ready"), 1)
            n = v.value_load(npass[0:1, 0:1], min_val=1, max_val=MAXPASS)

            def pair_tables(p):
                V.tensor_tensor(grp[gp, 4:5], grp[gp, 3:4], grp[gp, 2:3], ALU.add)
                V.tensor_tensor(grp[gp, 5:6], grp[gp, 0:1], grp[gp, 3:4], ALU.subtract).then_inc(sem("g1"), 1)
                v.wait_ge(sem("g1"), p + 1)
                V.tensor_scalar(grp[gp, 5:6], grp[gp, 5:6], -float(RW), None, ALU.mult)
                V.tensor_scalar(from_[gp, :], iotaK[gp, :], grp[gp, 3:4], None, ALU.is_ge).then_inc(sem("g2"), 1)
                v.wait_ge(sem("g2"), p + 1)
                V.scalar_tensor_tensor(inside[gp, :], iotaK[gp, :], grp[gp, 4:5], from_[gp, :], ALU.is_lt, ALU.mult)
                V.tensor_scalar(tv[gp, :], iotaK[gp, :], -float(RW), grp[gp, 5:6], ALU.mult, ALU.add).then_inc(sem("g3"), 1)
                v.wait_ge(sem("g3"), p + 1)
                V.tensor_scalar(grp[gp, 3:4], grp[gp, 3:4], -float(NPAIR), None, ALU.add)
                V.tensor_tensor(wneg[gp, :], tv[gp, :], inside[gp, :], ALU.mult).then_inc(sem("picks"), 1)
                v.wait_ge(sem("table_psum"), p + 1)
                V.tensor_scalar(wk[0:1, :], bank[4][0:1, 0:NPAIR], -1.0 / RW, 0.25, ALU.mult, ALU.add)
                V.tensor_copy(loT.rearrange("p (k j) -> p k j", j=CH), bank[2][:, 0:NPAIR * CH].rearrange("p (j k) -> p k j", j=CH))
                V.tensor_copy(qT.rearrange("p (k j) -> p k j", j=CH),
                              bank[3][:, 0:NPAIR * CH].rearrange("p (j k) -> p k j", j=CH)).then_inc(sem("tables"), 1)
                v.wait_ge(sem("tables"), p + 1)

            def onehots(base, off):
                for b in range(2):
                    at_least(v, "counted", base + (b - 1) * LB)
                    lo = loT[:, bass.ds((off + b * LB) * CH, LC)].unsqueeze(1).to_broadcast([P, P, LC])
                    V.tensor_tensor(L_ring[:, b, :, :], iotaL, lo, ALU.is_equal)
                    for k in range(b * LB, (b + 1) * LB):
                        at_least(v, "counted", base + (k + 1 - RR))
                        for j in range(CH):
                            ins = V.tensor_scalar(R_ring[:, k % RR, j, :], iotaR, qT[:, bass.ds(off * CH + (k * CH + j), 1)],
                                                  None, ALU.is_equal)
                        ins.then_inc(sem("onehots"), 1)

            pair_tables(0)
            for i in range(NB // 2):
                onehots(i * 2 * LB, i * 2 * LB)
            with v.If(n > 1):
                with v.Fori(1, n) as p:
                    v.wait_ge(sem("added"), p * NPAIR)
                    pair_tables(p)
                    v.sem_inc(sem("dve_step"), 1)
                    with v.Fori(0, NB // 2) as i:
                        onehots(p * NPAIR + i * 2 * LB, i * 2 * LB)

            v.wait_ge(sem("hist_done"), 1)
            for h in range(H):
                v.wait_ge(sem(f"thr_ld{h % 2}"), 16 * (h // 2 + 1))
                for s in range(T):
                    i = h * T + s
                    if i >= RZ:
                        v.wait_ge(sem("cz_used"), i - RZ + 1)
                    V.scalar_tensor_tensor(cz[:, i % RZ, :], thr_bc[:, h % 2, :], sc[:, s, H + h:H + h + 1],
                                           C[:, s, :], ALU.is_le, ALU.mult).then_inc(sem("cz_made"), 1)
            v.wait_ge(sem("nacc_made"), H)

            def token_sum(t):
                v.wait_ge(sem("xT_ready"), T + t + 1)
                V.tensor_reduce(msum[:, t, :], x2T[:, t, :, :], AX.X, ALU.add)

            for t in range(T):
                v.wait_ge(sem("U_done"), t + 1)
                for g2 in range(2):
                    hh = slice(4 * g2, 4 * g2 + 4)
                    ins = V.tensor_tensor(num[:, hh, :], bank[4 + 2 * (t % 2) + g2][:, 0:4 * FE].rearrange("p (h f) -> p h f", f=FE),
                                          bc(A2[:, t, hh], [P, 4, FE]), ALU.mult)
                ins.then_inc(sem("U_used"), 1)
                v.wait_ge(sem("U_used"), t + 1)
                link(V.tensor_tensor(num[:, :, :], num[:, :, :], nacc[:, t, :, :], ALU.add))
                link(V.tensor_scalar(rden[:, :], num[:, :, F], 1e-30, None, ALU.max))
                link(V.reciprocal(rden[:, :], rden[:, :]))
                link(V.tensor_tensor(num[:, :, 0:F], num[:, :, 0:F], bc(rden, [P, H, F]), ALU.mult))
                xt = x[:, t, :]
                V.tensor_tensor(xt.rearrange("p (h f) -> p h f", f=F), xt.rearrange("p (h f) -> p h f", f=F),
                                num[:, :, 0:F], ALU.add).then_inc(sem("x2_made"), 1)
                v.wait_ge(sem("x2_made"), t + 1)
                ln_stats(T + t, xt)
                ln_norm(T + t, xt, xh_ring[:, t % 2, :])
                if t >= 2:
                    token_sum(t - 2)
            token_sum(T - 2)
            token_sum(T - 1)
            v.wait_ge(sem("deg_made"), T)
            V.tensor_scalar(deg[:, :], deg[:, :], 1.0, None, ALU.add).then_inc(sem("dis_in"), 1)
            v.wait_ge(sem("dis_in"), 1)
            link(V.tensor_reduce(mean, msum.rearrange("p t k -> p k t"), AX.X, ALU.add))
            V.tensor_scalar(mean, mean, 1.0 / NODES, None, ALU.mult).then_inc(sem("mean_ready"), 1)
            v.wait_ge(sem("dis_sqrt"), 1)
            link(V.reciprocal(dis[:, :], dis[:, :]))
            v.wait_ge(sem("gate_psum"), 1)
            v.wait_ge(sem("ld_w1"), 80)
            link(V.tensor_tensor(gt[0:1, 0, :], bank[2][0:1, 0:E0], bg[:, :], ALU.add))
            V.tensor_reduce(gs[0:1, 0:1], gt[0:1, 0, :], AX.X, ALU.max, negate=True).then_inc(sem("gate_in"), 1)
            v.wait_ge(sem("gate_exp"), 1)
            link(V.tensor_reduce(gs[0:1, 2:3], gt[0:1, 1, :], AX.X, ALU.max))
            link(V.tensor_scalar(gt[0:1, 2, :], gt[0:1, 1, :], gs[0:1, 2:3], None, ALU.is_ge))
            link(V.tensor_tensor(gt[0:1, 2, :], gt[0:1, 2, :], iota16[0:1, :], ALU.mult))
            link(V.tensor_reduce(gs[0:1, 3:4], gt[0:1, 2, :], AX.X, ALU.min))
            V.tensor_scalar(gidx[0:1, :], gs[0:1, 3:4], 99.0, None, ALU.add).then_inc(sem("gate_idx"), 1)
            V.reciprocal(gs[0:1, 4:5], gs[0:1, 1:2]).then_inc(sem("gate_made"), 1)
            v.wait_ge(sem("gate_bc"), 1)
            link(V.tensor_copy(gs[:, 5:6], bank[7][:, 0:1]))
            v.wait_ge(sem("ld_we"), 32)

            def x3(t):
                v.wait_ge(sem("ff_done"), t + 1)
                tmp = num[:, :, :].rearrange("p h f -> p (h f)")[:, 0:D]
                V.tensor_tensor(tmp, bank[2 + t % 2][:, :], be_bc[:, :], ALU.add).then_inc(sem("ff_used"), 1)
                v.wait_ge(sem("ff_used"), t + 1)
                link(V.scalar_tensor_tensor(x[:, t, :], tmp, gs[:, 5:6], x[:, t, :], ALU.mult, ALU.add))
                ln_stats(2 * T + t, x[:, t, :])
                ln_norm(2 * T + t, x[:, t, :], xh_ring[:, t % 2, :])

            def message(t):
                v.wait_ge(sem("linC"), t + 1)
                if t >= 2:
                    v.wait_ge(sem("h_lo"), t - 1)
                V.tensor_tensor(hs[:, t % 2, :], bank[4 + t % 2][:, :], gb_bc[:, :], ALU.add).then_inc(sem("h_used"), 1)
                v.wait_ge(sem("h_used"), t + 1)
                V.tensor_scalar(hs[:, t % 2, :], hs[:, t % 2, :], dis[:, t:t + 1], None, ALU.mult).then_inc(sem("hs_made"), 1)

            for t in range(T + 1):
                if t < T:
                    x3(t)
                if t >= 1:
                    message(t - 1)

            def logits(t):
                v.wait_ge(sem("linD"), t + 1)
                V.tensor_tensor(lg[:, t, :], bank[2 + t % 2][:, 0:E1], br_bc[:, :], ALU.add).then_inc(sem("lg_made"), 1)

            for t in range(T + 1):
                if t < T:
                    v.wait_ge(sem("x4_made"), t + 1)
                    ln_stats(3 * T + t, x[:, t, :])
                    ln_norm(3 * T + t, x[:, t, :], xh4[:, t, :])
                if t >= 1:
                    logits(t - 1)
            v.wait_ge(sem("lg_made"), T)
            S3 = [P, T, E1]
            link(V.tensor_reduce(mx10, lg, AX.X, ALU.max))
            V.tensor_tensor(ex, lg, bc(mx10, S3), ALU.subtract).then_inc(sem("rt_in"), 1)
            v.wait_ge(sem("rt_exp"), 1)
            link(V.tensor_reduce(G, ex, AX.X, ALU.add))
            V.reciprocal(G, G)
            link(V.tensor_reduce(mx10, ex, AX.X, ALU.max))
            link(V.tensor_tensor(eq, ex, bc(mx10, S3), ALU.is_ge))
            i8 = iota8[:, :].unsqueeze(1).to_broadcast(S3)
            link(V.tensor_tensor(eq, eq, i8, ALU.mult))
            link(V.tensor_reduce(em, eq, AX.X, ALU.min))
            V.tensor_tensor(oh, i8, bc(em, S3), ALU.is_equal).then_inc(sem("oh_made"), 1)
            v.wait_ge(sem("rank_psum"), 1)
            flat = lambda ap: ap.rearrange("p t e -> p (t e)")
            V.memset(pre[:, 0, :], 0.0)
            link(V.tensor_copy(flat(tot), bank[3][:, 0:T * E1]))
            for t in range(T):
                link(V.tensor_tensor(pre[:, t + 1, :], pre[:, t, :], tot[:, t, :], ALU.add))
            link(V.tensor_tensor(cmp_, iotaM[:, :].unsqueeze(1).to_broadcast([P, E1, T]), bc(pre[:, T, :], [P, E1, T]), ALU.is_lt))
            link(V.tensor_reduce(tl, cmp_, AX.X, ALU.add))
            link(V.tensor_tensor_scan(cum, ones[:, 0:E1], tl, 0.0, ALU.mult, ALU.add))
            link(V.tensor_tensor(base, cum, tl, ALU.subtract))
            V.tensor_tensor(tcmp, bc(iotaJ[:, :], [P, NT, E1 - 1]), cum[:, 0:E1 - 1].unsqueeze(1).to_broadcast([P, NT, E1 - 1]), ALU.is_ge)
            link(V.tensor_scalar(base, base, float(P), None, ALU.mult))
            link(V.tensor_reduce(te_f, tcmp, AX.X, ALU.add))
            V.tensor_copy(te, te_f).then_inc(sem("te_ready"), 1)
            link(V.tensor_tensor(slot, pre[:, 0:T, :], base.unsqueeze(1).to_broadcast(S3), ALU.add))
            link(V.tensor_tensor(flat(slot), flat(slot), bank[2][:, 0:T * E1], ALU.add))
            link(V.tensor_tensor(slot, slot, oh, ALU.mult))
            link(V.tensor_reduce(pos_f, slot, AX.X, ALU.add))
            V.tensor_copy(pos, pos_f).then_inc(sem("pos_ready"), 1)

            def h_evac(j):
                v.wait_ge(sem("m1_done"), j + 1)
                v.wait_ge(sem(f"ld_xp{j % 2}"), 48 * (j // 2 + 1))
                if j >= 2:
                    v.wait_ge(sem("hT_psum"), j - 1)
                V.tensor_tensor(h_sb[:, j % 2, :], bank[6 + j % 2][:, :], b1_bc[:, j % 2, :], ALU.add).then_inc(sem("h1_made"), 1)

            def y_evac(j):
                v.wait_ge(sem("m2_done"), j + 1)
                if j >= 2:
                    v.wait_ge(sem(f"y_st{j % 2}"), 16 * (j // 2))
                V.tensor_tensor(y_sb[:, j % 2, :], bank[2 + j % 2][:, :], b2_bc[:, j % 2, :], ALU.add).then_inc(sem("y_made"), 1)

            h_evac(0)
            for j in range(NT):
                if j + 1 < NT:
                    h_evac(j + 1)
                y_evac(j)
            for t in range(T):
                v.wait_ge(sem(f"gathered{t}"), 16)
                V.scalar_tensor_tensor(yg[:, t, :], yg[:, t, :], G[:, t:t + 1], x[:, t, :], ALU.mult, ALU.add).then_inc(sem("final"), 1)

        @block.tensor
        def _(pe):
            mm = nc.tensor.matmul

            def transposes(src, b, name):
                for k in range(K):
                    ins = nc.tensor.transpose(b[:, k * P:(k + 1) * P], src[:, k * P:(k + 1) * P], ident[:, :])
                ins.then_inc(sem(name), 1)

            def tile_T(n, src, b):
                pe.wait_ge(sem("xh_made"), n + 1)
                if n >= 2:
                    pe.wait_ge(sem("xT_ready"), n - 1)
                transposes(src, b, "xt_psum")

            def linear(lhs, rhs, out, name=None):
                for k in range(K):
                    ins = mm(out, lhs[:, k, :], rhs(k), start=k == 0, stop=k == K - 1)
                if name:
                    ins.then_inc(sem(name), 1)

            pe.wait_ge(sem("consts"), 1)
            pe.wait_ge(sem("n_ready"), 1)
            mm(bank[5][0:NG, 0:1], tri[0:NG, 0:NG], grp[0:NG, 2:3], start=True, stop=True)
            pe.wait_ge(sem("wa_ready"), 1)

            def lin_a(t):
                pe.wait_ge(sem("xT_ready"), t + 1)
                if t >= 2:
                    pe.wait_ge(sem("evacA"), t - 1)
                xT = xT_ring[:, t % 2, :, :]
                linear(xT, lambda k: W0[:, k, :, :].rearrange("p h f -> p (h f)"), bank[2 + t % 2][:, :])
                linear(xT, lambda k: Wa[:, k, :], bank[4 + t % 2][:, 0:2 * H], "linA")

            tile_T(0, xh_ring[:, 0, :], bank[6])
            tile_T(1, xh_ring[:, 1, :], bank[7])
            for t in range(T):
                lin_a(t)
                if t + 2 < T:
                    tile_T(t + 2, xh_ring[:, t % 2, :], bank[6 + t % 2])
            pe.wait_ge(sem("xT_ready"), T)
            pe.wait_ge(sem("ld_gw"), 16)
            for k in range(K):
                if k >= 2:
                    pe.wait_ge(sem("gwT_ready"), k - 1)
                for o in range(K):
                    ins = nc.tensor.transpose(bank[6 + k % 2][:, o * P:(o + 1) * P], gW[:, o, k * P:(k + 1) * P], ident[:, :])
                ins.then_inc(sem("gwT_psum"), 1)
            pe.wait_ge(sem("thr_made"), 1)
            pe.wait_ge(sem("gwT_ready"), K)
            for i, n in enumerate((4, 4, 2)):
                for q in range(n):
                    ins = nc.tensor.transpose(bank[5 + i][0:H, q * P:(q + 1) * P], thr[:, 4 * i + q, :], ident[:, :])
                ins.then_inc(sem("thrT_psum"), 1)
            pe.wait_ge(sem("thrT_ready"), 3)
            mm(bank[5][0:NG, 0:1], tri[0:NG, 0:NG], grp[0:NG, 2:3], start=True, stop=True)
            mm(bank[4][0:1, 32:33], ones[0:NG, 0:1], grp[0:NG, 2:3], start=True, stop=True).then_inc(sem("rb_psum"), 1)

            pe.wait_ge(sem("npass_ready"), 1)
            n = pe.value_load(npass[0:1, 0:1], min_val=1, max_val=MAXPASS)

            def pair_matmuls(p):
                pe.wait_ge(sem("picks"), p + 1)
                for j in range(CH):
                    e = slice(j * P, (j + 1) * P)
                    o = slice(j * NPAIR, (j + 1) * NPAIR)
                    mm(bank[2][:, o], lo_f[0:NG, e], inside[0:NG, :], start=True, stop=True)
                    mm(bank[3][:, o], q_f[0:NG, e], inside[0:NG, :], start=True, stop=False)
                    mm(bank[3][:, o], ones[0:NG, :], wneg[0:NG, :], start=False, stop=True)
                mm(bank[4][0:1, 0:NPAIR], ones[0:NG, 0:1], wneg[0:NG, :], start=True, stop=True).then_inc(sem("table_psum"), 1)

            def count(base):
                for k in range(2 * LB):
                    pe.wait_ge(sem("onehots"), base + (k + 1))
                    at_least(pe, "staged", base + (k - 1))
                    for j in range(CH):
                        ins = mm(bank[k % 2][:, 0:RW], L_ring[:, k // LB, :, (k % LB) * CH + j], R_ring[:, k % RR, j, :],
                                 start=j == 0, stop=j == CH - 1)
                    ins.then_inc(sem("counted"), 1)

            pair_matmuls(0)
            for i in range(NB // 2):
                count(i * 2 * LB)
            with pe.If(n > 1):
                with pe.Fori(1, n) as p:
                    pair_matmuls(p)
                    with pe.Fori(0, NB // 2) as i:
                        count(p * NPAIR + i * 2 * LB)

            pe.wait_ge(sem("hist_done"), 1)
            for h in range(H):
                if h:
                    pe.wait_ge(sem("raw_made"), 4 * h)
                for b in range(4):
                    w = min(3, T - 3 * b) * 2 * FE
                    mm(bank[b][:, 0:w], zero16[:, 0:P], zero16[:, 0:w], start=True, stop=False)
                pe.wait_ge(sem("v_lo"), 2 * h + 2)
                for s in range(T):
                    i = h * T + s
                    pe.wait_ge(sem("cz_made"), i + 1)
                    for t in range(T):
                        for part in range(2):
                            ins = mm(acc_region(t), cz[:, i % RZ, t * P:(t + 1) * P],
                                     VP[:, s, part, h, :, :].rearrange("p b f -> p (b f)"), start=False,
                                     stop=s == T - 1 and part == 1 and (t % 3 == 2 or t == T - 1))
                    ins.then_inc(sem("cz_used"), 1)
                pe.wait_ge(sem("cz_used"), (h + 1) * T)
                pe.sem_inc(sem("acc_done"), 1)
            def all_edges(t):
                if t >= 2:
                    pe.wait_ge(sem("U_used"), t - 1)
                for g2 in range(2):
                    for s in range(T):
                        for part in range(2):
                            ins = mm(bank[4 + 2 * (t % 2) + g2][:, 0:4 * FE].rearrange("p (h f) -> p h f", f=FE), C[:, s, t * P:(t + 1) * P],
                                     VP[:, s, part, 4 * g2:4 * g2 + 4, 1, :], start=s == 0 and part == 0,
                                     stop=s == T - 1 and part == 1)
                ins.then_inc(sem("U_done"), 1)

            all_edges(0)
            all_edges(1)
            pe.wait_ge(sem("raw_made"), 4 * H)
            for t in range(T):
                tile_T(T + t, xh_ring[:, t % 2, :], bank[t % 2])
                if t + 2 < T:
                    all_edges(t + 2)
            pe.wait_ge(sem("mean_ready"), 1)
            pe.wait_ge(sem("ld_w1"), 80)
            for k in range(K):
                ins = mm(bank[2][0:1, 0:E0], mean[:, k:k + 1], Wg[:, k, :], start=k == 0, stop=k == K - 1)
            ins.then_inc(sem("gate_psum"), 1)
            pe.wait_ge(sem("gate_made"), 1)
            mm(bank[7][:, 0:1], ones[0:1, :], gs[0:1, 4:5], start=True, stop=True).then_inc(sem("gate_bc"), 1)
            pe.wait_ge(sem("ld_we"), 32)

            def ff(t):
                pe.wait_ge(sem("xT_ready"), T + t + 1)
                if t >= 2:
                    pe.wait_ge(sem("ff_used"), t - 1)
                linear(x2T[:, t, :, :], lambda k: We[:, k, :], bank[2 + t % 2][:, :], "ff_done")

            def lin_c(t):
                pe.wait_ge(sem("xT_ready"), 2 * T + t + 1)
                if t >= 2:
                    pe.wait_ge(sem("h_used"), t - 1)
                linear(xT_ring[:, t % 2, :, :], lambda k: gWT[:, k, :], bank[4 + t % 2][:, :], "linC")

            ff(0)
            ff(1)
            for t in range(T):
                tile_T(2 * T + t, xh_ring[:, t % 2, :], bank[t % 2])
                if t + 2 < T:
                    ff(t + 2)
                lin_c(t)
            pe.wait_ge(sem("loops"), 1)
            pe.wait_ge(sem("h_lo"), T)

            def agg(t):
                if t >= 2:
                    pe.wait_ge(sem("relu_made"), t - 1)
                for s in range(T):
                    for part in range(2):
                        ins = mm(bank[6 + t % 2][:, :], C[:, s, t * P:(t + 1) * P], hp[:, s, part, :],
                                 start=s == 0 and part == 0, stop=s == T - 1 and part == 1)
                ins.then_inc(sem("agg_done"), 1)

            def lin_d(t):
                pe.wait_ge(sem("xT_ready"), 3 * T + t + 1)
                if t >= 2:
                    pe.wait_ge(sem("lg_made"), t - 1)
                linear(xT_ring[:, t % 2, :, :], lambda k: Wr[:, k, :], bank[2 + t % 2][:, 0:E1], "linD")

            agg(0)
            agg(1)
            for t in range(T):
                tile_T(3 * T + t, xh4[:, t, :], bank[t % 2])
                if t + 2 < T:
                    agg(t + 2)
                lin_d(t)
            pe.wait_ge(sem("oh_made"), 1)
            pe.wait_ge(sem("lg_made"), T)
            ohf = oh.rearrange("p t e -> p (t e)")
            mm(bank[2][:, 0:T * E1], tri[:, :], ohf, start=True, stop=True)
            mm(bank[3][:, 0:T * E1], ones[:, :], ohf, start=True, stop=True).then_inc(sem("rank_psum"), 1)

            def token_T(j):
                pe.wait_ge(sem(f"ld_xp{j % 2}"), 48 * (j // 2 + 1))
                if j >= 2:
                    pe.wait_ge(sem("xpT"), j - 1)
                transposes(xp[:, j % 2, :], bank[4 + j % 2], "xpT_psum")

            def m1(j, e):
                pe.wait_ge(sem("xpT"), j + 1)
                if j >= 2:
                    pe.wait_ge(sem("h1_made"), j - 1)
                linear(xT_ring[:, j % 2, :, :], lambda k: W1[:, bass.ds(e, 1), k, :].rearrange("p a f -> p (a f)"), bank[6 + j % 2][:, :], "m1_done")

            def hidden_T(j):
                pe.wait_ge(sem("h1_made"), j + 1)
                if j >= 2:
                    pe.wait_ge(sem("hT_ready"), j - 1)
                transposes(h_sb[:, j % 2, :], bank[j % 2], "hT_psum")

            def m2(j, e):
                pe.wait_ge(sem("hT_ready"), j + 1)
                if j >= 2:
                    pe.wait_ge(sem("y_made"), j - 1)
                linear(hT[:, j % 2, :, :], lambda k: W2[:, bass.ds(e, 1), k, :].rearrange("p a f -> p (a f)"), bank[2 + j % 2][:, :], "m2_done")

            pe.wait_ge(sem("te_ready"), 1)
            pe.wait_ge(sem("pos_ready"), 1)
            ex_of = lambda j: pe.value_load(te[0:1, j:j + 1], min_val=0, max_val=E1 - 1)
            token_T(0)
            pe.wait_ge(sem("ld_W1"), 16 * E1)
            e = ex_of(0)
            m1(0, e)
            for j in range(NT):
                if j + 1 < NT:
                    token_T(j + 1)
                    e_next = ex_of(j + 1)
                    m1(j + 1, e_next)
                hidden_T(j)
                if j == 0:
                    pe.wait_ge(sem("ld_W2"), 16 * E1)
                m2(j, e)
                e = e_next


_INS = ['x', 'src', 'dst', 'L0_gnn_Ws', 'L0_gnn_Wb', 'L0_gnn_a_w', 'L0_gnn_a_b', 'L0_ffn_Wg', 'L0_ffn_bg',
        'L0_ffn_We', 'L0_ffn_be', 'L1_gnn_W', 'L1_gnn_b', 'L1_ffn_Wr', 'L1_ffn_br', 'L1_ffn_W1', 'L1_ffn_b1',
        'L1_ffn_W2', 'L1_ffn_b2']


def kernel(**inputs):
    import concourse.bacc as _bacc
    from concourse.bass_utils import run_bass_kernel_spmd as _run

    nc = _bacc.Bacc("TRN2", target_bir_lowering=False, num_devices=1)
    arrays, args = {}, []
    for name in _INS:
        a = np.ascontiguousarray(inputs[name])
        arrays[f"in_{name}"] = a
        args.append(nc.dram_tensor(f"in_{name}", a.shape, mybir.dt.from_np(a.dtype), kind="ExternalInput").ap())
    args.append(nc.dram_tensor("out", (NODES, D), F32, kind="ExternalOutput").ap())
    gnn_ffn_kernel(nc, *args)
    r = _run(nc, [arrays], core_ids=[0])
    return r.results[0]["out"]
```

```python
import numpy as np
import concourse.bass as bass
from concourse import mybir
from contextlib import ExitStack

F32 = mybir.dt.float32
F16 = mybir.dt.float16
I32 = mybir.dt.int32
ALU = mybir.AluOpType
ACT = mybir.ActivationFunctionType
AX = mybir.AxisListType

P = 128
NODES, D = 1250, 512
T = (NODES + P - 1) // P
NP = T * P
LAST = NODES - (T - 1) * P
K = D // P

EDGES = 40000
CH = 3
GE = CH * P
NG = (EDGES + GE - 1) // GE
GLAST = EDGES - (NG - 1) * GE
WN = 32
NW = NP // WN
RW = WN * T
NPAIR = NG + NW - 1
LB = 8
LC = LB * CH
NB = NPAIR // LB
MAXPASS = (NG * NW + NPAIR - 1) // NPAIR
RR, RS = 4, 4

H, F = 8, 64
FE = F + 1
E0, E1 = 16, 8
NT = (NP + E1 * (P - 1)) // P
RZ = 4
BY_ACT = (1, 3, 4, 5, 7, 9)
STEEP = 1e30
RX, RB, RY = 4, 3, 3
B_LN, B_EVAC, B_GW, B_CS = 3, 5, 14, 16
EPS = 1e-5
SLOPE = 0.2


def gnn_ffn_kernel(nc, x_d, src_d, dst_d, Ws_d, Wb_d, aw_d, ab_d, Wg_d, bg_d, We_d, be_d, gW_d, gb_d,
                   Wr_d, br_d, W1_d, b1_d, W2_d, b2_d, out_d):
    ctx = ExitStack()
    with ctx:
        def sb(name, shape, dt=F32):
            return ctx.enter_context(nc.sbuf_tensor(name, shape, dt))

        sems = {}

        def sem(name):
            if name not in sems:
                sems[name] = ctx.enter_context(nc.semaphore(name))
            return sems[name]

        def carve(region, at, shape, dt=F32):
            n = int(np.prod(shape))
            words = n if dt in (F32, I32) else (n + 1) // 2
            v = region[:, at:at + words]
            if dt != F32:
                v = v.bitcast(dt)
            if len(shape) > 1:
                names = " ".join(f"a{i}" for i in range(len(shape)))
                v = v.rearrange(f"p ({names}) -> p {names}", **{f"a{i}": s for i, s in enumerate(shape)})
            return v, at + words

        x = sb("x", [P, T, D])
        ident = sb("ident", [P, P])
        ident16 = sb("ident16", [P, P], F16)
        tri = sb("tri", [P, P])
        ones = sb("ones", [P, P])
        zero16 = sb("zero16", [P, 400], F16)
        xh_ring = sb("xh_ring", [P, 2, D])
        xT_ring = sb("xT_ring", [P, 2, K, P])
        gb_bc = sb("gb_bc", [P, D])
        be_bc = sb("be_bc", [P, D])
        num = sb("num", [P, H, FE])
        Wg = sb("Wg", [P, K, E0])
        Wr = sb("Wr", [P, K, E1])
        bg = sb("bg", [1, E0])
        br_bc = sb("br_bc", [P, E1])
        st = sb("st", [P, 2, 6])
        mv = sb("mv", [P, 2, 2])
        ve = sb("ve", [P, 2])
        sd = sb("sd", [P, 2])
        rs = sb("rs", [P, 2])
        deg = sb("deg", [P, T])
        dis = sb("dis", [P, T])
        iota8 = sb("iota8", [P, E1])
        iota16 = sb("iota16", [P, E0])
        small = sb("small", [P, 1536])

        mid = sb("mid", [P, E1 * K * D])
        C, o = carve(mid, 0, [T, NP], F16)
        gWT, o = carve(mid, o, [K, D])
        free0 = o
        hp, o = carve(mid, o, [T, 2, D], F16)
        We, o = carve(mid, o, [K, D])
        Wx, o = carve(mid, free0, [T, H, FE])
        raw0, o = carve(mid, o, [T, 2, FE])
        z0, o = carve(mid, o, [NP], F16)
        W2, _ = carve(mid, 0, [E1, K, D])

        big = sb("big", [P, E1 * K * D])
        src_i, o = carve(big, 0, [GE], I32)
        dst_i, o = carve(big, o, [GE], I32)
        lo_i, o = carve(big, o, [GE], I32)
        hi_i, o = carve(big, o, [GE], I32)
        w_i, o = carve(big, o, [GE], I32)
        lo_f, o = carve(big, o, [GE])
        q_f, o = carve(big, o, [GE])
        iotaL, o = carve(big, o, [P, LC], F16)
        iotaR, o = carve(big, o, [RW], F16)
        L_ring, o = carve(big, o, [2, P, LC], F16)
        R_ring, o = carve(big, o, [RR, CH, RW], F16)
        stage, o = carve(big, o, [RS, T, WN], F16)
        loT, o = carve(big, o, [NPAIR * CH], F16)
        qT, o = carve(big, o, [NPAIR * CH])
        iotaK, o = carve(big, o, [NPAIR])
        from_, o = carve(big, o, [NPAIR])
        inside, o = carve(big, o, [NPAIR])
        tv, o = carve(big, o, [NPAIR])
        wneg, o = carve(big, o, [NPAIR])
        wk, o = carve(big, o, [NPAIR], I32)
        W0, o = carve(big, o, [K, H, F])
        a_bc, o = carve(big, o, [H, 2 * F])
        Wb_bc, o = carve(big, o, [H, F])
        watmp, o = carve(big, o, [H, F])
        VP, o = carve(big, 0, [T, 2, H, 2, FE], F16)
        nacc, o = carve(big, o, [T, H, FE])
        z1, o = carve(big, o, [NP], F16)
        W1, _ = carve(big, 0, [E1, K, D])
        yg, _ = carve(big, 0, [T, D])

        aux = sb("aux", [P, T * D])
        thr_bc, _ = carve(aux, 0, [2, NP])
        x2T, _ = carve(aux, 0, [T, K, P])
        xh4, _ = carve(aux, 0, [T, D])
        xp, o = carve(aux, 0, [RX, D])
        h_sb, o = carve(aux, o, [2, D])
        y_sb, o = carve(aux, o, [RY, D])
        hT = xh_ring[:, :, :].rearrange("p a (k m) -> p a k m", k=K)

        raw1, o = carve(aux, 2 * NP, [T, 2, FE])
        junk, o = carve(aux, o, [NP], F16)
        work = sb("work", [P, 2 * T * FE + RZ * NP // 2])
        vtmp, o = carve(work, 0, [2, T, FE])
        cz, o = carve(work, o, [RZ, NP], F16)
        b1_bc, o = carve(work, 0, [RB, D])
        b2_bc, o = carve(work, o, [RB, D])
        thrT, _ = carve(work, 0, [NP])
        hs, o = carve(work, 0, [2, D])
        rtmp, o = carve(work, o, [2, D])
        gW, _ = carve(work, 1812, [K, D])
        zero, _ = carve(work, NP, [1, D])
        raw = [raw0, raw1]
        zmask = [z0, z1]

        at = 0
        Wa, at = carve(small, at, [K, 2 * H])
        cb, at = carve(small, at, [2 * H])
        ab_bc, at = carve(small, at, [H])
        sc, at = carve(small, at, [T, 2 * H])
        atb, at = carve(small, at, [T, H])
        thr, at = carve(small, at, [T, H])
        asmax, at = carve(small, at, [H])
        cs, at = carve(small, at, [H])
        zz, at = carve(small, at, [T, H])
        ll, at = carve(small, at, [T, H])
        e1t, at = carve(small, at, [T, H])
        e2t, at = carve(small, at, [T, H])
        d1t, at = carve(small, at, [T, H])
        A1, at = carve(small, at, [T, H])
        A2, at = carve(small, at, [T, H])
        B1, at = carve(small, at, [T, H])
        B2, at = carve(small, at, [T, H])
        steep, at = carve(small, at, [T, H])
        grp, at = carve(small, at, [8])
        kt, at = carve(small, at, [MAXPASS])
        npass, at = carve(small, at, [1], I32)
        rden, at = carve(small, at, [H])
        msum, at = carve(small, at, [T, K])
        mean, at = carve(small, at, [K])
        gt, at = carve(small, at, [4, E0])
        gs, at = carve(small, at, [8])
        gidx, at = carve(small, at, [1], I32)
        at = 0
        lg, at = carve(small, at, [T, E1])
        ex, at = carve(small, at, [T, E1])
        mx10, at = carve(small, at, [T])
        G, at = carve(small, at, [T])
        em, at = carve(small, at, [T])
        oh, at = carve(small, at, [T, E1])
        eq, at = carve(small, at, [T, E1])
        tot, at = carve(small, at, [T, E1])
        pre, at = carve(small, at, [T + 1, E1])
        cmp_, at = carve(small, at, [E1, T])
        tl, at = carve(small, at, [E1])
        cum, at = carve(small, at, [E1])
        base, at = carve(small, at, [E1])
        slot, at = carve(small, at, [T, E1])
        pos_f, at = carve(small, at, [T])
        pos, at = carve(small, at, [T], I32)
        tcmp, at = carve(small, at, [NT, E1 - 1])
        te_f, at = carve(small, at, [NT])
        te, at = carve(small, at, [NT], I32)
        iotaM = sb("iotaM", [P, T])
        iotaJ = sb("iotaJ", [P, NT])

        bank = [ctx.enter_context(nc.psum_tensor(f"bank{i}", [P, 512], F32)) for i in range(8)]

        thr_d = nc.dram_tensor("thr_scratch", [H, NP], F32, kind="Internal").ap()
        xp_d = nc.dram_tensor("xperm_scratch", [NT * P, D], F32, kind="Internal").ap()
        yp_d = nc.dram_tensor("yperm_scratch", [NT * P, D], F32, kind="Internal").ap()

        block = ctx.enter_context(nc.Block())

        def at_least(eng, name, value):
            if isinstance(value, int) and value <= 0:
                return
            eng.wait_ge(sem(name), value)

        def bc(ap, shape):
            return ap.unsqueeze(len(ap.shape)).to_broadcast(shape)

        def acc_region(h, t):
            return bank[4 * (h % 2) + t // 3][:, (t % 3) * 2 * FE:(t % 3 + 1) * 2 * FE]

        @block.sync
        def _(sp):
            sp.wait_ge(sem("edge_pads"), 2)
            full = (NG - 1) * GE
            for i_d, i_sb in ((src_d, src_i), (dst_d, dst_i)):
                sp.dma_start(i_sb[0:NG - 1, :], i_d[0:full].rearrange("(g e) -> g e", e=GE)).then_inc(sem("ld_edges"), 16)
                sp.dma_start(i_sb[NG - 1:NG, 0:GLAST], i_d[full:EDGES].rearrange("(g e) -> g e", g=1)).then_inc(sem("ld_edges"), 16)
            for k in range(K):
                sp.dma_start(W0[:, k, :, :], Ws_d[:, k * P:(k + 1) * P, :].rearrange("h p f -> p h f")).then_inc(sem("ld_w0"), 16)
            sp.dma_start(a_bc, aw_d.partition_broadcast(P)).then_inc(sem("ld_w0"), 16)
            sp.dma_start(Wb_bc, Wb_d.partition_broadcast(P)).then_inc(sem("ld_w0"), 16)
            sp.dma_start(ab_bc, ab_d.partition_broadcast(P)).then_inc(sem("ld_w0"), 16)
            sp.dma_start(x[:, 0:T - 1, :], x_d[0:(T - 1) * P, :].rearrange("(t p) d -> p t d", p=P)).then_inc(sem("ld_x"), 16)
            sp.wait_ge(sem("x_pad"), 1)
            sp.dma_start(x[0:LAST, T - 1, :], x_d[(T - 1) * P:NODES, :]).then_inc(sem("ld_x"), 16)
            sp.dma_start(gW, gW_d.rearrange("(k p) i -> p k i", p=P)).then_inc(sem("ld_gw"), 16)
            for dst, src in ((gb_bc[:, :], gb_d.partition_broadcast(P)),
                             (Wg[:, :, :], Wg_d.rearrange("(k p) e -> p k e", p=P)),
                             (Wr[:, :, :], Wr_d.rearrange("(k p) e -> p k e", p=P)),
                             (bg[:, :], bg_d.rearrange("(a e) -> a e", a=1)),
                             (br_bc[:, :], br_d.partition_broadcast(P))):
                sp.dma_start(dst, src).then_inc(sem("ld_w1"), 16)
            sp.wait_ge(sem("zero_set"), 1)
            sp.dma_start(xp_d.rearrange("(j p) d -> p j d", p=P),
                         zero[:, 0:1, :].to_broadcast([P, NT, D])).then_inc(sem("xp_zeroed"), 16)
            sp.wait_ge(sem("thrT_ready"), 3)
            sp.dma_start(thr_d, thrT[0:H, :]).then_inc(sem("thr_out"), 16)
            sp.wait_ge(sem("thr_out"), 16)
            for h in range(H):
                if h >= 2:
                    sp.wait_ge(sem("cz_made"), T * (h - 1))
                sp.dma_start(thr_bc[:, h % 2, :], thr_d[h, :].partition_broadcast(P)).then_inc(sem(f"thr_ld{h % 2}"), 16)
            sp.wait_ge(sem("gate_idx"), 1)
            e = sp.value_load(gidx[0:1, 0:1], min_val=0, max_val=E0 - 1)
            sp.dma_start(We, We_d[bass.ds(e, 1), :, :].rearrange("a (k p) o -> p (a k) o", p=P)).then_inc(sem("ld_we"), 16)
            sp.dma_start(be_bc[:, :], be_d[bass.ds(e, 1), :].rearrange("a o -> (a o)").partition_broadcast(P)).then_inc(sem("ld_we"), 16)
            sp.wait_ge(sem("x2_made"), T)
            for i in range(E1):
                sp.dma_start(W1[:, i, :, :], W1_d[i].rearrange("(k p) f -> p k f", p=P)).then_inc(sem(f"ld_W1"), 16)
            sp.wait_ge(sem("agg_done"), T)
            for i in range(E1):
                sp.dma_start(W2[:, i, :, :], W2_d[i].rearrange("(k p) f -> p k f", p=P)).then_inc(sem(f"ld_W2"), 16)
            sp.wait_ge(sem("te_ready"), 1)
            sp.wait_ge(sem("scattered"), 16 * T)
            for j in range(NT):
                e = sp.value_load(te[0:1, j:j + 1], min_val=0, max_val=E1 - 1)
                if j >= RX:
                    sp.wait_ge(sem("xpT_psum"), j + 1 - RX)
                sp.dma_start(xp[:, j % RX, :], xp_d[j * P:(j + 1) * P, :]).then_inc(sem(f"ld_xp{j % RX}"), 16)
                if j >= RB:
                    sp.wait_ge(sem("y_made"), j + 1 - RB)
                s = sem(f"ld_b{j % RB}")
                sp.dma_start(b1_bc[:, j % RB, :], b1_d[bass.ds(e, 1), :].rearrange("a o -> (a o)").partition_broadcast(P)).then_inc(s, 16)
                sp.dma_start(b2_bc[:, j % RB, :], b2_d[bass.ds(e, 1), :].rearrange("a o -> (a o)").partition_broadcast(P)).then_inc(s, 16)
            sp.wait_ge(sem("out_done"), 16 * (T + 1))

        @block.gpsimd
        def _(g):
            nc.gpsimd.memset(src_i[96:NG, :], 0).then_inc(sem("edge_pads"), 1)
            nc.gpsimd.memset(dst_i[96:NG, :], NP).then_inc(sem("edge_pads"), 1)
            nc.gpsimd.memset(x[96:P, T - 1, :], 0.0).then_inc(sem("x_pad"), 1)
            g.wait_ge(sem("x_pad"), 1)
            nc.gpsimd.memset(ones[:, :], 1.0).then_inc(sem("pc"), 1)
            nc.gpsimd.memset(ident[:, :], 0.0).then_inc(sem("pc"), 1)
            g.wait_ge(sem("pc"), 2)
            nc.gpsimd.affine_select(out=tri[:, :], in_=ones[:, :], compare_op=ALU.is_gt, fill=0.0,
                                    base=0, pattern=[[1, P]], channel_multiplier=-1)
            nc.gpsimd.affine_select(out=ident[:, :], in_=ident[:, :], compare_op=ALU.not_equal, fill=1.0,
                                    base=0, pattern=[[-1, P]], channel_multiplier=1).then_inc(sem("pc"), 1)
            kw = dict(allow_small_or_imprecise_dtypes=True, channel_multiplier=0)
            nc.gpsimd.iota(iotaK, [[1, NPAIR]], base=0, **kw)
            nc.gpsimd.iota(iotaR, [[1, RW]], base=1, **kw)
            nc.gpsimd.iota(iotaL, [[1, P], [0, LC]], base=0, **kw).then_inc(sem("consts"), 1)
            nc.gpsimd.memset(C.bitcast(F32), 0.0).then_inc(sem("C_zeroed"), 1)
            nc.gpsimd.memset(zero[:, 0, :], 0.0).then_inc(sem("zero_set"), 1)
            nc.gpsimd.memset(zero16[:, :], 0.0)
            nc.gpsimd.iota(iota8[:, :], [[1, E1]], base=-99, **kw)
            nc.gpsimd.iota(iota16[:, :], [[1, E0]], base=-99, **kw)
            nc.gpsimd.iota(iotaM[:, :], [[P, T]], base=0, **kw)
            nc.gpsimd.iota(iotaJ[:, :], [[1, NT]], base=0, **kw)
            nc.gpsimd.memset(Wx[:, :, :, F:FE], 1.0)
            g.wait_ge(sem("pc"), 3)
            nc.gpsimd.tensor_copy(ident16[:, :], ident[:, :]).then_inc(sem("pool_ready"), 1)

            g.wait_ge(sem("C_zeroed"), 1)

            def add_batch(base, off):
                for k in range(LB):
                    w = g.value_load(wk[0:1, bass.ds(off + k, 1)], min_val=0, max_val=NW - 1)
                    g.wait_ge(sem("staged"), base + (k + 1))
                    at_least(g, "added", base + k)
                    if not isinstance(base, int):
                        g.sem_inc(sem("pool_step"), 1)
                    dst = C[:, :, bass.ds(w * WN, WN)]
                    nc.gpsimd.tensor_tensor(dst, dst, stage[:, k % RS, :, :], ALU.add).then_inc(sem("added"), 1)

            g.wait_ge(sem("tables"), 1)
            for b in range(NB):
                if b == B_CS:
                    g.wait_ge(sem("asmax"), 1)
                    nc.gpsimd.partition_all_reduce(cs, asmax, P, bass.bass_isa.ReduceOp.max).then_inc(sem("cs_ready"), 1)
                add_batch(b * LB, b * LB)
            n = g.value_load(npass[0:1, 0:1], min_val=1, max_val=MAXPASS)
            with g.If(n > 1):
                with g.Fori(1, n) as p:
                    g.wait_ge(sem("tables"), p + 1)
                    g.sem_inc(sem("pool_step"), 1)
                    with g.Fori(0, NB) as i:
                        add_batch(p * NPAIR + i * LB, i * LB)
            g.wait_ge(sem("added"), n * NPAIR)
            g.sem_inc(sem("hist_done"), 1)

            g.wait_ge(sem("exps"), 1)
            g.wait_ge(sem("evacA"), T)

            def value(i):
                h, b = divmod(i, 2)
                if i >= 2:
                    g.wait_ge(sem("v_lo"), i - 1)
                nc.gpsimd.tensor_tensor(vtmp[:, i % 2, :, :], Wx[:, :, h, :],
                                        bc((B1, B2)[b][:, :, h], [P, T, FE]), ALU.mult).then_inc(sem("v_made"), 1)

            def low(i):
                h, b = divmod(i, 2)
                g.wait_ge(sem("v_hi"), i + 1)
                nc.gpsimd.tensor_tensor(VP[:, :, 1, h, b, :], vtmp[:, i % 2, :, :], VP[:, :, 0, h, b, :],
                                        ALU.subtract).then_inc(sem("v_lo"), 1)

            def numer(h):
                g.wait_ge(sem("raw_made"), 4 * (h + 1))
                r = raw[h % 2]
                nc.gpsimd.tensor_tensor(r[:, :, 0, :], r[:, :, 0, :], bc(A1[:, :, h], [P, T, FE]), ALU.mult).then_inc(sem("pn"), 1)
                nc.gpsimd.tensor_tensor(r[:, :, 1, :], r[:, :, 1, :], bc(A2[:, :, h], [P, T, FE]), ALU.mult).then_inc(sem("pn"), 1)
                g.wait_ge(sem("pn"), 2 * (h + 1))
                nc.gpsimd.tensor_tensor(nacc[:, :, h, :], r[:, :, 0, :], r[:, :, 1, :], ALU.subtract).then_inc(sem("nacc_made"), 1)

            g.wait_ge(sem("thr_out"), 16)
            g.wait_ge(sem("xp_zeroed"), 16)
            for h in range(H + 1):
                if h < H:
                    for f in (value, low):
                        f(2 * h)
                        f(2 * h + 1)
                if h >= 2:
                    numer(h - 2)
            numer(H - 1)

            g.wait_ge(sem("U_done"), T)
            g.wait_ge(sem("deg_made"), T)
            for s in range(T):
                d = C[:, s, s * P:(s + 1) * P]
                last = nc.gpsimd.tensor_tensor(d, d, ident16[:, :], ALU.add)
            last.then_inc(sem("loops"), 1)
            for t in range(T):
                g.wait_ge(sem("h_hi"), t + 1)
                nc.gpsimd.tensor_tensor(hp[:, t, 1, :], hs[:, t % 2, :], hp[:, t, 0, :], ALU.subtract).then_inc(sem("h_lo"), 1)
            for t in range(T):
                g.wait_ge(sem("relu_made"), t + 1)
                nc.gpsimd.tensor_tensor(x[:, t, :], x[:, t, :], rtmp[:, t % 2, :], ALU.add).then_inc(sem("x4_made"), 1)
            g.wait_ge(sem("pos_ready"), 1)
            g.wait_ge(sem("xp_zeroed"), 16)
            for t in range(T):
                nc.gpsimd.indirect_dma_start(xp_d, bass.IndirectOffsetOnAxis(ap=pos[:, t:t + 1], axis=0),
                                             xh4[:, t, :], None).then_inc(sem("scattered"), 16)
            g.wait_ge(sem("y_stored"), 16 * NT)
            for t in range(T):
                nc.gpsimd.indirect_dma_start(yg[:, t, :], None, yp_d,
                                             bass.IndirectOffsetOnAxis(ap=pos[:, t:t + 1], axis=0)).then_inc(sem(f"gathered{t}"), 16)

        @block.scalar
        def _(a):
            act = nc.scalar.activation

            def ln_sqrt(n):
                a.wait_ge(sem("ln_var"), n + 1)
                act(sd[:, n % 2:n % 2 + 1], ve[:, n % 2:n % 2 + 1], ACT.Sqrt).then_inc(sem("ln_sd"), 1)

            def ln_copy(n, b, dst):
                a.wait_ge(sem("xt_psum"), n + 1)
                act(dst, b[:, :].rearrange("p (k m) -> p k m", k=K), ACT.Copy).then_inc(sem("xT_ready"), 1)

            def stage_batch(base):
                for k in range(LB):
                    a.wait_ge(sem("counted"), base + (k + 1))
                    at_least(a, "added", base + (k + 1 - RS))
                    act(stage[:, k % RS, :, :], bank[k % 2][:, 0:RW].rearrange("p (d s) -> p s d", s=T),
                        ACT.Copy).then_inc(sem("staged"), 1)

            for b in range(NB):
                t = b - B_LN
                if 0 <= t < T:
                    ln_sqrt(t)
                stage_batch(b * LB)
                if 0 <= t < T:
                    if t >= 2:
                        a.wait_ge(sem("linA"), t - 1)
                    ln_copy(t, bank[6 + t % 2], xT_ring[:, t % 2, :, :])
                if b == B_GW:
                    for k in range(K):
                        a.wait_ge(sem("gwT_psum"), k + 1)
                        act(gWT[:, k, :], bank[6 + k % 2][:, :], ACT.Copy).then_inc(sem("gwT_ready"), 1)
                if b == B_CS:
                    for i, n in enumerate((4, 4, 2)):
                        a.wait_ge(sem("thrT_psum"), i + 1)
                        act(thrT[0:H, i * 512:i * 512 + n * P], bank[5 + i][0:H, 0:n * P], ACT.Copy).then_inc(sem("thrT_ready"), 1)
            a.wait_ge(sem("exp_in"), 1)
            act(B1, d1t, ACT.Exp)
            act(B2, d1t, ACT.Exp, scale=SLOPE)
            act(A1, e1t, ACT.Exp)
            act(A2, e2t, ACT.Exp).then_inc(sem("exps"), 1)
            n = a.value_load(npass[0:1, 0:1], min_val=1, max_val=MAXPASS)
            with a.If(n > 1):
                with a.Fori(1, n) as p:
                    with a.Fori(0, NB) as i:
                        stage_batch(p * NPAIR + i * LB)

            def hi(i):
                h, b = divmod(i, 2)
                a.wait_ge(sem("v_made"), i + 1)
                act(VP[:, :, 0, h, b, :], vtmp[:, i % 2, :, :], ACT.Copy).then_inc(sem("v_hi"), 1)

            def raw_copy(h):
                if h >= 2:
                    a.wait_ge(sem("nacc_made"), h - 1)
                for b in range(4):
                    n3 = min(3, T - 3 * b)
                    a.wait_ge(sem("acc_done"), h + 1)
                    act(raw[h % 2][:, 3 * b:3 * b + n3, :, :],
                        bank[4 * (h % 2) + b][:, 0:n3 * 2 * FE].rearrange("p (t b f) -> p t b f", b=2, f=FE),
                        ACT.Copy).then_inc(sem("raw_made"), 1)

            def mask(h, m):
                i = h * len(BY_ACT) + m
                if i >= 2:
                    h2, m2 = divmod(i - 2, len(BY_ACT))
                    a.wait_ge(sem("cz_made"), h2 * T + BY_ACT[m2] + 1)
                s = BY_ACT[m]
                act(zmask[i % 2], thr_bc[:, h % 2, :], ACT.Sigmoid, bias=steep[:, s, h:h + 1], scale=-STEEP).then_inc(sem("z_made"), 1)

            a.wait_ge(sem("hist_done"), 1)
            hi(0)
            hi(1)
            for h in range(H):
                a.wait_ge(sem(f"thr_ld{h % 2}"), 16 * (h // 2 + 1))
                for m in range(len(BY_ACT)):
                    mask(h, m)
                    if m == 1 and h + 1 < H:
                        hi(2 * h + 2)
                        hi(2 * h + 3)
                    if m == 3 and h:
                        raw_copy(h - 1)
            raw_copy(H - 1)

            def degree(s):
                if s:
                    a.wait_ge(sem("deg_made"), s)
                act(junk, C[:, s, :], ACT.Copy, accum_out=deg[:, s:s + 1]).then_inc(sem("deg_made"), 1)

            for s in range(T - 1):
                degree(s) if s < 4 else None
            for t in range(T):
                ln_sqrt(T + t)
                if 4 + t < T:
                    degree(4 + t)
                ln_copy(T + t, bank[4 + t % 2], x2T[:, t, :, :])
            a.wait_ge(sem("dis_in"), 1)
            act(dis[:, :], deg[:, :], ACT.Sqrt).then_inc(sem("dis_sqrt"), 1)
            a.wait_ge(sem("gate_in"), 1)
            act(gt[0:1, 1, :], gt[0:1, 0, :], ACT.Exp, bias=gs[0:1, 0:1], accum_out=gs[0:1, 1:2]).then_inc(sem("gate_exp"), 1)
            for t in range(T + 1):
                if t < T:
                    ln_sqrt(2 * T + t)
                    if t >= 2:
                        a.wait_ge(sem("linC"), t - 1)
                    ln_copy(2 * T + t, bank[t % 2], xT_ring[:, t % 2, :, :])
                if t >= 1:
                    a.wait_ge(sem("hs_made"), t)
                    act(hp[:, t - 1, 0, :], hs[:, (t - 1) % 2, :], ACT.Copy).then_inc(sem("h_hi"), 1)
            for t in range(T + 1):
                if t < T:
                    a.wait_ge(sem("agg_done"), t + 1)
                    if t >= 2:
                        a.wait_ge(sem("x4_made"), t - 1)
                    act(rtmp[:, t % 2, :], bank[6 + t % 2][:, :], ACT.Relu, scale=dis[:, t:t + 1]).then_inc(sem("relu_made"), 1)
                    ln_sqrt(3 * T + t)
                if t >= 1:
                    if t >= 3:
                        a.wait_ge(sem("linD"), t - 2)
                    ln_copy(3 * T + t - 1, bank[(t - 1) % 2], xT_ring[:, (t - 1) % 2, :, :])
            a.wait_ge(sem("rt_in"), 1)
            act(ex, ex, ACT.Exp).then_inc(sem("rt_exp"), 1)

            def xp_copy(j):
                a.wait_ge(sem("xpT_psum"), j + 1)
                if j >= 2:
                    a.wait_ge(sem("m1_done"), j - 1)
                act(xT_ring[:, j % 2, :, :], bank[4 + j % 2][:, :].rearrange("p (k m) -> p k m", k=K),
                    ACT.Copy).then_inc(sem("xpT"), 1)

            def store(j):
                a.wait_ge(sem("y_made"), j + 1)
                a.dma_start(yp_d[j * P:(j + 1) * P, :], y_sb[:, j % RY, :]).then_inc(sem(f"y_st{j % RY}"), 16)

            xp_copy(0)
            xp_copy(1)
            for j in range(NT):
                a.wait_ge(sem("hT_psum"), j + 1)
                if j >= 2:
                    a.wait_ge(sem("m2_done"), j - 1)
                act(hT[:, j % 2, :, :], bank[j % 2][:, :].rearrange("p (k m) -> p k m", k=K),
                    ACT.Relu).then_inc(sem("hT_ready"), 1)
                if j + 2 < NT:
                    xp_copy(j + 2)
                if j:
                    store(j - 1)
            store(NT - 1)
            for r in range(RY):
                a.wait_ge(sem(f"y_st{r}"), 16 * len(range(r, NT, RY)))
            a.sem_inc(sem("y_stored"), 16 * NT)
            for t in range(T):
                a.wait_ge(sem("final"), t + 1)
                if t < T - 1:
                    a.dma_start(out_d[t * P:(t + 1) * P, :], yg[:, t, :]).then_inc(sem("out_done"), 16)
                else:
                    a.dma_start(out_d[t * P:NODES, :], yg[0:LAST, t, :]).then_inc(sem("out_done"), 16)
            a.sem_inc(sem("out_done"), 16)

        @block.vector
        def _(v):
            V = nc.vector
            count = [0]

            def link(ins):
                count[0] += 1
                ins.then_inc(sem("dve"), 1)
                v.wait_ge(sem("dve"), count[0])

            def ln_stats(n, xt):
                i = n % 2
                link(V.bn_stats(st[:, i, :], xt))
                link(V.bn_aggr(mv[:, i, :], st[:, i, :]))
                V.tensor_scalar(ve[:, i:i + 1], mv[:, i, 1:2], EPS, None, ALU.add).then_inc(sem("ln_var"), 1)

            def ln_norm(n, xt, dst):
                i = n % 2
                v.wait_ge(sem("ln_sd"), n + 1)
                link(V.reciprocal(rs[:, i:i + 1], sd[:, i:i + 1]))
                if n >= 2:
                    v.wait_ge(sem("xt_psum"), n - 1)
                V.tensor_scalar(dst, xt, mv[:, i, 0:1], rs[:, i:i + 1], ALU.subtract, ALU.mult).then_inc(sem("xh_made"), 1)

            v.wait_ge(sem("ld_edges"), 64)
            gp = slice(0, NG)
            V.tensor_scalar(lo_i[gp, :], src_i[gp, :], P - 1, None, ALU.bitwise_and)
            V.tensor_scalar(hi_i[gp, :], src_i[gp, :], 7, None, ALU.logical_shift_right)
            V.tensor_scalar(w_i[gp, :], dst_i[gp, :], 5, None, ALU.logical_shift_right)
            link(V.tensor_scalar(q_f[gp, :], dst_i[gp, :], float(T), 1.0, ALU.mult, ALU.add))
            V.tensor_copy(lo_f[gp, :], lo_i[gp, :])
            V.tensor_tensor(q_f[gp, :], q_f[gp, :], hi_i[gp, :], ALU.add)
            V.tensor_reduce(grp[gp, 0:1], w_i[gp, :], AX.X, ALU.min)
            link(V.tensor_reduce(grp[gp, 1:2], w_i[gp, :], AX.X, ALU.max))
            link(V.tensor_scalar(grp[gp, 2:3], grp[gp, 1:2], float(NW - 1), 1.0, ALU.min, ALU.add))
            V.tensor_tensor(grp[gp, 2:3], grp[gp, 2:3], grp[gp, 0:1], ALU.subtract).then_inc(sem("n_ready"), 1)

            def score_weights(k):
                if k == 0:
                    v.wait_ge(sem("ld_w0"), 16 * (K + 3))
                w, dst = (W0[:, k, :, :], Wa[:, k, :]) if k < K else (Wb_bc, cb)
                for i in range(2):
                    link(V.tensor_tensor(watmp, w, a_bc[:, :, i * F:(i + 1) * F], ALU.mult))
                    ins = V.tensor_reduce(dst[:, i * H:(i + 1) * H], watmp, AX.X, ALU.add)
                    if k == K and i == 1:
                        ins.then_inc(sem("wa_ready"), 1)
                    else:
                        link(ins)

            def evac_a(t):
                v.wait_ge(sem("linA"), t + 1)
                V.tensor_tensor(Wx[:, t, :, 0:F], bank[2 + t % 2][:, :].rearrange("p (h f) -> p h f", h=H), Wb_bc, ALU.add)
                V.tensor_tensor(sc[:, t, :], bank[4 + t % 2][:, 0:2 * H], cb, ALU.add).then_inc(sem("evacA"), 1)

            def scores():
                v.wait_ge(sem("evacA"), T)
                link(V.tensor_tensor(atb, sc[:, :, 0:H], ab_bc.unsqueeze(1).to_broadcast([P, T, H]), ALU.add))
                V.tensor_scalar(thr, atb, -1.0, None, ALU.mult).then_inc(sem("thr_made"), 1)
                V.tensor_scalar(steep, sc[:, :, H:2 * H], STEEP, None, ALU.mult)
                V.tensor_reduce(asmax, sc[:, :, H:2 * H].rearrange("p t h -> p h t"), AX.X, ALU.max).then_inc(sem("asmax"), 1)

            def exponents():
                v.wait_ge(sem("cs_ready"), 1)
                csb = cs.unsqueeze(1).to_broadcast([P, T, H])
                V.tensor_tensor(d1t, sc[:, :, H:2 * H], csb, ALU.subtract)
                link(V.tensor_tensor(zz, atb, csb, ALU.add))
                link(V.scalar_tensor_tensor(ll, zz, SLOPE, zz, ALU.mult, ALU.max))
                V.tensor_tensor(e1t, zz, ll, ALU.subtract)
                V.scalar_tensor_tensor(e2t, zz, SLOPE, ll, ALU.mult, ALU.subtract).then_inc(sem("exp_in"), 1)

            v.wait_ge(sem("rb_psum"), 1)
            v.wait_ge(sem("consts"), 1)
            V.tensor_copy(grp[gp, 3:4], bank[5][gp, 0:1])
            link(V.tensor_scalar(kt[0:1, :], iotaK[0:1, 0:MAXPASS], float(NPAIR), None, ALU.mult))
            link(V.tensor_scalar(kt[0:1, :], kt[0:1, :], bank[4][0:1, 32:33], None, ALU.is_lt))
            link(V.tensor_reduce(grp[0:1, 6:7], kt[0:1, :], AX.X, ALU.add))
            V.tensor_copy(npass[0:1, :], grp[0:1, 6:7]).then_inc(sem("npass_ready"), 1)

            def pair_tables(p):
                V.tensor_tensor(grp[gp, 4:5], grp[gp, 3:4], grp[gp, 2:3], ALU.add)
                V.tensor_tensor(grp[gp, 5:6], grp[gp, 0:1], grp[gp, 3:4], ALU.subtract).then_inc(sem("g1"), 1)
                v.wait_ge(sem("g1"), p + 1)
                V.tensor_scalar(grp[gp, 5:6], grp[gp, 5:6], -float(RW), None, ALU.mult)
                V.tensor_scalar(from_[gp, :], iotaK[gp, :], grp[gp, 3:4], None, ALU.is_ge).then_inc(sem("g2"), 1)
                v.wait_ge(sem("g2"), p + 1)
                V.scalar_tensor_tensor(inside[gp, :], iotaK[gp, :], grp[gp, 4:5], from_[gp, :], ALU.is_lt, ALU.mult)
                V.tensor_scalar(tv[gp, :], iotaK[gp, :], -float(RW), grp[gp, 5:6], ALU.mult, ALU.add).then_inc(sem("g3"), 1)
                v.wait_ge(sem("g3"), p + 1)
                V.tensor_scalar(grp[gp, 3:4], grp[gp, 3:4], -float(NPAIR), None, ALU.add)
                V.tensor_tensor(wneg[gp, :], tv[gp, :], inside[gp, :], ALU.mult).then_inc(sem("picks"), 1)
                v.wait_ge(sem("table_psum"), p + 1)
                V.tensor_scalar(wk[0:1, :], bank[4][0:1, 0:NPAIR], -1.0 / RW, 0.25, ALU.mult, ALU.add)
                V.tensor_copy(loT.rearrange("p (k j) -> p k j", j=CH), bank[2][:, 0:NPAIR * CH].rearrange("p (j k) -> p k j", j=CH))
                V.tensor_copy(qT.rearrange("p (k j) -> p k j", j=CH),
                              bank[3][:, 0:NPAIR * CH].rearrange("p (j k) -> p k j", j=CH)).then_inc(sem("tables"), 1)
                v.wait_ge(sem("tables"), p + 1)

            def onehots(base, off, slot):
                at_least(v, "counted", base - LB)
                lo = loT[:, bass.ds(off * CH, LC)].unsqueeze(1).to_broadcast([P, P, LC])
                V.tensor_tensor(L_ring[:, slot, :, :], iotaL, lo, ALU.is_equal)
                for k in range(LB):
                    at_least(v, "counted", base + (k + 1 - RR))
                    for j in range(CH):
                        ins = V.tensor_scalar(R_ring[:, k % RR, j, :], iotaR, qT[:, bass.ds(off * CH + (k * CH + j), 1)],
                                              None, ALU.is_equal)
                    ins.then_inc(sem("onehots"), 1)

            pair_tables(0)
            for b in range(NB):
                t = b - B_LN
                if t == 0:
                    v.wait_ge(sem("ld_x"), 32)
                if 0 <= t < T:
                    ln_stats(t, x[:, t, :])
                onehots(b * LB, b * LB, b % 2)
                if b <= K:
                    score_weights(b)
                if 0 <= t < T:
                    ln_norm(t, x[:, t, :], xh_ring[:, t % 2, :])
                if 0 <= b - B_EVAC < T:
                    evac_a(b - B_EVAC)
                if b == B_EVAC + T:
                    scores()
            exponents()
            v.wait_ge(sem("npass_ready"), 1)
            n = v.value_load(npass[0:1, 0:1], min_val=1, max_val=MAXPASS)
            with v.If(n > 1):
                with v.Fori(1, n) as p:
                    v.wait_ge(sem("added"), p * NPAIR)
                    pair_tables(p)
                    v.sem_inc(sem("dve_step"), 1)
                    with v.Fori(0, NB // 2) as i:
                        for b in range(2):
                            onehots(p * NPAIR + i * 2 * LB + b * LB, i * 2 * LB + b * LB, b)

            v.wait_ge(sem("hist_done"), 1)
            for h in range(H):
                v.wait_ge(sem(f"thr_ld{h % 2}"), 16 * (h // 2 + 1))
                for s in range(T):
                    i = h * T + s
                    if i >= RZ:
                        v.wait_ge(sem("cz_used"), i - RZ + 1)
                    if s in BY_ACT:
                        m = h * len(BY_ACT) + BY_ACT.index(s)
                        v.wait_ge(sem("z_made"), m + 1)
                        V.tensor_tensor(cz[:, i % RZ, :], zmask[m % 2], C[:, s, :], ALU.mult).then_inc(sem("cz_made"), 1)
                    else:
                        V.scalar_tensor_tensor(cz[:, i % RZ, :], thr_bc[:, h % 2, :], sc[:, s, H + h:H + h + 1],
                                               C[:, s, :], ALU.is_le, ALU.mult).then_inc(sem("cz_made"), 1)
            v.wait_ge(sem("nacc_made"), H)

            def token_sum(t):
                v.wait_ge(sem("xT_ready"), T + t + 1)
                V.tensor_reduce(msum[:, t, :], x2T[:, t, :, :], AX.X, ALU.add)

            for t in range(T):
                v.wait_ge(sem("U_done"), t + 1)
                for g2 in range(2):
                    hh = slice(4 * g2, 4 * g2 + 4)
                    ins = V.tensor_tensor(num[:, hh, :], bank[2 * (t % 2) + g2][:, 0:4 * FE].rearrange("p (h f) -> p h f", f=FE),
                                          bc(A2[:, t, hh], [P, 4, FE]), ALU.mult)
                ins.then_inc(sem("U_used"), 1)
                v.wait_ge(sem("U_used"), t + 1)
                link(V.tensor_tensor(num[:, :, :], num[:, :, :], nacc[:, t, :, :], ALU.add))
                link(V.tensor_scalar(rden[:, :], num[:, :, F], 1e-30, None, ALU.max))
                link(V.reciprocal(rden[:, :], rden[:, :]))
                link(V.tensor_tensor(num[:, :, 0:F], num[:, :, 0:F], bc(rden, [P, H, F]), ALU.mult))
                xt = x[:, t, :]
                V.tensor_tensor(xt.rearrange("p (h f) -> p h f", f=F), xt.rearrange("p (h f) -> p h f", f=F),
                                num[:, :, 0:F], ALU.add).then_inc(sem("x2_made"), 1)
                v.wait_ge(sem("x2_made"), t + 1)
                ln_stats(T + t, xt)
                ln_norm(T + t, xt, xh_ring[:, t % 2, :])
                if t >= 2:
                    token_sum(t - 2)
            token_sum(T - 2)
            token_sum(T - 1)
            v.wait_ge(sem("deg_made"), T)
            V.tensor_scalar(deg[:, :], deg[:, :], 1.0, None, ALU.add).then_inc(sem("dis_in"), 1)
            v.wait_ge(sem("dis_in"), 1)
            link(V.tensor_reduce(mean, msum.rearrange("p t k -> p k t"), AX.X, ALU.add))
            V.tensor_scalar(mean, mean, 1.0 / NODES, None, ALU.mult).then_inc(sem("mean_ready"), 1)
            v.wait_ge(sem("dis_sqrt"), 1)
            link(V.reciprocal(dis[:, :], dis[:, :]))
            v.wait_ge(sem("gate_psum"), 1)
            v.wait_ge(sem("ld_w1"), 80)
            link(V.tensor_tensor(gt[0:1, 0, :], bank[2][0:1, 0:E0], bg[:, :], ALU.add))
            V.tensor_reduce(gs[0:1, 0:1], gt[0:1, 0, :], AX.X, ALU.max, negate=True).then_inc(sem("gate_in"), 1)
            v.wait_ge(sem("gate_exp"), 1)
            link(V.tensor_reduce(gs[0:1, 2:3], gt[0:1, 1, :], AX.X, ALU.max))
            link(V.tensor_scalar(gt[0:1, 2, :], gt[0:1, 1, :], gs[0:1, 2:3], None, ALU.is_ge))
            link(V.tensor_tensor(gt[0:1, 2, :], gt[0:1, 2, :], iota16[0:1, :], ALU.mult))
            link(V.tensor_reduce(gs[0:1, 3:4], gt[0:1, 2, :], AX.X, ALU.min))
            V.tensor_scalar(gidx[0:1, :], gs[0:1, 3:4], 99.0, None, ALU.add).then_inc(sem("gate_idx"), 1)
            V.reciprocal(gs[0:1, 4:5], gs[0:1, 1:2]).then_inc(sem("gate_made"), 1)
            v.wait_ge(sem("gate_bc"), 1)
            link(V.tensor_copy(gs[:, 5:6], bank[7][:, 0:1]))
            v.wait_ge(sem("ld_we"), 32)

            def x3(t):
                v.wait_ge(sem("ff_done"), t + 1)
                tmp = num[:, :, :].rearrange("p h f -> p (h f)")[:, 0:D]
                V.tensor_tensor(tmp, bank[2 + t % 2][:, :], be_bc[:, :], ALU.add).then_inc(sem("ff_used"), 1)
                v.wait_ge(sem("ff_used"), t + 1)
                link(V.scalar_tensor_tensor(x[:, t, :], tmp, gs[:, 5:6], x[:, t, :], ALU.mult, ALU.add))
                ln_stats(2 * T + t, x[:, t, :])
                ln_norm(2 * T + t, x[:, t, :], xh_ring[:, t % 2, :])

            def message(t):
                v.wait_ge(sem("linC"), t + 1)
                if t >= 2:
                    v.wait_ge(sem("h_lo"), t - 1)
                V.tensor_tensor(hs[:, t % 2, :], bank[4 + t % 2][:, :], gb_bc[:, :], ALU.add).then_inc(sem("h_used"), 1)
                v.wait_ge(sem("h_used"), t + 1)
                V.tensor_scalar(hs[:, t % 2, :], hs[:, t % 2, :], dis[:, t:t + 1], None, ALU.mult).then_inc(sem("hs_made"), 1)

            for t in range(T + 1):
                if t < T:
                    x3(t)
                if t >= 1:
                    message(t - 1)

            def logits(t):
                v.wait_ge(sem("linD"), t + 1)
                V.tensor_tensor(lg[:, t, :], bank[2 + t % 2][:, 0:E1], br_bc[:, :], ALU.add).then_inc(sem("lg_made"), 1)

            for t in range(T + 1):
                if t < T:
                    v.wait_ge(sem("x4_made"), t + 1)
                    ln_stats(3 * T + t, x[:, t, :])
                    ln_norm(3 * T + t, x[:, t, :], xh4[:, t, :])
                if t >= 1:
                    logits(t - 1)
            v.wait_ge(sem("lg_made"), T)
            S3 = [P, T, E1]
            link(V.tensor_reduce(mx10, lg, AX.X, ALU.max))
            V.tensor_tensor(ex, lg, bc(mx10, S3), ALU.subtract).then_inc(sem("rt_in"), 1)
            v.wait_ge(sem("rt_exp"), 1)
            link(V.tensor_reduce(G, ex, AX.X, ALU.add))
            V.reciprocal(G, G)
            link(V.tensor_reduce(mx10, ex, AX.X, ALU.max))
            link(V.tensor_tensor(eq, ex, bc(mx10, S3), ALU.is_ge))
            i8 = iota8[:, :].unsqueeze(1).to_broadcast(S3)
            link(V.tensor_tensor(eq, eq, i8, ALU.mult))
            link(V.tensor_reduce(em, eq, AX.X, ALU.min))
            V.tensor_tensor(oh, i8, bc(em, S3), ALU.is_equal).then_inc(sem("oh_made"), 1)
            v.wait_ge(sem("rank_psum"), 1)
            flat = lambda ap: ap.rearrange("p t e -> p (t e)")
            V.memset(pre[:, 0, :], 0.0)
            link(V.tensor_copy(flat(tot), bank[3][:, 0:T * E1]))
            for t in range(T):
                link(V.tensor_tensor(pre[:, t + 1, :], pre[:, t, :], tot[:, t, :], ALU.add))
            link(V.tensor_tensor(cmp_, iotaM[:, :].unsqueeze(1).to_broadcast([P, E1, T]), bc(pre[:, T, :], [P, E1, T]), ALU.is_lt))
            link(V.tensor_reduce(tl, cmp_, AX.X, ALU.add))
            link(V.tensor_tensor_scan(cum, ones[:, 0:E1], tl, 0.0, ALU.mult, ALU.add))
            link(V.tensor_tensor(base, cum, tl, ALU.subtract))
            V.tensor_tensor(tcmp, bc(iotaJ[:, :], [P, NT, E1 - 1]), cum[:, 0:E1 - 1].unsqueeze(1).to_broadcast([P, NT, E1 - 1]), ALU.is_ge)
            link(V.tensor_scalar(base, base, float(P), None, ALU.mult))
            link(V.tensor_reduce(te_f, tcmp, AX.X, ALU.add))
            V.tensor_copy(te, te_f).then_inc(sem("te_ready"), 1)
            link(V.tensor_tensor(slot, pre[:, 0:T, :], base.unsqueeze(1).to_broadcast(S3), ALU.add))
            link(V.tensor_tensor(flat(slot), flat(slot), bank[2][:, 0:T * E1], ALU.add))
            link(V.tensor_tensor(slot, slot, oh, ALU.mult))
            link(V.tensor_reduce(pos_f, slot, AX.X, ALU.add))
            V.tensor_copy(pos, pos_f).then_inc(sem("pos_ready"), 1)

            def h_evac(j):
                v.wait_ge(sem("m1_done"), j + 1)
                v.wait_ge(sem(f"ld_b{j % RB}"), 32 * (j // RB + 1))
                if j >= 2:
                    v.wait_ge(sem("hT_psum"), j - 1)
                V.tensor_tensor(h_sb[:, j % 2, :], bank[6 + j % 2][:, :], b1_bc[:, j % RB, :], ALU.add).then_inc(sem("h1_made"), 1)

            def y_evac(j):
                v.wait_ge(sem("m2_done"), j + 1)
                if j >= RY:
                    v.wait_ge(sem(f"y_st{j % RY}"), 16 * (j // RY))
                V.tensor_tensor(y_sb[:, j % RY, :], bank[2 + j % 2][:, :], b2_bc[:, j % RB, :], ALU.add).then_inc(sem("y_made"), 1)

            h_evac(0)
            for j in range(NT):
                if j + 1 < NT:
                    h_evac(j + 1)
                y_evac(j)
            for t in range(T):
                v.wait_ge(sem(f"gathered{t}"), 16)
                V.scalar_tensor_tensor(yg[:, t, :], yg[:, t, :], G[:, t:t + 1], x[:, t, :], ALU.mult, ALU.add).then_inc(sem("final"), 1)

        @block.tensor
        def _(pe):
            mm = nc.tensor.matmul

            def transposes(src, b, name):
                for k in range(K):
                    ins = nc.tensor.transpose(b[:, k * P:(k + 1) * P], src[:, k * P:(k + 1) * P], ident[:, :])
                ins.then_inc(sem(name), 1)

            def tile_T(n, src, b):
                pe.wait_ge(sem("xh_made"), n + 1)
                if n >= 2:
                    pe.wait_ge(sem("xT_ready"), n - 1)
                transposes(src, b, "xt_psum")

            def linear(lhs, rhs, out, name=None):
                for k in range(K):
                    ins = mm(out, lhs[:, k, :], rhs(k), start=k == 0, stop=k == K - 1)
                if name:
                    ins.then_inc(sem(name), 1)

            pe.wait_ge(sem("pc"), 3)
            pe.wait_ge(sem("n_ready"), 1)
            mm(bank[5][0:NG, 0:1], tri[0:NG, 0:NG], grp[0:NG, 2:3], start=True, stop=True)
            mm(bank[4][0:1, 32:33], ones[0:NG, 0:1], grp[0:NG, 2:3], start=True, stop=True).then_inc(sem("rb_psum"), 1)

            def lin_a(t):
                if t == 0:
                    pe.wait_ge(sem("wa_ready"), 1)
                pe.wait_ge(sem("xT_ready"), t + 1)
                if t >= 2:
                    pe.wait_ge(sem("evacA"), t - 1)
                xT = xT_ring[:, t % 2, :, :]
                linear(xT, lambda k: W0[:, k, :, :].rearrange("p h f -> p (h f)"), bank[2 + t % 2][:, :])
                linear(xT, lambda k: Wa[:, k, :], bank[4 + t % 2][:, 0:2 * H], "linA")

            def second_weights():
                pe.wait_ge(sem("xT_ready"), T)
                pe.wait_ge(sem("ld_gw"), 16)
                for k in range(K):
                    if k >= 2:
                        pe.wait_ge(sem("gwT_ready"), k - 1)
                    for o in range(K):
                        ins = nc.tensor.transpose(bank[6 + k % 2][:, o * P:(o + 1) * P], gW[:, o, k * P:(k + 1) * P], ident[:, :])
                    ins.then_inc(sem("gwT_psum"), 1)

            def thresholds():
                pe.wait_ge(sem("thr_made"), 1)
                pe.wait_ge(sem("gwT_ready"), K)
                for i, n in enumerate((4, 4, 2)):
                    for q in range(n):
                        ins = nc.tensor.transpose(bank[5 + i][0:H, q * P:(q + 1) * P], thr[:, 4 * i + q, :], ident[:, :])
                    ins.then_inc(sem("thrT_psum"), 1)

            def pair_matmuls(p):
                pe.wait_ge(sem("picks"), p + 1)
                for j in range(CH):
                    e = slice(j * P, (j + 1) * P)
                    o = slice(j * NPAIR, (j + 1) * NPAIR)
                    mm(bank[2][:, o], lo_f[0:NG, e], inside[0:NG, :], start=True, stop=True)
                    mm(bank[3][:, o], q_f[0:NG, e], inside[0:NG, :], start=True, stop=False)
                    mm(bank[3][:, o], ones[0:NG, :], wneg[0:NG, :], start=False, stop=True)
                mm(bank[4][0:1, 0:NPAIR], ones[0:NG, 0:1], wneg[0:NG, :], start=True, stop=True).then_inc(sem("table_psum"), 1)

            def count(base, slot):
                for k in range(LB):
                    pe.wait_ge(sem("onehots"), base + (k + 1))
                    at_least(pe, "staged", base + (k - 1))
                    for j in range(CH):
                        ins = mm(bank[k % 2][:, 0:RW], L_ring[:, slot, :, k * CH + j], R_ring[:, k % RR, j, :],
                                 start=j == 0, stop=j == CH - 1)
                    ins.then_inc(sem("counted"), 1)

            pair_matmuls(0)
            for b in range(NB):
                count(b * LB, b % 2)
                t = b - B_LN
                if 0 <= t < T:
                    tile_T(t, xh_ring[:, t % 2, :], bank[6 + t % 2])
                if 0 <= t - 1 < T:
                    lin_a(t - 1)
                if b == B_GW:
                    second_weights()
                if b == B_CS:
                    thresholds()
            n = pe.value_load(npass[0:1, 0:1], min_val=1, max_val=MAXPASS)
            with pe.If(n > 1):
                with pe.Fori(1, n) as p:
                    pair_matmuls(p)
                    with pe.Fori(0, NB // 2) as i:
                        for b in range(2):
                            count(p * NPAIR + i * 2 * LB + b * LB, b)

            pe.wait_ge(sem("hist_done"), 1)
            pe.wait_ge(sem("thrT_ready"), 3)
            for h in range(H):
                if h >= 2:
                    pe.wait_ge(sem("raw_made"), 4 * (h - 1))
                for b in range(4):
                    w = min(3, T - 3 * b) * 2 * FE
                    mm(bank[4 * (h % 2) + b][:, 0:w], zero16[:, 0:P], zero16[:, 0:w], start=True, stop=False)
                pe.wait_ge(sem("v_lo"), 2 * h + 2)
                for s in range(T):
                    i = h * T + s
                    pe.wait_ge(sem("cz_made"), i + 1)
                    for t in range(T):
                        for part in range(2):
                            ins = mm(acc_region(h, t), cz[:, i % RZ, t * P:(t + 1) * P],
                                     VP[:, s, part, h, :, :].rearrange("p b f -> p (b f)"), start=False,
                                     stop=s == T - 1 and part == 1 and (t % 3 == 2 or t == T - 1))
                    ins.then_inc(sem("cz_used"), 1)
                pe.wait_ge(sem("cz_used"), (h + 1) * T)
                pe.sem_inc(sem("acc_done"), 1)
            def all_edges(t):
                if t >= 2:
                    pe.wait_ge(sem("U_used"), t - 1)
                for g2 in range(2):
                    for s in range(T):
                        for part in range(2):
                            ins = mm(bank[2 * (t % 2) + g2][:, 0:4 * FE].rearrange("p (h f) -> p h f", f=FE), C[:, s, t * P:(t + 1) * P],
                                     VP[:, s, part, 4 * g2:4 * g2 + 4, 1, :], start=s == 0 and part == 0,
                                     stop=s == T - 1 and part == 1)
                ins.then_inc(sem("U_done"), 1)

            pe.wait_ge(sem("raw_made"), 4 * (H - 1))
            all_edges(0)
            all_edges(1)
            pe.wait_ge(sem("raw_made"), 4 * H)
            for t in range(T):
                tile_T(T + t, xh_ring[:, t % 2, :], bank[4 + t % 2])
                if t + 2 < T:
                    all_edges(t + 2)
            pe.wait_ge(sem("mean_ready"), 1)
            pe.wait_ge(sem("ld_w1"), 80)
            for k in range(K):
                ins = mm(bank[2][0:1, 0:E0], mean[:, k:k + 1], Wg[:, k, :], start=k == 0, stop=k == K - 1)
            ins.then_inc(sem("gate_psum"), 1)
            pe.wait_ge(sem("gate_made"), 1)
            mm(bank[7][:, 0:1], ones[0:1, :], gs[0:1, 4:5], start=True, stop=True).then_inc(sem("gate_bc"), 1)
            pe.wait_ge(sem("ld_we"), 32)

            def ff(t):
                pe.wait_ge(sem("xT_ready"), T + t + 1)
                if t >= 2:
                    pe.wait_ge(sem("ff_used"), t - 1)
                linear(x2T[:, t, :, :], lambda k: We[:, k, :], bank[2 + t % 2][:, :], "ff_done")

            def lin_c(t):
                pe.wait_ge(sem("xT_ready"), 2 * T + t + 1)
                if t >= 2:
                    pe.wait_ge(sem("h_used"), t - 1)
                linear(xT_ring[:, t % 2, :, :], lambda k: gWT[:, k, :], bank[4 + t % 2][:, :], "linC")

            ff(0)
            ff(1)
            for t in range(T):
                tile_T(2 * T + t, xh_ring[:, t % 2, :], bank[t % 2])
                if t + 2 < T:
                    ff(t + 2)
                lin_c(t)
            pe.wait_ge(sem("loops"), 1)
            pe.wait_ge(sem("h_lo"), T)

            def agg(t):
                if t >= 2:
                    pe.wait_ge(sem("relu_made"), t - 1)
                for s in range(T):
                    for part in range(2):
                        ins = mm(bank[6 + t % 2][:, :], C[:, s, t * P:(t + 1) * P], hp[:, s, part, :],
                                 start=s == 0 and part == 0, stop=s == T - 1 and part == 1)
                ins.then_inc(sem("agg_done"), 1)

            def lin_d(t):
                pe.wait_ge(sem("xT_ready"), 3 * T + t + 1)
                if t >= 2:
                    pe.wait_ge(sem("lg_made"), t - 1)
                linear(xT_ring[:, t % 2, :, :], lambda k: Wr[:, k, :], bank[2 + t % 2][:, 0:E1], "linD")

            agg(0)
            agg(1)
            for t in range(T):
                tile_T(3 * T + t, xh4[:, t, :], bank[t % 2])
                if t + 2 < T:
                    agg(t + 2)
                lin_d(t)
            pe.wait_ge(sem("oh_made"), 1)
            pe.wait_ge(sem("lg_made"), T)
            ohf = oh.rearrange("p t e -> p (t e)")
            mm(bank[2][:, 0:T * E1], tri[:, :], ohf, start=True, stop=True)
            mm(bank[3][:, 0:T * E1], ones[:, :], ohf, start=True, stop=True).then_inc(sem("rank_psum"), 1)

            def token_T(j):
                pe.wait_ge(sem(f"ld_xp{j % RX}"), 16 * (j // RX + 1))
                if j >= 2:
                    pe.wait_ge(sem("xpT"), j - 1)
                transposes(xp[:, j % RX, :], bank[4 + j % 2], "xpT_psum")

            def m1(j, e):
                pe.wait_ge(sem("xpT"), j + 1)
                if j >= 2:
                    pe.wait_ge(sem("h1_made"), j - 1)
                linear(xT_ring[:, j % 2, :, :], lambda k: W1[:, bass.ds(e, 1), k, :].rearrange("p a f -> p (a f)"), bank[6 + j % 2][:, :], "m1_done")

            def hidden_T(j):
                pe.wait_ge(sem("h1_made"), j + 1)
                if j >= 2:
                    pe.wait_ge(sem("hT_ready"), j - 1)
                transposes(h_sb[:, j % 2, :], bank[j % 2], "hT_psum")

            def m2(j, e):
                pe.wait_ge(sem("hT_ready"), j + 1)
                if j >= 2:
                    pe.wait_ge(sem("y_made"), j - 1)
                linear(hT[:, j % 2, :, :], lambda k: W2[:, bass.ds(e, 1), k, :].rearrange("p a f -> p (a f)"), bank[2 + j % 2][:, :], "m2_done")

            pe.wait_ge(sem("te_ready"), 1)
            pe.wait_ge(sem("pos_ready"), 1)
            ex_of = lambda j: pe.value_load(te[0:1, j:j + 1], min_val=0, max_val=E1 - 1)
            token_T(0)
            pe.wait_ge(sem("ld_W1"), 16 * E1)
            e = ex_of(0)
            m1(0, e)
            token_T(1)
            e_next = ex_of(1)
            for j in range(NT):
                if j + 1 < NT:
                    m1(j + 1, e_next)
                hidden_T(j)
                if j + 2 < NT:
                    token_T(j + 2)
                    e_after = ex_of(j + 2)
                if j == 0:
                    pe.wait_ge(sem("ld_W2"), 16 * E1)
                m2(j, e)
                e, e_next = e_next, e_after


_INS = ['x', 'src', 'dst', 'L0_gnn_Ws', 'L0_gnn_Wb', 'L0_gnn_a_w', 'L0_gnn_a_b', 'L0_ffn_Wg', 'L0_ffn_bg',
        'L0_ffn_We', 'L0_ffn_be', 'L1_gnn_W', 'L1_gnn_b', 'L1_ffn_Wr', 'L1_ffn_br', 'L1_ffn_W1', 'L1_ffn_b1',
        'L1_ffn_W2', 'L1_ffn_b2']


def kernel(**inputs):
    import concourse.bacc as _bacc
    from concourse.bass_utils import run_bass_kernel_spmd as _run

    nc = _bacc.Bacc("TRN2", target_bir_lowering=False, num_devices=1)
    arrays, args = {}, []
    for name in _INS:
        a = np.ascontiguousarray(inputs[name])
        arrays[f"in_{name}"] = a
        args.append(nc.dram_tensor(f"in_{name}", a.shape, mybir.dt.from_np(a.dtype), kind="ExternalInput").ap())
    args.append(nc.dram_tensor("out", (NODES, D), F32, kind="ExternalOutput").ap())
    gnn_ffn_kernel(nc, *args)
    r = _run(nc, [arrays], core_ids=[0])
    return r.results[0]["out"]
```

```python
import numpy as np
import concourse.bass as bass
from concourse import mybir
from contextlib import ExitStack

F32 = mybir.dt.float32
F16 = mybir.dt.float16
I32 = mybir.dt.int32
ALU = mybir.AluOpType
ACT = mybir.ActivationFunctionType
AX = mybir.AxisListType

P = 128
NODES, D = 1250, 512
T = (NODES + P - 1) // P
NP = T * P
LAST = NODES - (T - 1) * P
K = D // P

EDGES = 40000
CH = 3
GE = CH * P
NG = (EDGES + GE - 1) // GE
GLAST = EDGES - (NG - 1) * GE
WN = 32
NW = NP // WN
RW = WN * T
NPAIR = NG + NW - 1
LB = 8
LC = LB * CH
NB = NPAIR // LB
MAXPASS = (NG * NW + NPAIR - 1) // NPAIR
HB = LB // 2
HC = HB * CH
RS = 8

H, F = 8, 64
FE = F + 1
E0, E1 = 16, 8
S1 = 208
SPILL = E1 * S1
NO = (NODES - S1 + P - 1) // P
ROW = D + 3 + E1
FAR = 4096
WS = 256.0
RZ = 4
BY_ACT = (1, 3, 4, 5, 7, 9)
STEEP = 1e30
RX = 4
RW32 = 6
BEGIN = {1 + t: t for t in range(T)}
B_GW = max(BEGIN) + 2
B_CS = B_GW + 2
EPS = 1e-5
SLOPE = 0.2


def gnn_ffn_kernel(nc, x_d, src_d, dst_d, Ws_d, Wb_d, aw_d, ab_d, Wg_d, bg_d, We_d, be_d, gW_d, gb_d,
                   Wr_d, br_d, W1_d, b1_d, W2_d, b2_d, out_d):
    ctx = ExitStack()
    with ctx:
        def sb(name, shape, dt=F32):
            return ctx.enter_context(nc.sbuf_tensor(name, shape, dt))

        sems = {}

        def sem(name):
            if name not in sems:
                sems[name] = ctx.enter_context(nc.semaphore(name))
            return sems[name]

        def carve(region, at, shape, dt=F32):
            n = int(np.prod(shape))
            words = n if dt in (F32, I32) else (n + 1) // 2
            v = region[:, at:at + words]
            if dt != F32:
                v = v.bitcast(dt)
            if len(shape) > 1:
                names = " ".join(f"a{i}" for i in range(len(shape)))
                v = v.rearrange(f"p ({names}) -> p {names}", **{f"a{i}": s for i, s in enumerate(shape)})
            return v, at + words

        row = sb("row", [P, T, ROW])
        x = row[:, :, 0:D]
        ident = sb("ident", [P, P])
        ident16 = sb("ident16", [P, P], F16)
        tri = sb("tri", [P, P])
        ones = sb("ones", [P, P])
        zero16 = sb("zero16", [P, 400], F16)
        xh_ring = sb("xh_ring", [P, 2, D])
        xT_ring = sb("xT_ring", [P, 2, K, P])
        gb_bc = sb("gb_bc", [P, D])
        be_bc = sb("be_bc", [P, D])
        num = sb("num", [P, H, FE])
        Wg = sb("Wg", [P, K, E0])
        Wr = sb("Wr", [P, K, E1])
        bg = sb("bg", [1, E0])
        br_bc = sb("br_bc", [P, E1])
        b1_nat = sb("b1_nat", [E1 * K, P])
        b1T = sb("b1T", [P, E1, K])
        st = sb("st", [P, 2, 6])
        mv = sb("mv", [P, 2, 2])
        ve = sb("ve", [P, 2])
        sd = sb("sd", [P, 2])
        rs = sb("rs", [P, 2])
        deg = sb("deg", [P, T])
        dis = sb("dis", [P, T])
        iota8 = sb("iota8", [P, E1])
        iota16 = sb("iota16", [P, E0])
        small = sb("small", [P, 1536])

        mid = sb("mid", [P, E1 * K * D])
        C, o = carve(mid, 0, [T, NP], F16)
        gWT, o = carve(mid, o, [K, D])
        free0 = o
        hp, o = carve(mid, o, [T, 2, D], F16)
        We, o = carve(mid, o, [K, D])
        Wx, o = carve(mid, free0, [T, H, FE])
        raw0, o = carve(mid, o, [T, 2, FE])
        z0, o = carve(mid, o, [NP], F16)

        big = sb("big", [P, E1 * K * D])
        src_i, o = carve(big, 0, [GE], I32)
        dst_i, o = carve(big, o, [GE], I32)
        lo_i, o = carve(big, o, [GE], I32)
        hi_i, o = carve(big, o, [GE], I32)
        w_i, o = carve(big, o, [GE], I32)
        lo_f, o = carve(big, o, [GE])
        q_f, o = carve(big, o, [GE])
        iotaL, o = carve(big, o, [P, LC], F16)
        L_ring, o = carve(big, o, [2, P, LC], F16)
        R_ring, o = carve(big, o, [2, RW, HC], F16)
        stage, o = carve(big, o, [RS, T, WN], F16)
        loT, o = carve(big, o, [NPAIR * CH], F16)
        qT, o = carve(big, o, [NPAIR * CH], F16)
        iotaK, o = carve(big, o, [NPAIR])
        from_, o = carve(big, o, [NPAIR])
        inside, o = carve(big, o, [NPAIR])
        tv, o = carve(big, o, [NPAIR])
        wneg, o = carve(big, o, [NPAIR])
        wk, o = carve(big, o, [NPAIR], I32)
        W0, o = carve(big, o, [K, H, F])
        VP, o = carve(big, 0, [T, 2, H, 2, FE], F16)
        nacc, o = carve(big, o, [T, H, FE])
        z1, o = carve(big, o, [NP], F16)
        unit = 2 * K * D
        W32 = [carve(big, i * unit, [2, K, D])[0] for i in range(3)] + \
              [carve(mid, unit // 2 + i * unit, [2, K, D])[0] for i in range(3)]
        W16 = [[carve(big, 3 * unit + l * K * D, [2, K, D], F16)[0] for l in range(2)],
               [carve(mid, 0, [2, K, D], F16)[0], carve(mid, unit // 2 + 3 * unit, [2, K, D], F16)[0]]]

        aux = sb("aux", [P, T * D])
        thr_bc, _ = carve(aux, 0, [2, NP])
        x2T, _ = carve(aux, 0, [T, K, P])
        xs, o = carve(aux, 0, [RX, 2, ROW])
        ids, o = carve(aux, o, [RX, 2], I32)

        iotaR, o = carve(aux, 2 * NP, [RW, HC], F16)
        Wb_bc, o = carve(aux, o, [H, F])
        a_blk, o = carve(aux, 0, [K, 2 * H])
        WbT, o = carve(aux, o, [K])
        a_nat, o = carve(aux, o, [3, 2, F])
        raw1, o = carve(aux, 2 * NP, [T, 2, FE])
        junk, o = carve(aux, o, [NP], F16)
        work = sb("work", [P, 2 * T * FE + RZ * NP // 2])
        vtmp, o = carve(work, 0, [2, T, FE])
        cz, o = carve(work, o, [RZ, NP], F16)
        xT16, o = carve(work, 0, [2, 2, K, S1], F16)
        hT16, o = carve(work, o, [2, 2, K, S1], F16)
        h32 = xT_ring[:, :, :, :].rearrange("p a k m -> p (a k m)")[:, 0:4 * S1].rearrange("p (a b m) -> p a b m", a=2, b=2)
        b2_ring = [gb_bc, be_bc]
        W0T, _ = carve(work, 0, [2, D])
        thrT, _ = carve(work, 0, [NP])
        hs, o = carve(work, 0, [2, D])
        rtmp, o = carve(work, o, [2, D])
        gW, _ = carve(work, 1812, [K, D])
        zero, _ = carve(work, NP, [1, ROW])
        raw = [raw0, raw1]
        zmask = [z0, z1]

        at = 0
        Wa, at = carve(small, at, [K, 2 * H])
        cb, at = carve(small, at, [2 * H])
        ab_bc, at = carve(small, at, [H])
        sc, at = carve(small, at, [T, 2 * H])
        atb, at = carve(small, at, [T, H])
        thr, at = carve(small, at, [T, H])
        asmax, at = carve(small, at, [H])
        cs, at = carve(small, at, [H])
        zz, at = carve(small, at, [T, H])
        ll, at = carve(small, at, [T, H])
        e1t, at = carve(small, at, [T, H])
        e2t, at = carve(small, at, [T, H])
        d1t, at = carve(small, at, [T, H])
        A1, at = carve(small, at, [T, H])
        A2, at = carve(small, at, [T, H])
        B1, at = carve(small, at, [T, H])
        B2, at = carve(small, at, [T, H])
        steep, at = carve(small, at, [T, H])
        grp, at = carve(small, at, [8])
        kt, at = carve(small, at, [MAXPASS])
        npass, at = carve(small, at, [1], I32)
        rden, at = carve(small, at, [H])
        msum, at = carve(small, at, [T, K])
        mean, at = carve(small, at, [K])
        gt, at = carve(small, at, [4, E0])
        gs, at = carve(small, at, [8])
        gidx, at = carve(small, at, [1], I32)
        at = 0
        lg, at = carve(small, at, [T, E1])
        mx10, at = carve(small, at, [T])
        em, at = carve(small, at, [T])
        oh, at = carve(small, at, [T, E1])
        osum, at = carve(small, at, [T, E1])
        eq, at = carve(small, at, [T, E1])
        rank, at = carve(small, at, [T])
        first, at = carve(small, at, [T])
        over, at = carve(small, at, [T])
        pos, at = carve(small, at, [T], I32)
        cmp_, at = carve(small, at, [E1, NO])
        tl, at = carve(small, at, [E1])
        cum, at = carve(small, at, [E1])
        base, at = carve(small, at, [E1])
        tcmp, at = carve(small, at, [NO, E1 - 1])
        te_f, at = carve(small, at, [NO])
        te, at = carve(small, at, [NO], I32)
        nspill, at = carve(small, at, [1], I32)
        b1o, at = carve(small, at, [K])
        gsum, at = carve(small, at, [RX, 2])
        gate, at = carve(small, at, [RX, 2])
        gate_ws, at = carve(small, at, [RX, 2])
        iotaM = sb("iotaM", [P, NO])
        iotaJ = sb("iotaJ", [P, NO])
        valid = sb("valid", [P, 1])

        bank = [ctx.enter_context(nc.psum_tensor(f"bank{i}", [P, 512], F32)) for i in range(8)]

        thr_d = nc.dram_tensor("thr_scratch", [H, NP], F32, kind="Internal").ap()
        xp_d = nc.dram_tensor("xperm_scratch", [SPILL + NO * P, ROW], F32, kind="Internal").ap()

        block = ctx.enter_context(nc.Block())

        def at_least(eng, name, value):
            if isinstance(value, int) and value <= 0:
                return
            eng.wait_ge(sem(name), value)

        def bc(ap, shape):
            return ap.unsqueeze(len(ap.shape)).to_broadcast(shape)

        def acc_region(h, t):
            return bank[4 * (h % 2) + t // 3][:, (t % 3) * 2 * FE:(t % 3 + 1) * 2 * FE]

        @block.sync
        def _(sp):
            sp.wait_ge(sem("edge_pads"), 2)
            full = (NG - 1) * GE
            for i_d, i_sb in ((src_d, src_i), (dst_d, dst_i)):
                sp.dma_start(i_sb[0:NG - 1, :], i_d[0:full].rearrange("(g e) -> g e", e=GE)).then_inc(sem("ld_edges"), 16)
                sp.dma_start(i_sb[NG - 1:NG, 0:GLAST], i_d[full:EDGES].rearrange("(g e) -> g e", g=1)).then_inc(sem("ld_edges"), 16)
            for k in range(K):
                sp.dma_start(W0[:, k, :, :], Ws_d[:, k * P:(k + 1) * P, :].rearrange("h p f -> p h f")).then_inc(sem("ld_w0"), 16)
            for c in range(2):
                sp.dma_start(a_nat[0:K, c, :, :], aw_d[:, c * F:(c + 1) * F].rearrange("(b h) f -> b h f", h=2)).then_inc(sem("ld_a"), 16)
            sp.dma_start(a_nat[0:K, 2, :, :], Wb_d.rearrange("(b h) f -> b h f", h=2)).then_inc(sem("ld_a"), 16)
            sp.dma_start(Wb_bc, Wb_d.partition_broadcast(P)).then_inc(sem("ld_w0"), 16)
            sp.dma_start(ab_bc, ab_d.partition_broadcast(P)).then_inc(sem("ld_w0"), 16)
            sp.dma_start(x[:, 0:T - 1, :], x_d[0:(T - 1) * P, :].rearrange("(t p) d -> p t d", p=P)).then_inc(sem("ld_x"), 16)
            sp.wait_ge(sem("x_pad"), 1)
            sp.dma_start(x[0:LAST, T - 1, :], x_d[(T - 1) * P:NODES, :]).then_inc(sem("ld_x"), 16)
            sp.dma_start(gW, gW_d.rearrange("(k p) i -> p k i", p=P)).then_inc(sem("ld_gw"), 16)
            for dst, src in ((gb_bc[:, :], gb_d.partition_broadcast(P)),
                             (Wg[:, :, :], Wg_d.rearrange("(k p) e -> p k e", p=P)),
                             (Wr[:, :, :], Wr_d.rearrange("(k p) e -> p k e", p=P)),
                             (bg[:, :], bg_d.rearrange("(a e) -> a e", a=1)),
                             (br_bc[:, :], br_d.partition_broadcast(P)),
                             (b1_nat[:, :], b1_d.rearrange("e (k p) -> (e k) p", p=P))):
                sp.dma_start(dst, src).then_inc(sem("ld_w1"), 16)
            sp.wait_ge(sem("zero_set"), 1)
            sp.dma_start(xp_d.rearrange("(j p) d -> p j d", p=P),
                         zero[:, 0:1, :].to_broadcast([P, SPILL // P + NO, ROW])).then_inc(sem("xp_zeroed"), 16)
            sp.wait_ge(sem("thrT_ready"), 3)
            sp.dma_start(thr_d, thrT[0:H, :]).then_inc(sem("thr_out"), 16)
            sp.wait_ge(sem("thr_out"), 16)
            for h in range(H):
                if h >= 2:
                    sp.wait_ge(sem("cz_made"), T * (h - 1))
                sp.dma_start(thr_bc[:, h % 2, :], thr_d[h, :].partition_broadcast(P)).then_inc(sem(f"thr_ld{h % 2}"), 16)
            sp.wait_ge(sem("gate_idx"), 1)
            e = sp.value_load(gidx[0:1, 0:1], min_val=0, max_val=E0 - 1)
            sp.dma_start(We, We_d[bass.ds(e, 1), :, :].rearrange("a (k p) o -> p (a k) o", p=P)).then_inc(sem("ld_we"), 16)
            sp.dma_start(be_bc[:, :], be_d[bass.ds(e, 1), :].rearrange("a o -> (a o)").partition_broadcast(P)).then_inc(sem("ld_we"), 16)

            def load_weights(e):
                r = e % RW32
                for l, w_d in enumerate((W1_d, W2_d)):
                    sp.dma_start(W32[r][:, l, :, :], w_d[e].rearrange("(k p) f -> p k f", p=P)).then_inc(sem(f"ld_w32_{r}"), 16)

            def load_b2(e):
                sp.dma_start(b2_ring[e % 2][:, :], b2_d[e].partition_broadcast(P)).then_inc(sem(f"ld_b2_{e % 2}"), 16)

            sp.wait_ge(sem("x2_made"), T)
            for e in range(3):
                load_weights(e)
            sp.wait_ge(sem("h_used"), T)
            load_b2(0)
            load_b2(1)
            sp.wait_ge(sem("scattered"), 16 * T)
            def load_tokens(e):
                sp.dma_start(xs[:, e % RX, :, :], xp_d[e * S1:e * S1 + 2 * P, :].rearrange("(j p) d -> p j d", p=P)).then_inc(sem(f"ld_xs{e % RX}"), 16)

            for e in range(RX):
                load_tokens(e)
            sp.wait_ge(sem("agg_done"), T)
            for e in range(3, RW32):
                load_weights(e)
            for e in range(2, E1):
                if e + RW32 - 3 < E1 and e >= 3:
                    sp.wait_ge(sem("w_lo0"), e - 2)
                    sp.wait_ge(sem("w_lo1"), e - 2)
                    load_weights(e + RW32 - 3)
                sp.wait_ge(sem("b2_used"), e - 1)
                load_b2(e)
                if e + 2 in range(RX, E1):
                    sp.wait_ge(sem(f"put{(e + 2) % RX}"), 32 * ((e + 2) // RX))
                    load_tokens(e + 2)
            for r in range(RX):
                sp.wait_ge(sem(f"put{r}"), 32 * (E1 // RX))
            n = sp.value_load(nspill[0:1, 0:1], min_val=0, max_val=NO)
            sp.sem_inc(sem("o_done"), 1)
            with sp.If(n > 0):
                sp.wait_ge(sem("o_scattered"), 16 * T)
                with sp.Fori(0, n) as i:
                    sp.wait_ge(sem("o_done"), i + 1)
                    sp.sem_inc(sem("sp_step"), 1)
                    e = sp.value_load(te[0:1, bass.ds(i, 1)], min_val=0, max_val=E1 - 1)
                    sp.dma_start(W32[0][:, 0, :, :], W1_d[bass.ds(e, 1), :, :].rearrange("a (k p) f -> p (a k) f", p=P)).then_inc(sem("o_ld"), 16)
                    sp.dma_start(W32[0][:, 1, :, :], W2_d[bass.ds(e, 1), :, :].rearrange("a (k p) f -> p (a k) f", p=P)).then_inc(sem("o_ld"), 16)
                    sp.dma_start(gb_bc[:, :], b2_d[bass.ds(e, 1), :].rearrange("a o -> (a o)").partition_broadcast(P)).then_inc(sem("o_ld"), 16)
                    sp.dma_start(xs[:, 0, 0, :], xp_d[bass.ds(i * P + SPILL, P), :]).then_inc(sem("o_ld"), 16)
                sp.wait_ge(sem("o_done"), n + 1)
                sp.sem_inc(sem("sp_step"), 1)

        @block.gpsimd
        def _(g):
            nc.gpsimd.memset(src_i[96:NG, :], 0).then_inc(sem("edge_pads"), 1)
            nc.gpsimd.memset(dst_i[96:NG, :], NP).then_inc(sem("edge_pads"), 1)
            nc.gpsimd.memset(x[96:P, T - 1, :], 0.0).then_inc(sem("x_pad"), 1)
            g.wait_ge(sem("x_pad"), 1)
            nc.gpsimd.memset(a_blk, 0.0).then_inc(sem("a_zeroed"), 1)
            nc.gpsimd.memset(ones[:, :], 1.0).then_inc(sem("pc"), 1)
            nc.gpsimd.memset(ident[:, :], 0.0).then_inc(sem("pc"), 1)
            g.wait_ge(sem("pc"), 2)
            nc.gpsimd.affine_select(out=tri[:, :], in_=ones[:, :], compare_op=ALU.is_gt, fill=0.0,
                                    base=0, pattern=[[1, P]], channel_multiplier=-1)
            nc.gpsimd.affine_select(out=ident[:, :], in_=ident[:, :], compare_op=ALU.not_equal, fill=1.0,
                                    base=0, pattern=[[-1, P]], channel_multiplier=1).then_inc(sem("pc"), 1)
            kw = dict(allow_small_or_imprecise_dtypes=True, channel_multiplier=0)
            nc.gpsimd.iota(iotaK, [[1, NPAIR]], base=0, **kw)
            nc.gpsimd.iota(iotaL, [[1, P], [0, LC]], base=0, **kw).then_inc(sem("consts"), 1)
            nc.gpsimd.iota(iotaR, [[1, RW], [0, HC]], base=1, **kw).then_inc(sem("iotaR_set"), 1)
            nc.gpsimd.memset(C.bitcast(F32), 0.0).then_inc(sem("C_zeroed"), 1)
            nc.gpsimd.memset(zero[:, 0, :], 0.0).then_inc(sem("zero_set"), 1)
            nc.gpsimd.memset(zero16[:, :], 0.0)
            nc.gpsimd.iota(iota8[:, :], [[1, E1]], base=-99, **kw)
            nc.gpsimd.iota(iota16[:, :], [[1, E0]], base=-99, **kw)
            nc.gpsimd.iota(iotaM[:, :], [[P, NO]], base=S1, **kw)
            nc.gpsimd.iota(iotaJ[:, :], [[1, NO]], base=0, **kw)
            nc.gpsimd.affine_select(out=valid[:, :], in_=ones[:, 0:1], compare_op=ALU.is_gt, fill=0.0,
                                    base=LAST, pattern=[[0, 1]], channel_multiplier=-1)
            nc.gpsimd.iota(row[:, :, D + 2:D + 3].rearrange("p t a -> p (t a)"), [[P, T]], base=-FAR,
                           allow_small_or_imprecise_dtypes=True, channel_multiplier=1)
            nc.gpsimd.memset(Wx[:, :, :, F:FE], 1.0)
            g.wait_ge(sem("pc"), 3)
            nc.gpsimd.tensor_copy(ident16[:, :], ident[:, :]).then_inc(sem("pool_ready"), 1)

            g.wait_ge(sem("C_zeroed"), 1)

            def add_batch(base, off):
                for k in range(LB):
                    w = g.value_load(wk[0:1, bass.ds(off + k, 1)], min_val=0, max_val=NW - 1)
                    g.wait_ge(sem("staged"), base + (k + 1))
                    at_least(g, "added", base + k)
                    if not isinstance(base, int):
                        g.sem_inc(sem("pool_step"), 1)
                    dst = C[:, :, bass.ds(w * WN, WN)]
                    nc.gpsimd.tensor_tensor(dst, dst, stage[:, k % RS, :, :], ALU.add).then_inc(sem("added"), 1)

            g.wait_ge(sem("tables"), 1)
            for b in range(NB):
                if b == B_CS:
                    g.wait_ge(sem("asmax"), 1)
                    nc.gpsimd.partition_all_reduce(cs, asmax, P, bass.bass_isa.ReduceOp.max).then_inc(sem("cs_ready"), 1)
                add_batch(b * LB, b * LB)
            n = g.value_load(npass[0:1, 0:1], min_val=1, max_val=MAXPASS)
            with g.If(n > 1):
                with g.Fori(1, n) as p:
                    g.wait_ge(sem("tables"), p + 1)
                    g.sem_inc(sem("pool_step"), 1)
                    with g.Fori(0, NB) as i:
                        add_batch(p * NPAIR + i * LB, i * LB)
            g.wait_ge(sem("added"), n * NPAIR)
            g.sem_inc(sem("hist_done"), 1)

            g.wait_ge(sem("exps"), 1)
            g.wait_ge(sem("evacA"), T)

            def value(i):
                h, b = divmod(i, 2)
                if i >= 2:
                    g.wait_ge(sem("v_lo"), i - 1)
                nc.gpsimd.tensor_tensor(vtmp[:, i % 2, :, :], Wx[:, :, h, :],
                                        bc((B1, B2)[b][:, :, h], [P, T, FE]), ALU.mult).then_inc(sem("v_made"), 1)

            def low(i):
                h, b = divmod(i, 2)
                g.wait_ge(sem("v_hi"), i + 1)
                nc.gpsimd.tensor_tensor(VP[:, :, 1, h, b, :], vtmp[:, i % 2, :, :], VP[:, :, 0, h, b, :],
                                        ALU.subtract).then_inc(sem("v_lo"), 1)

            def numer(h):
                g.wait_ge(sem("raw_made"), 4 * (h + 1))
                r = raw[h % 2]
                nc.gpsimd.tensor_tensor(r[:, :, 0, :], r[:, :, 0, :], bc(A1[:, :, h], [P, T, FE]), ALU.mult).then_inc(sem("pn"), 1)
                nc.gpsimd.tensor_tensor(r[:, :, 1, :], r[:, :, 1, :], bc(A2[:, :, h], [P, T, FE]), ALU.mult).then_inc(sem("pn"), 1)
                g.wait_ge(sem("pn"), 2 * (h + 1))
                nc.gpsimd.tensor_tensor(nacc[:, :, h, :], r[:, :, 0, :], r[:, :, 1, :], ALU.subtract).then_inc(sem("nacc_made"), 1)

            g.wait_ge(sem("thr_out"), 16)
            g.wait_ge(sem("xp_zeroed"), 16)
            for h in range(H + 1):
                if h < H:
                    for f in (value, low):
                        f(2 * h)
                        f(2 * h + 1)
                if h >= 2:
                    numer(h - 2)
            numer(H - 1)

            g.wait_ge(sem("U_done"), T)
            g.wait_ge(sem("deg_made"), T)
            for s in range(T):
                d = C[:, s, s * P:(s + 1) * P]
                last = nc.gpsimd.tensor_tensor(d, d, ident16[:, :], ALU.add)
            last.then_inc(sem("loops"), 1)
            for t in range(T):
                g.wait_ge(sem("h_hi"), t + 1)
                nc.gpsimd.tensor_tensor(hp[:, t, 1, :], hs[:, t % 2, :], hp[:, t, 0, :], ALU.subtract).then_inc(sem("h_lo"), 1)

            def split_w2(e):
                g.wait_ge(sem("w_hi1"), e + 1)
                w = W16[e % 2][1]
                nc.gpsimd.tensor_tensor(w[:, 1, :, :], W32[e % RW32][:, 1, :, :], w[:, 0, :, :],
                                        ALU.subtract).then_inc(sem("w_lo1"), 1)

            def put(e):
                g.wait_ge(sem("res_made"), 2 * (e + 1))
                r = e % RX
                for j, m in enumerate((P, S1 - P)):
                    nc.gpsimd.indirect_dma_start(out_d, bass.IndirectOffsetOnAxis(ap=ids[0:m, r, j:j + 1], axis=0),
                                                 xs[0:m, r, j, 0:D], None, bounds_check=NODES - 1,
                                                 oob_is_err=False).then_inc(sem(f"put{r}"), 16)

            split_w2(0)

            def scatter(t):
                m = P if t < T - 1 else LAST
                g.wait_ge(sem("pos_ready"), t + 1)
                nc.gpsimd.indirect_dma_start(xp_d, bass.IndirectOffsetOnAxis(ap=pos[0:m, t:t + 1], axis=0),
                                             row[0:m, t, :], None, bounds_check=SPILL - 1,
                                             oob_is_err=False).then_inc(sem("scattered"), 16)

            g.wait_ge(sem("xp_zeroed"), 16)
            for t in range(T + 3):
                if t < T:
                    g.wait_ge(sem("relu_made"), t + 1)
                    nc.gpsimd.tensor_tensor(x[:, t, :], x[:, t, :], rtmp[:, t % 2, :], ALU.add).then_inc(sem("x4_made"), 1)
                if t >= 3:
                    scatter(t - 3)
            split_w2(1)
            for e in range(E1):
                put(e)
                if e + 2 < E1:
                    split_w2(e + 2)
            n = g.value_load(nspill[0:1, 0:1], min_val=0, max_val=NO)
            with g.If(n > 0):
                g.wait_ge(sem("o_pos"), 1)
                for t in range(T):
                    m = P if t < T - 1 else LAST
                    nc.gpsimd.indirect_dma_start(xp_d, bass.IndirectOffsetOnAxis(ap=pos[0:m, t:t + 1], axis=0),
                                                 row[0:m, t, :], None, bounds_check=SPILL + NO * P - 1,
                                                 oob_is_err=False).then_inc(sem("o_scattered"), 16)
                with g.Fori(0, n) as i:
                    g.wait_ge(sem("o_res"), i + 1)
                    g.sem_inc(sem("pool_step"), 1)
                    nc.gpsimd.indirect_dma_start(out_d, bass.IndirectOffsetOnAxis(ap=ids[:, 0, 0:1], axis=0),
                                                 xs[:, 0, 0, 0:D], None, bounds_check=NODES - 1,
                                                 oob_is_err=False).then_inc(sem("o_put"), 16)
                    g.wait_ge(sem("o_put"), 16 * i + 16)
                    g.sem_inc(sem("o_done"), 1)

        @block.scalar
        def _(a):
            act = nc.scalar.activation

            def ln_sqrt(n):
                a.wait_ge(sem("ln_var"), n + 1)
                act(sd[:, n % 2:n % 2 + 1], ve[:, n % 2:n % 2 + 1], ACT.Sqrt).then_inc(sem("ln_sd"), 1)

            def ln_copy(n, b, dst):
                a.wait_ge(sem("xt_psum"), n + 1)
                act(dst, b[:, :].rearrange("p (k m) -> p k m", k=K), ACT.Copy).then_inc(sem("xT_ready"), 1)

            def stage_batch(base):
                for k in range(LB):
                    a.wait_ge(sem("counted"), base + (k + 1))
                    at_least(a, "added", base + (k + 1 - RS))
                    act(stage[:, k % RS, :, :], bank[k % 2][:, 0:RW].rearrange("p (d s) -> p s d", s=T),
                        ACT.Copy).then_inc(sem("staged"), 1)

            def score_weights(b):
                if b == 0:
                    a.wait_ge(sem("a_psum"), 1)
                    a.wait_ge(sem("a_zeroed"), 1)
                    flat_a = a_blk.rearrange("p b c -> p (b c)")
                    for c in range(2):
                        for h in range(2):
                            r = slice(h * F, (h + 1) * F)
                            act(flat_a[r, c * H + h::2 * H + 2], bank[5][r, 256 + c * K:256 + (c + 1) * K], ACT.Copy)
                    act(WbT, bank[5][:, 256 + 2 * K:256 + 3 * K], ACT.Copy).then_inc(sem("a_spread"), 1)
                if b < 2:
                    for k in (2 * b, 2 * b + 1):
                        a.wait_ge(sem("w0T_psum"), k + 1)
                        if k >= 2:
                            a.wait_ge(sem("w0T_used"), k - 1)
                        act(W0T[:, k % 2, :], bank[6 + k % 2][:, :], ACT.Copy).then_inc(sem("w0T_ready"), 1)
                else:
                    a.wait_ge(sem("wa_psum"), 1)
                    act(Wa.rearrange("p k c -> p (k c)"), bank[5][:, 0:K * 2 * H], ACT.Copy)
                    act(cb, bank[5][:, K * 2 * H:(K + 1) * 2 * H], ACT.Copy).then_inc(sem("wa_ready"), 1)

            for b in range(NB):
                if b in BEGIN:
                    ln_sqrt(BEGIN[b])
                stage_batch(b * LB)
                if b < 3:
                    score_weights(b)
                if b - 1 in BEGIN:
                    t = BEGIN[b - 1]
                    if t >= 2:
                        a.wait_ge(sem("linA"), t - 1)
                    ln_copy(t, bank[6 + t % 2], xT_ring[:, t % 2, :, :])
                if b == B_GW:
                    for k in range(K):
                        a.wait_ge(sem("gwT_psum"), k + 1)
                        act(gWT[:, k, :], bank[6 + k % 2][:, :], ACT.Copy).then_inc(sem("gwT_ready"), 1)
                if b == B_CS:
                    for i, n in enumerate((4, 4, 2)):
                        a.wait_ge(sem("thrT_psum"), i + 1)
                        act(thrT[0:H, i * 512:i * 512 + n * P], bank[5 + i][0:H, 0:n * P], ACT.Copy).then_inc(sem("thrT_ready"), 1)
            a.wait_ge(sem("exp_in"), 1)
            act(B1, d1t, ACT.Exp)
            act(B2, d1t, ACT.Exp, scale=SLOPE)
            act(A1, e1t, ACT.Exp)
            act(A2, e2t, ACT.Exp).then_inc(sem("exps"), 1)
            n = a.value_load(npass[0:1, 0:1], min_val=1, max_val=MAXPASS)
            with a.If(n > 1):
                with a.Fori(1, n) as p:
                    with a.Fori(0, NB) as i:
                        stage_batch(p * NPAIR + i * LB)

            def hi(i):
                h, b = divmod(i, 2)
                a.wait_ge(sem("v_made"), i + 1)
                act(VP[:, :, 0, h, b, :], vtmp[:, i % 2, :, :], ACT.Copy).then_inc(sem("v_hi"), 1)

            def raw_copy(h):
                if h >= 2:
                    a.wait_ge(sem("nacc_made"), h - 1)
                for b in range(4):
                    n3 = min(3, T - 3 * b)
                    a.wait_ge(sem("acc_done"), h + 1)
                    act(raw[h % 2][:, 3 * b:3 * b + n3, :, :],
                        bank[4 * (h % 2) + b][:, 0:n3 * 2 * FE].rearrange("p (t b f) -> p t b f", b=2, f=FE),
                        ACT.Copy).then_inc(sem("raw_made"), 1)

            def mask(h, m):
                i = h * len(BY_ACT) + m
                if i >= 2:
                    h2, m2 = divmod(i - 2, len(BY_ACT))
                    a.wait_ge(sem("cz_made"), h2 * T + BY_ACT[m2] + 1)
                s = BY_ACT[m]
                act(zmask[i % 2], thr_bc[:, h % 2, :], ACT.Sigmoid, bias=steep[:, s, h:h + 1], scale=-STEEP).then_inc(sem("z_made"), 1)

            a.wait_ge(sem("hist_done"), 1)
            hi(0)
            hi(1)
            for h in range(H):
                a.wait_ge(sem(f"thr_ld{h % 2}"), 16 * (h // 2 + 1))
                for m in range(len(BY_ACT)):
                    mask(h, m)
                    if m == 1 and h + 1 < H:
                        hi(2 * h + 2)
                        hi(2 * h + 3)
                    if m == 3 and h:
                        raw_copy(h - 1)
            raw_copy(H - 1)

            def degree(s):
                if s:
                    a.wait_ge(sem("deg_made"), s)
                act(junk, C[:, s, :], ACT.Copy, accum_out=deg[:, s:s + 1]).then_inc(sem("deg_made"), 1)

            for s in range(T - 1):
                degree(s) if s < 4 else None
            for t in range(T):
                ln_sqrt(T + t)
                if 4 + t < T:
                    degree(4 + t)
                ln_copy(T + t, bank[4 + t % 2], x2T[:, t, :, :])
            a.wait_ge(sem("dis_in"), 1)
            act(dis[:, :], deg[:, :], ACT.Sqrt).then_inc(sem("dis_sqrt"), 1)
            a.wait_ge(sem("gate_in"), 1)
            act(gt[0:1, 1, :], gt[0:1, 0, :], ACT.Exp, bias=gs[0:1, 0:1], accum_out=gs[0:1, 1:2]).then_inc(sem("gate_exp"), 1)
            for t in range(T + 1):
                if t < T:
                    ln_sqrt(2 * T + t)
                    if t >= 2:
                        a.wait_ge(sem("linC"), t - 1)
                    ln_copy(2 * T + t, bank[t % 2], xT_ring[:, t % 2, :, :])
                if t >= 1:
                    a.wait_ge(sem("hs_made"), t)
                    act(hp[:, t - 1, 0, :], hs[:, (t - 1) % 2, :], ACT.Copy).then_inc(sem("h_hi"), 1)
            def w_hi(e, l):
                a.wait_ge(sem(f"ld_w32_{e % RW32}"), 32 * (e // RW32 + 1))
                if e >= 2:
                    a.wait_ge(sem(("m1_done", "m2_done")[l]), 2 * (e - 1))
                w = W32[e % RW32][:, l, :, :]
                if l:
                    act(w, w, ACT.Copy, scale=WS).then_inc(sem("w_scaled"), 1)
                    a.wait_ge(sem("w_scaled"), e + 1)
                act(W16[e % 2][l][:, 0, :, :], w, ACT.Copy, scale=1.0 if l else WS).then_inc(sem(f"w_hi{l}"), 1)

            w_hi(0, 1)
            w_hi(0, 0)
            for t in range(T + 1):
                if t < T:
                    a.wait_ge(sem("agg_done"), t + 1)
                    if t >= 2:
                        a.wait_ge(sem("x4_made"), t - 1)
                    act(rtmp[:, t % 2, :], bank[6 + t % 2][:, :], ACT.Relu, scale=dis[:, t:t + 1]).then_inc(sem("relu_made"), 1)
                    ln_sqrt(3 * T + t)
                if t >= 1:
                    if t >= 3:
                        a.wait_ge(sem("linD"), t - 2)
                    ln_copy(3 * T + t - 1, bank[(t - 1) % 2], xT_ring[:, (t - 1) % 2, :, :])
            a.wait_ge(sem("agg_done"), T)
            w_hi(1, 1)
            w_hi(1, 0)
            a.wait_ge(sem("b1_psum"), 1)
            act(b1T[:, :, :].rearrange("p e k -> p (e k)"), bank[7][:, 0:E1 * K], ACT.Copy).then_inc(sem("b1_made"), 1)
            a.wait_ge(sem("b1_made"), 1)

            def gates(e):
                r = e % RX
                a.wait_ge(sem(f"ld_xs{r}"), 16 * (e // RX + 1))
                for j in range(2):
                    lg_x = xs[:, r, j, D + 3:ROW]
                    act(lg_x, lg_x, ACT.Exp, accum_out=gsum[:, r, j:j + 1]).then_inc(sem("gates_summed"), 1)

            def x_hi(e):
                if e >= 2:
                    a.wait_ge(sem("m1_done"), 2 * (e - 1))
                for q in range(2):
                    a.wait_ge(sem("xs_psum"), 2 * e + q + 1)
                    act(xT16[:, e % 2, 0, 2 * q:2 * q + 2, :], bank[q][:, 0:2 * S1].rearrange("p (k m) -> p k m", k=2),
                        ACT.Copy).then_inc(sem("x_hi"), 1)

            def hidden(e):
                for q in range(2):
                    i = 2 * e + q
                    a.wait_ge(sem("m1_done"), i + 1)
                    if i >= 2:
                        a.wait_ge(sem("h_lo16"), i - 1)
                    for b in range(2):
                        f = 2 * q + b
                        act(h32[:, q, b, :], bank[2 + q][:, b * S1:(b + 1) * S1], ACT.Relu,
                            bias=b1T[:, e, f:f + 1], scale=1.0 / WS).then_inc(sem("h32_made"), 1)

            x_hi(0)
            gates(0)
            hidden(0)
            x_hi(1)
            w_hi(2, 0)
            gates(1)
            for e in range(E1):
                if e + 1 < E1:
                    hidden(e + 1)
                if e + 3 < E1:
                    w_hi(e + 3, 0)
                if e + 2 < E1:
                    x_hi(e + 2)
                    w_hi(e + 2, 1)
                    gates(e + 2)
            n = a.value_load(nspill[0:1, 0:1], min_val=0, max_val=NO)
            with a.If(n > 0):
                with a.Fori(0, n) as i:
                    a.wait_ge(sem("o_ld"), 64 * i + 64)
                    a.sem_inc(sem("act_step"), 1)
                    act(xs[:, 0, 0, D + 3:ROW], xs[:, 0, 0, D + 3:ROW], ACT.Exp, accum_out=gsum[:, 0, 0:1]).then_inc(sem("o_summed"), 1)
                    a.wait_ge(sem("o_xT_psum"), i + 1)
                    a.sem_inc(sem("act_step"), 1)
                    act(xT_ring[:, 0, :, :], bank[0][:, :].rearrange("p (k m) -> p k m", k=K), ACT.Copy).then_inc(sem("o_xT"), 1)
                    a.wait_ge(sem("o_m1"), i + 1)
                    a.sem_inc(sem("act_step"), 1)
                    for f in range(K):
                        act(xT_ring[:, 1, f, :], bank[2][:, f * P:(f + 1) * P], ACT.Relu, bias=b1o[:, f:f + 1]).then_inc(sem("o_hT"), 1)

        @block.vector
        def _(v):
            V = nc.vector
            count = [0]

            def link(ins):
                count[0] += 1
                ins.then_inc(sem("dve"), 1)
                v.wait_ge(sem("dve"), count[0])

            def ln_stats(n, xt, keep=None):
                i = n % 2
                m = mv[:, i, :] if keep is None else keep
                link(V.bn_stats(st[:, i, :], xt))
                link(V.bn_aggr(m, st[:, i, :]))
                V.tensor_scalar(ve[:, i:i + 1], m[:, 1:2], EPS, None, ALU.add).then_inc(sem("ln_var"), 1)

            def ln_norm(n, xt, dst, keep=None):
                i = n % 2
                m, r = (mv[:, i, 0:1], rs[:, i:i + 1]) if keep is None else (keep[:, 0:1], keep[:, 1:2])
                v.wait_ge(sem("ln_sd"), n + 1)
                link(V.reciprocal(r, sd[:, i:i + 1]))
                if n >= 2:
                    v.wait_ge(sem("xt_psum"), n - 1)
                V.tensor_scalar(dst, xt, m, r, ALU.subtract, ALU.mult).then_inc(sem("xh_made"), 1)

            v.wait_ge(sem("ld_edges"), 64)
            gp = slice(0, NG)
            V.tensor_scalar(lo_i[gp, :], src_i[gp, :], P - 1, None, ALU.bitwise_and)
            V.tensor_scalar(hi_i[gp, :], src_i[gp, :], 7, None, ALU.logical_shift_right)
            V.tensor_scalar(w_i[gp, :], dst_i[gp, :], 5, None, ALU.logical_shift_right)
            link(V.tensor_scalar(q_f[gp, :], dst_i[gp, :], float(T), 1.0, ALU.mult, ALU.add))
            V.tensor_copy(lo_f[gp, :], lo_i[gp, :])
            V.tensor_tensor(q_f[gp, :], q_f[gp, :], hi_i[gp, :], ALU.add)
            V.tensor_reduce(grp[gp, 0:1], w_i[gp, :], AX.X, ALU.min)
            link(V.tensor_reduce(grp[gp, 1:2], w_i[gp, :], AX.X, ALU.max))
            link(V.tensor_scalar(grp[gp, 2:3], grp[gp, 1:2], float(NW - 1), 1.0, ALU.min, ALU.add))
            V.tensor_tensor(grp[gp, 2:3], grp[gp, 2:3], grp[gp, 0:1], ALU.subtract).then_inc(sem("n_ready"), 1)

            def evac_a(t):
                v.wait_ge(sem("linA"), t + 1)
                V.tensor_tensor(Wx[:, t, :, 0:F], bank[2 + t % 2][:, :].rearrange("p (h f) -> p h f", h=H), Wb_bc, ALU.add)
                V.tensor_tensor(sc[:, t, :], bank[4 + t % 2][:, 0:2 * H], cb, ALU.add).then_inc(sem("evacA"), 1)

            def scores():
                v.wait_ge(sem("evacA"), T)
                link(V.tensor_tensor(atb, sc[:, :, 0:H], ab_bc.unsqueeze(1).to_broadcast([P, T, H]), ALU.add))
                V.tensor_scalar(thr, atb, -1.0, None, ALU.mult).then_inc(sem("thr_made"), 1)
                V.tensor_scalar(steep, sc[:, :, H:2 * H], STEEP, None, ALU.mult)
                V.tensor_reduce(asmax, sc[:, :, H:2 * H].rearrange("p t h -> p h t"), AX.X, ALU.max).then_inc(sem("asmax"), 1)

            def exponents():
                v.wait_ge(sem("cs_ready"), 1)
                csb = cs.unsqueeze(1).to_broadcast([P, T, H])
                V.tensor_tensor(d1t, sc[:, :, H:2 * H], csb, ALU.subtract)
                link(V.tensor_tensor(zz, atb, csb, ALU.add))
                link(V.scalar_tensor_tensor(ll, zz, SLOPE, zz, ALU.mult, ALU.max))
                V.tensor_tensor(e1t, zz, ll, ALU.subtract)
                V.scalar_tensor_tensor(e2t, zz, SLOPE, ll, ALU.mult, ALU.subtract).then_inc(sem("exp_in"), 1)

            v.wait_ge(sem("rb_psum"), 1)
            v.wait_ge(sem("consts"), 1)
            V.tensor_copy(grp[gp, 3:4], bank[5][gp, 0:1])
            link(V.tensor_scalar(kt[0:1, :], iotaK[0:1, 0:MAXPASS], float(NPAIR), None, ALU.mult))
            link(V.tensor_scalar(kt[0:1, :], kt[0:1, :], bank[4][0:1, 32:33], None, ALU.is_lt))
            link(V.tensor_reduce(grp[0:1, 6:7], kt[0:1, :], AX.X, ALU.add))
            V.tensor_copy(npass[0:1, :], grp[0:1, 6:7]).then_inc(sem("npass_ready"), 1)

            def pair_tables(p):
                V.tensor_tensor(grp[gp, 4:5], grp[gp, 3:4], grp[gp, 2:3], ALU.add)
                V.tensor_tensor(grp[gp, 5:6], grp[gp, 0:1], grp[gp, 3:4], ALU.subtract).then_inc(sem("g1"), 1)
                v.wait_ge(sem("g1"), p + 1)
                V.tensor_scalar(grp[gp, 5:6], grp[gp, 5:6], -float(RW), None, ALU.mult)
                V.tensor_scalar(from_[gp, :], iotaK[gp, :], grp[gp, 3:4], None, ALU.is_ge).then_inc(sem("g2"), 1)
                v.wait_ge(sem("g2"), p + 1)
                V.scalar_tensor_tensor(inside[gp, :], iotaK[gp, :], grp[gp, 4:5], from_[gp, :], ALU.is_lt, ALU.mult)
                V.tensor_scalar(tv[gp, :], iotaK[gp, :], -float(RW), grp[gp, 5:6], ALU.mult, ALU.add).then_inc(sem("g3"), 1)
                v.wait_ge(sem("g3"), p + 1)
                V.tensor_scalar(grp[gp, 3:4], grp[gp, 3:4], -float(NPAIR), None, ALU.add)
                V.tensor_tensor(wneg[gp, :], tv[gp, :], inside[gp, :], ALU.mult).then_inc(sem("picks"), 1)
                v.wait_ge(sem("table_psum"), p + 1)
                V.tensor_scalar(wk[0:1, :], bank[4][0:1, 0:NPAIR], -1.0 / RW, 0.25, ALU.mult, ALU.add)
                V.tensor_copy(loT.rearrange("p (k j) -> p k j", j=CH), bank[2][:, 0:NPAIR * CH].rearrange("p (j k) -> p k j", j=CH))
                V.tensor_scalar(qT.rearrange("p (k j) -> p k j", j=CH),
                                bank[3][:, 0:NPAIR * CH].rearrange("p (j k) -> p k j", j=CH),
                                0.0, RW + 1.0, ALU.max, ALU.min).then_inc(sem("tables"), 1)
                v.wait_ge(sem("tables"), p + 1)

            def onehots(base, off, slot):
                at_least(v, "counted", base - LB)
                lo = loT[:, bass.ds(off * CH, LC)].unsqueeze(1).to_broadcast([P, P, LC])
                V.tensor_tensor(L_ring[:, slot, :, :], iotaL, lo, ALU.is_equal)
                for b in range(2):
                    at_least(v, "counted", base + (b - 1) * HB)
                    q = qT[:, bass.ds(off * CH + b * HC, HC)].unsqueeze(1).to_broadcast([P, RW, HC])
                    V.tensor_tensor(R_ring[:, b, :, :], iotaR, q, ALU.is_equal).then_inc(sem("onehots"), HB)

            pair_tables(0)
            v.wait_ge(sem("iotaR_set"), 1)
            for b in range(NB):
                if b == 1:
                    v.wait_ge(sem("ld_x"), 32)
                if b in BEGIN:
                    ln_stats(BEGIN[b], x[:, BEGIN[b], :])
                onehots(b * LB, b * LB, b % 2)
                if b - 1 in BEGIN:
                    t = BEGIN[b - 1]
                    ln_norm(t, x[:, t, :], xh_ring[:, t % 2, :])
                if b - 3 in BEGIN:
                    evac_a(BEGIN[b - 3])
                    if BEGIN[b - 3] == T - 1:
                        scores()
            exponents()
            v.wait_ge(sem("npass_ready"), 1)
            n = v.value_load(npass[0:1, 0:1], min_val=1, max_val=MAXPASS)
            with v.If(n > 1):
                with v.Fori(1, n) as p:
                    v.wait_ge(sem("added"), p * NPAIR)
                    pair_tables(p)
                    v.sem_inc(sem("dve_step"), 1)
                    with v.Fori(0, NB // 2) as i:
                        for b in range(2):
                            onehots(p * NPAIR + i * 2 * LB + b * LB, i * 2 * LB + b * LB, b)

            v.wait_ge(sem("hist_done"), 1)
            for h in range(H):
                v.wait_ge(sem(f"thr_ld{h % 2}"), 16 * (h // 2 + 1))
                for s in range(T):
                    i = h * T + s
                    if i >= RZ:
                        v.wait_ge(sem("cz_used"), i - RZ + 1)
                    if s in BY_ACT:
                        m = h * len(BY_ACT) + BY_ACT.index(s)
                        v.wait_ge(sem("z_made"), m + 1)
                        V.tensor_tensor(cz[:, i % RZ, :], zmask[m % 2], C[:, s, :], ALU.mult).then_inc(sem("cz_made"), 1)
                    else:
                        V.scalar_tensor_tensor(cz[:, i % RZ, :], thr_bc[:, h % 2, :], sc[:, s, H + h:H + h + 1],
                                               C[:, s, :], ALU.is_le, ALU.mult).then_inc(sem("cz_made"), 1)
            v.wait_ge(sem("nacc_made"), H)

            def token_sum(t):
                v.wait_ge(sem("xT_ready"), T + t + 1)
                V.tensor_reduce(msum[:, t, :], x2T[:, t, :, :], AX.X, ALU.add)

            for t in range(T):
                v.wait_ge(sem("U_done"), t + 1)
                for g2 in range(2):
                    hh = slice(4 * g2, 4 * g2 + 4)
                    ins = V.tensor_tensor(num[:, hh, :], bank[2 * (t % 2) + g2][:, 0:4 * FE].rearrange("p (h f) -> p h f", f=FE),
                                          bc(A2[:, t, hh], [P, 4, FE]), ALU.mult)
                ins.then_inc(sem("U_used"), 1)
                v.wait_ge(sem("U_used"), t + 1)
                link(V.tensor_tensor(num[:, :, :], num[:, :, :], nacc[:, t, :, :], ALU.add))
                link(V.tensor_scalar(rden[:, :], num[:, :, F], 1e-30, None, ALU.max))
                link(V.reciprocal(rden[:, :], rden[:, :]))
                link(V.tensor_tensor(num[:, :, 0:F], num[:, :, 0:F], bc(rden, [P, H, F]), ALU.mult))
                xt = x[:, t, :]
                V.tensor_tensor(xt.rearrange("p (h f) -> p h f", f=F), xt.rearrange("p (h f) -> p h f", f=F),
                                num[:, :, 0:F], ALU.add).then_inc(sem("x2_made"), 1)
                v.wait_ge(sem("x2_made"), t + 1)
                ln_stats(T + t, xt)
                ln_norm(T + t, xt, xh_ring[:, t % 2, :])
                if t >= 2:
                    token_sum(t - 2)
            token_sum(T - 2)
            token_sum(T - 1)
            v.wait_ge(sem("deg_made"), T)
            V.tensor_scalar(deg[:, :], deg[:, :], 1.0, None, ALU.add).then_inc(sem("dis_in"), 1)
            v.wait_ge(sem("dis_in"), 1)
            link(V.tensor_reduce(mean, msum.rearrange("p t k -> p k t"), AX.X, ALU.add))
            V.tensor_scalar(mean, mean, 1.0 / NODES, None, ALU.mult).then_inc(sem("mean_ready"), 1)
            v.wait_ge(sem("dis_sqrt"), 1)
            link(V.reciprocal(dis[:, :], dis[:, :]))
            v.wait_ge(sem("gate_psum"), 1)
            v.wait_ge(sem("ld_w1"), 96)
            link(V.tensor_tensor(gt[0:1, 0, :], bank[2][0:1, 0:E0], bg[:, :], ALU.add))
            V.tensor_reduce(gs[0:1, 0:1], gt[0:1, 0, :], AX.X, ALU.max, negate=True).then_inc(sem("gate_in"), 1)
            v.wait_ge(sem("gate_exp"), 1)
            link(V.tensor_reduce(gs[0:1, 2:3], gt[0:1, 1, :], AX.X, ALU.max))
            link(V.tensor_scalar(gt[0:1, 2, :], gt[0:1, 1, :], gs[0:1, 2:3], None, ALU.is_ge))
            link(V.tensor_tensor(gt[0:1, 2, :], gt[0:1, 2, :], iota16[0:1, :], ALU.mult))
            link(V.tensor_reduce(gs[0:1, 3:4], gt[0:1, 2, :], AX.X, ALU.min))
            V.tensor_scalar(gidx[0:1, :], gs[0:1, 3:4], 99.0, None, ALU.add).then_inc(sem("gate_idx"), 1)
            V.reciprocal(gs[0:1, 4:5], gs[0:1, 1:2]).then_inc(sem("gate_made"), 1)
            v.wait_ge(sem("gate_bc"), 1)
            link(V.tensor_copy(gs[:, 5:6], bank[7][:, 0:1]))
            v.wait_ge(sem("ld_we"), 32)

            def x3(t):
                v.wait_ge(sem("ff_done"), t + 1)
                tmp = num[:, :, :].rearrange("p h f -> p (h f)")[:, 0:D]
                V.tensor_tensor(tmp, bank[2 + t % 2][:, :], be_bc[:, :], ALU.add).then_inc(sem("ff_used"), 1)
                v.wait_ge(sem("ff_used"), t + 1)
                link(V.scalar_tensor_tensor(x[:, t, :], tmp, gs[:, 5:6], x[:, t, :], ALU.mult, ALU.add))
                ln_stats(2 * T + t, x[:, t, :])
                ln_norm(2 * T + t, x[:, t, :], xh_ring[:, t % 2, :])

            def message(t):
                v.wait_ge(sem("linC"), t + 1)
                if t >= 2:
                    v.wait_ge(sem("h_lo"), t - 1)
                V.tensor_tensor(hs[:, t % 2, :], bank[4 + t % 2][:, :], gb_bc[:, :], ALU.add).then_inc(sem("h_used"), 1)
                v.wait_ge(sem("h_used"), t + 1)
                V.tensor_scalar(hs[:, t % 2, :], hs[:, t % 2, :], dis[:, t:t + 1], None, ALU.mult).then_inc(sem("hs_made"), 1)

            for t in range(T + 1):
                if t < T:
                    x3(t)
                if t >= 1:
                    message(t - 1)

            def split_w1(e):
                v.wait_ge(sem("w_hi0"), e + 1)
                w = W16[e % 2][0]
                V.scalar_tensor_tensor(w[:, 1, :, :], W32[e % RW32][:, 0, :, :], WS, w[:, 0, :, :],
                                       ALU.mult, ALU.subtract).then_inc(sem("w_lo0"), 1)

            split_w1(0)

            def logits(t):
                v.wait_ge(sem("linD"), t + 1)
                V.tensor_tensor(lg[:, t, :], bank[2 + t % 2][:, 0:E1], br_bc[:, :], ALU.add).then_inc(sem("lg_made"), 1)
                v.wait_ge(sem("lg_made"), t + 1)
                link(V.tensor_reduce(mx10[:, t:t + 1], lg[:, t, :], AX.X, ALU.max))
                V.tensor_scalar(row[:, t, D + 3:ROW], lg[:, t, :], mx10[:, t:t + 1], None, ALU.subtract)
                link(V.scalar_tensor_tensor(eq[:, t, :], lg[:, t, :], mx10[:, t:t + 1], iota8[:, :], ALU.is_ge, ALU.mult))
                link(V.tensor_reduce(em[:, t:t + 1], eq[:, t, :], AX.X, ALU.min))
                V.tensor_scalar(first[:, t:t + 1], em[:, t:t + 1], float(S1), 99.0 * S1, ALU.mult, ALU.add)
                if t < T - 1:
                    ins = V.tensor_scalar(oh[:, t, :], iota8[:, :], em[:, t:t + 1], None, ALU.is_equal)
                else:
                    ins = V.tensor_scalar(oh[:, t, :], iota8[:, :], em[:, t:t + 1], valid[:, 0:1], ALU.is_equal, ALU.mult)
                ins.then_inc(sem("oh_made"), 1)
                v.wait_ge(sem("oh_made"), t + 1)
                if t:
                    V.tensor_tensor(osum[:, t, :], osum[:, t - 1, :], oh[:, t, :], ALU.add).then_inc(sem("osum_made"), 1)
                else:
                    V.tensor_copy(osum[:, 0, :], oh[:, 0, :]).then_inc(sem("osum_made"), 1)
                v.wait_ge(sem("osum_made"), t + 1)

            def place(t):
                v.wait_ge(sem("rank_psum"), t + 1)
                link(V.tensor_tensor(eq[:, t, :], bank[4 + t % 2][:, 0:E1], oh[:, t, :], ALU.mult))
                link(V.tensor_reduce(rank[:, t:t + 1], eq[:, t, :], AX.X, ALU.add))
                link(V.tensor_scalar(over[:, t:t + 1], rank[:, t:t + 1], float(S1), float(FAR), ALU.is_ge, ALU.mult))
                V.scalar_tensor_tensor(pos[:, t:t + 1], rank[:, t:t + 1], first[:, t:t + 1], over[:, t:t + 1],
                                       ALU.add, ALU.add).then_inc(sem("pos_ready"), 1)

            for t in range(T + 1):
                if t < T:
                    v.wait_ge(sem("x4_made"), t + 1)
                    ln_stats(3 * T + t, x[:, t, :], row[:, t, D:D + 2])
                    ln_norm(3 * T + t, x[:, t, :], xh_ring[:, t % 2, :], row[:, t, D:D + 2])
                if t >= 1:
                    logits(t - 1)
                if t >= 2:
                    place(t - 2)
            place(T - 1)
            v.wait_ge(sem("total_psum"), 1)
            link(V.tensor_tensor(cmp_, iotaM[:, :].unsqueeze(1).to_broadcast([P, E1, NO]), bc(bank[6][:, 0:E1], [P, E1, NO]), ALU.is_lt))
            link(V.tensor_reduce(tl, cmp_, AX.X, ALU.add))
            link(V.tensor_tensor_scan(cum, ones[:, 0:E1], tl, 0.0, ALU.mult, ALU.add))
            link(V.tensor_tensor(tcmp, bc(iotaJ[:, :], [P, NO, E1 - 1]), cum[:, 0:E1 - 1].unsqueeze(1).to_broadcast([P, NO, E1 - 1]), ALU.is_ge))
            link(V.tensor_reduce(te_f, tcmp, AX.X, ALU.add))
            V.tensor_copy(te, te_f)
            V.tensor_copy(nspill[0:1, :], cum[0:1, E1 - 1:E1]).then_inc(sem("te_ready"), 1)
            split_w1(1)

            def norm_rows(e):
                r = e % RX
                v.wait_ge(sem(f"ld_xs{r}"), 16 * (e // RX + 1))
                if e:
                    v.wait_ge(sem("xs_psum"), 2 * e)
                for j in range(2):
                    ins = V.tensor_scalar(xh_ring[:, j, :], xs[:, r, j, 0:D], xs[:, r, j, D:D + 1], xs[:, r, j, D + 1:D + 2],
                                          ALU.subtract, ALU.mult)
                    ins.then_inc(sem("xs_normed"), 1)
                V.tensor_scalar(ids[:, r, :], xs[:, r, :, D + 2], float(FAR), None, ALU.add).then_inc(sem("ids_made"), 1)

            def x_lo(e):
                for q in range(2):
                    v.wait_ge(sem("x_hi"), 2 * e + q + 1)
                    V.tensor_tensor(xT16[:, e % 2, 1, 2 * q:2 * q + 2, :], bank[q][:, 0:2 * S1].rearrange("p (k m) -> p k m", k=2),
                                    xT16[:, e % 2, 0, 2 * q:2 * q + 2, :], ALU.subtract).then_inc(sem("x_lo"), 1)

            def h_split(e):
                if e >= 2:
                    v.wait_ge(sem("m2_done"), 2 * (e - 1))
                for q in range(2):
                    f = slice(2 * q, 2 * q + 2)
                    v.wait_ge(sem("h32_made"), 4 * e + 2 * q + 2)
                    link(V.tensor_copy(hT16[:, e % 2, 0, f, :], h32[:, q, :, :]))
                    V.tensor_tensor(hT16[:, e % 2, 1, f, :], h32[:, q, :, :], hT16[:, e % 2, 0, f, :], ALU.subtract).then_inc(sem("h_lo16"), 1)

            def add_bias(e):
                r = e % RX
                v.wait_ge(sem("xs_normed"), 2 * (e + 1))
                v.wait_ge(sem(f"ld_b2_{e % 2}"), 16 * (e // 2 + 1))
                v.wait_ge(sem("gates_summed"), 2 * (e + 1))
                link(V.reciprocal(gate[:, r, :], gsum[:, r, :]))
                V.tensor_scalar(gate_ws[:, r, :], gate[:, r, :], 1.0 / WS, None, ALU.mult)
                for j in range(2):
                    ins = V.scalar_tensor_tensor(xs[:, r, j, 0:D], b2_ring[e % 2][:, :], gate[:, r, j:j + 1],
                                                 xs[:, r, j, 0:D], ALU.mult, ALU.add)
                ins.then_inc(sem("b2_used"), 1)

            def result(e):
                r = e % RX
                v.wait_ge(sem("b2_used"), e + 1)
                for j, m in enumerate((P, S1 - P)):
                    v.wait_ge(sem("m2_done"), 2 * e + j + 1)
                    V.scalar_tensor_tensor(xs[0:m, r, j, 0:D], bank[4 + 2 * (e % 2) + j][0:m, :], gate_ws[0:m, r, j:j + 1],
                                           xs[0:m, r, j, 0:D], ALU.mult, ALU.add).then_inc(sem("res_made"), 1)

            norm_rows(0)
            x_lo(0)
            norm_rows(1)
            h_split(0)
            x_lo(1)
            norm_rows(2)
            split_w1(2)
            add_bias(0)
            for e in range(E1):
                if e + 1 < E1:
                    h_split(e + 1)
                if e + 2 < E1:
                    x_lo(e + 2)
                if e + 3 < E1:
                    split_w1(e + 3)
                if e + 1 < E1:
                    add_bias(e + 1)
                result(e)
                if e + 3 < E1:
                    norm_rows(e + 3)
            n = v.value_load(nspill[0:1, 0:1], min_val=0, max_val=NO)
            with v.If(n > 0):
                link(V.tensor_tensor(base, cum, tl, ALU.subtract))
                link(V.tensor_scalar(base, base, float(P), float(SPILL - S1), ALU.mult, ALU.add))
                link(V.tensor_tensor(eq, oh, base.unsqueeze(1).to_broadcast([P, T, E1]), ALU.mult))
                link(V.tensor_reduce(first, eq, AX.X, ALU.add))
                link(V.tensor_scalar(over, rank, float(S1), float(FAR), ALU.is_lt, ALU.mult))
                link(V.tensor_tensor(first, first, over, ALU.add))
                V.tensor_tensor(pos, first, rank, ALU.add).then_inc(sem("o_pos"), 1)
                with v.Fori(0, n) as i:
                    v.wait_ge(sem("o_ld"), 64 * i + 64)
                    v.sem_inc(sem("dve_step"), 1)
                    e = v.value_load(te[0:1, bass.ds(i, 1)], min_val=0, max_val=E1 - 1)
                    V.tensor_copy(b1o, b1T[:, bass.ds(e, 1), :].rearrange("p a k -> p (a k)"))
                    V.tensor_scalar(ids[:, 0, 0:1], xs[:, 0, 0, D + 2:D + 3], float(FAR), None, ALU.add)
                    V.tensor_scalar(xh_ring[:, 0, :], xs[:, 0, 0, 0:D], xs[:, 0, 0, D:D + 1], xs[:, 0, 0, D + 1:D + 2],
                                    ALU.subtract, ALU.mult).then_inc(sem("o_normed"), 1)
                    v.wait_ge(sem("o_normed"), i + 1)
                    v.sem_inc(sem("dve_step"), 1)
                    v.wait_ge(sem("o_summed"), i + 1)
                    v.sem_inc(sem("dve_step"), 1)
                    V.reciprocal(gate[:, 0, 0:1], gsum[:, 0, 0:1]).then_inc(sem("o_gate"), 1)
                    v.wait_ge(sem("o_gate"), i + 1)
                    v.sem_inc(sem("dve_step"), 1)
                    V.scalar_tensor_tensor(xs[:, 0, 0, 0:D], gb_bc[:, :], gate[:, 0, 0:1],
                                           xs[:, 0, 0, 0:D], ALU.mult, ALU.add).then_inc(sem("o_bias"), 1)
                    v.wait_ge(sem("o_bias"), i + 1)
                    v.sem_inc(sem("dve_step"), 1)
                    v.wait_ge(sem("o_m2"), i + 1)
                    v.sem_inc(sem("dve_step"), 1)
                    V.scalar_tensor_tensor(xs[:, 0, 0, 0:D], bank[4][:, :], gate[:, 0, 0:1],
                                           xs[:, 0, 0, 0:D], ALU.mult, ALU.add).then_inc(sem("o_res"), 1)

        @block.tensor
        def _(pe):
            mm = nc.tensor.matmul

            def transposes(src, b, name):
                for k in range(K):
                    ins = nc.tensor.transpose(b[:, k * P:(k + 1) * P], src[:, k * P:(k + 1) * P], ident[:, :])
                ins.then_inc(sem(name), 1)

            def tile_T(n, src, b):
                pe.wait_ge(sem("xh_made"), n + 1)
                if n >= 2:
                    pe.wait_ge(sem("xT_ready"), n - 1)
                transposes(src, b, "xt_psum")

            def linear(lhs, rhs, out, name=None):
                for k in range(K):
                    ins = mm(out, lhs[:, k, :], rhs(k), start=k == 0, stop=k == K - 1)
                if name:
                    ins.then_inc(sem(name), 1)

            pe.wait_ge(sem("pc"), 3)
            pe.wait_ge(sem("n_ready"), 1)
            mm(bank[5][0:NG, 0:1], tri[0:NG, 0:NG], grp[0:NG, 2:3], start=True, stop=True)
            mm(bank[4][0:1, 32:33], ones[0:NG, 0:1], grp[0:NG, 2:3], start=True, stop=True).then_inc(sem("rb_psum"), 1)

            def lin_a(t):
                if t == 0:
                    pe.wait_ge(sem("wa_ready"), 1)
                pe.wait_ge(sem("xT_ready"), t + 1)
                if t >= 2:
                    pe.wait_ge(sem("evacA"), t - 1)
                xT = xT_ring[:, t % 2, :, :]
                linear(xT, lambda k: W0[:, k, :, :].rearrange("p h f -> p (h f)"), bank[2 + t % 2][:, :])
                linear(xT, lambda k: Wa[:, k, :], bank[4 + t % 2][:, 0:2 * H], "linA")

            def second_weights():
                pe.wait_ge(sem("xT_ready"), T)
                pe.wait_ge(sem("ld_gw"), 16)
                for k in range(K):
                    if k >= 2:
                        pe.wait_ge(sem("gwT_ready"), k - 1)
                    for o in range(K):
                        ins = nc.tensor.transpose(bank[6 + k % 2][:, o * P:(o + 1) * P], gW[:, o, k * P:(k + 1) * P], ident[:, :])
                    ins.then_inc(sem("gwT_psum"), 1)

            def thresholds():
                pe.wait_ge(sem("thr_made"), 1)
                pe.wait_ge(sem("gwT_ready"), K)
                for i, n in enumerate((4, 4, 2)):
                    for q in range(n):
                        ins = nc.tensor.transpose(bank[5 + i][0:H, q * P:(q + 1) * P], thr[:, 4 * i + q, :], ident[:, :])
                    ins.then_inc(sem("thrT_psum"), 1)

            def pair_matmuls(p):
                pe.wait_ge(sem("picks"), p + 1)
                for j in range(CH):
                    e = slice(j * P, (j + 1) * P)
                    o = slice(j * NPAIR, (j + 1) * NPAIR)
                    mm(bank[2][:, o], lo_f[0:NG, e], inside[0:NG, :], start=True, stop=True)
                    mm(bank[3][:, o], q_f[0:NG, e], inside[0:NG, :], start=True, stop=False)
                    mm(bank[3][:, o], ones[0:NG, :], wneg[0:NG, :], start=False, stop=True)
                mm(bank[4][0:1, 0:NPAIR], ones[0:NG, 0:1], wneg[0:NG, :], start=True, stop=True).then_inc(sem("table_psum"), 1)

            def count_pair(base, slot, k):
                pe.wait_ge(sem("onehots"), base + (k + 1))
                at_least(pe, "staged", base + (k - 1))
                for j in range(CH):
                    ins = mm(bank[k % 2][:, 0:RW], L_ring[:, slot, :, k * CH + j], R_ring[:, k // HB, :, (k % HB) * CH + j],
                             start=j == 0, stop=j == CH - 1)
                ins.then_inc(sem("counted"), 1)

            def score_weights(b):
                if b == 0:
                    pe.wait_ge(sem("ld_w0"), 16 * (K + 2))
                    pe.wait_ge(sem("ld_a"), 16 * 3)
                    for c in range(3):
                        ins = nc.tensor.transpose(bank[5][:, 256 + c * K:256 + (c + 1) * K], a_nat[0:K, c, :, :].rearrange("b h f -> b (h f)"),
                                                  ident[0:K, 0:K])
                    ins.then_inc(sem("a_psum"), 1)
                else:
                    pe.wait_ge(sem("a_spread"), 1)
                    weights_of(2 * b - 2)
                    weights_of(2 * b - 1)
                if b < 2:
                    for k in (2 * b, 2 * b + 1):
                        transposes(W0[:, k, :, :].rearrange("p h f -> p (h f)"), bank[6 + k % 2], "w0T_psum")
                else:
                    for i in range(K):
                        ins = mm(bank[5][:, K * 2 * H:(K + 1) * 2 * H], WbT[:, i:i + 1].to_broadcast([P, P]), a_blk[:, i, :],
                                 start=i == 0, stop=i == K - 1)
                    ins.then_inc(sem("wa_psum"), 1)

            def weights_of(k):
                pe.wait_ge(sem("w0T_ready"), k + 1)
                for b in range(K):
                    ins = mm(bank[5][:, k * 2 * H:(k + 1) * 2 * H], W0T[:, k % 2, b * P:(b + 1) * P], a_blk[:, b, :],
                             start=b == 0, stop=b == K - 1)
                ins.then_inc(sem("w0T_used"), 1)

            pair_matmuls(0)
            for b in range(NB):
                for k in range(LB):
                    count_pair(b * LB, b % 2, k)
                    if k == HB - 1 and b - 2 in BEGIN:
                        lin_a(BEGIN[b - 2])
                if b < 3:
                    score_weights(b)
                if b - 1 in BEGIN:
                    t = BEGIN[b - 1]
                    tile_T(t, xh_ring[:, t % 2, :], bank[6 + t % 2])
                if b == B_GW:
                    second_weights()
                if b == B_CS:
                    thresholds()
            n = pe.value_load(npass[0:1, 0:1], min_val=1, max_val=MAXPASS)
            with pe.If(n > 1):
                with pe.Fori(1, n) as p:
                    pair_matmuls(p)
                    with pe.Fori(0, NB // 2) as i:
                        for b in range(2):
                            for k in range(LB):
                                count_pair(p * NPAIR + i * 2 * LB + b * LB, b, k)

            pe.wait_ge(sem("hist_done"), 1)
            pe.wait_ge(sem("thrT_ready"), 3)
            for h in range(H):
                if h >= 2:
                    pe.wait_ge(sem("raw_made"), 4 * (h - 1))
                for b in range(4):
                    w = min(3, T - 3 * b) * 2 * FE
                    mm(bank[4 * (h % 2) + b][:, 0:w], zero16[:, 0:P], zero16[:, 0:w], start=True, stop=False)
                pe.wait_ge(sem("v_lo"), 2 * h + 2)
                for s in range(T):
                    i = h * T + s
                    pe.wait_ge(sem("cz_made"), i + 1)
                    for t in range(T):
                        for part in range(2):
                            ins = mm(acc_region(h, t), cz[:, i % RZ, t * P:(t + 1) * P],
                                     VP[:, s, part, h, :, :].rearrange("p b f -> p (b f)"), start=False,
                                     stop=s == T - 1 and part == 1 and (t % 3 == 2 or t == T - 1))
                    ins.then_inc(sem("cz_used"), 1)
                pe.wait_ge(sem("cz_used"), (h + 1) * T)
                pe.sem_inc(sem("acc_done"), 1)
            def all_edges(t):
                if t >= 2:
                    pe.wait_ge(sem("U_used"), t - 1)
                for g2 in range(2):
                    for s in range(T):
                        for part in range(2):
                            ins = mm(bank[2 * (t % 2) + g2][:, 0:4 * FE].rearrange("p (h f) -> p h f", f=FE), C[:, s, t * P:(t + 1) * P],
                                     VP[:, s, part, 4 * g2:4 * g2 + 4, 1, :], start=s == 0 and part == 0,
                                     stop=s == T - 1 and part == 1)
                ins.then_inc(sem("U_done"), 1)

            pe.wait_ge(sem("raw_made"), 4 * (H - 1))
            all_edges(0)
            all_edges(1)
            pe.wait_ge(sem("raw_made"), 4 * H)
            for t in range(T):
                tile_T(T + t, xh_ring[:, t % 2, :], bank[4 + t % 2])
                if t + 2 < T:
                    all_edges(t + 2)
            pe.wait_ge(sem("mean_ready"), 1)
            pe.wait_ge(sem("ld_w1"), 96)
            for k in range(K):
                ins = mm(bank[2][0:1, 0:E0], mean[:, k:k + 1], Wg[:, k, :], start=k == 0, stop=k == K - 1)
            ins.then_inc(sem("gate_psum"), 1)
            pe.wait_ge(sem("gate_made"), 1)
            mm(bank[7][:, 0:1], ones[0:1, :], gs[0:1, 4:5], start=True, stop=True).then_inc(sem("gate_bc"), 1)
            pe.wait_ge(sem("ld_we"), 32)

            def ff(t):
                pe.wait_ge(sem("xT_ready"), T + t + 1)
                if t >= 2:
                    pe.wait_ge(sem("ff_used"), t - 1)
                linear(x2T[:, t, :, :], lambda k: We[:, k, :], bank[2 + t % 2][:, :], "ff_done")

            def lin_c(t):
                pe.wait_ge(sem("xT_ready"), 2 * T + t + 1)
                if t >= 2:
                    pe.wait_ge(sem("h_used"), t - 1)
                linear(xT_ring[:, t % 2, :, :], lambda k: gWT[:, k, :], bank[4 + t % 2][:, :], "linC")

            ff(0)
            ff(1)
            for t in range(T):
                tile_T(2 * T + t, xh_ring[:, t % 2, :], bank[t % 2])
                if t + 2 < T:
                    ff(t + 2)
                lin_c(t)
            pe.wait_ge(sem("loops"), 1)
            pe.wait_ge(sem("h_lo"), T)

            def agg(t):
                if t >= 2:
                    pe.wait_ge(sem("relu_made"), t - 1)
                for s in range(T):
                    for part in range(2):
                        ins = mm(bank[6 + t % 2][:, :], C[:, s, t * P:(t + 1) * P], hp[:, s, part, :],
                                 start=s == 0 and part == 0, stop=s == T - 1 and part == 1)
                ins.then_inc(sem("agg_done"), 1)

            def lin_d(t):
                pe.wait_ge(sem("xT_ready"), 3 * T + t + 1)
                if t >= 2:
                    pe.wait_ge(sem("lg_made"), t - 1)
                linear(xT_ring[:, t % 2, :, :], lambda k: Wr[:, k, :], bank[2 + t % 2][:, 0:E1], "linD")

            def ranks(t):
                pe.wait_ge(sem("oh_made"), t + 1)
                if t >= 2:
                    pe.wait_ge(sem("pos_ready"), t - 1)
                out = bank[4 + t % 2][:, 0:E1]
                ins = mm(out, tri[:, :], oh[:, t, :], start=True, stop=t == 0)
                if t:
                    pe.wait_ge(sem("osum_made"), t)
                    ins = mm(out, ones[:, :], osum[:, t - 1, :], start=False, stop=True)
                ins.then_inc(sem("rank_psum"), 1)

            agg(0)
            agg(1)
            for t in range(T):
                tile_T(3 * T + t, xh_ring[:, t % 2, :], bank[t % 2])
                if t + 2 < T:
                    agg(t + 2)
                lin_d(t)
                if t:
                    ranks(t - 1)
            ranks(T - 1)
            pe.wait_ge(sem("relu_made"), T)
            pe.wait_ge(sem("osum_made"), T)
            mm(bank[6][:, 0:E1], ones[:, :], osum[:, T - 1, :], start=True, stop=True).then_inc(sem("total_psum"), 1)
            nc.tensor.transpose(bank[7][:, 0:E1 * K], b1_nat[:, :], ident[0:E1 * K, 0:E1 * K]).then_inc(sem("b1_psum"), 1)

            def token_T(e):
                pe.wait_ge(sem("xs_normed"), 2 * (e + 1))
                for q in range(2):
                    if e:
                        pe.wait_ge(sem("x_lo"), 2 * (e - 1) + q + 1)
                    for kk in range(2):
                        k = 2 * q + kk
                        for j, m in enumerate((P, S1 - P)):
                            c = kk * S1 + j * P
                            ins = nc.tensor.transpose(bank[q][:, c:c + m], xh_ring[0:m, j, k * P:(k + 1) * P], ident[0:m, 0:m])
                    ins.then_inc(sem("xs_psum"), 1)

            PARTS = ((0, 0), (1, 0), (0, 1))

            def m1(e):
                pe.wait_ge(sem("w_lo0"), e + 1)
                pe.wait_ge(sem("x_lo"), 2 * e + 2)
                for q in range(2):
                    if e:
                        pe.wait_ge(sem("h32_made"), 4 * (e - 1) + 2 * q + 2)
                    for b in range(2):
                        f = slice((2 * q + b) * P, (2 * q + b + 1) * P)
                        for n, (k, (wp, xp)) in enumerate((k, c) for k in range(K) for c in PARTS):
                            ins = mm(bank[2 + q][:, b * S1:(b + 1) * S1], W16[e % 2][0][:, wp, k, f],
                                     xT16[:, e % 2, xp, k, :], start=n == 0, stop=n == 3 * K - 1)
                    ins.then_inc(sem("m1_done"), 1)

            def m2(e):
                pe.wait_ge(sem("w_lo1"), e + 1)
                pe.wait_ge(sem("h_lo16"), 2 * e + 2)
                if e >= 2:
                    pe.wait_ge(sem("res_made"), 2 * (e - 1))
                for j, m in enumerate((P, S1 - P)):
                    for n, (k, (wp, hp_)) in enumerate((k, c) for k in range(K) for c in PARTS):
                        ins = mm(bank[4 + 2 * (e % 2) + j][0:m, :], hT16[:, e % 2, hp_, k, j * P:j * P + m],
                                 W16[e % 2][1][:, wp, k, :], start=n == 0, stop=n == 3 * K - 1)
                    ins.then_inc(sem("m2_done"), 1)

            pe.wait_ge(sem("te_ready"), 1)
            pe.wait_ge(sem("b1_made"), 1)
            token_T(0)
            m1(0)
            token_T(1)
            for e in range(E1):
                if e + 1 < E1:
                    m1(e + 1)
                if e + 2 < E1:
                    token_T(e + 2)
                m2(e)
            pe.wait_ge(sem("res_made"), 2 * E1)
            n = pe.value_load(nspill[0:1, 0:1], min_val=0, max_val=NO)
            with pe.If(n > 0):
                with pe.Fori(0, n) as i:
                    pe.wait_ge(sem("o_normed"), i + 1)
                    pe.sem_inc(sem("pe_step"), 1)
                    for k in range(K):
                        ins = nc.tensor.transpose(bank[0][:, k * P:(k + 1) * P], xh_ring[:, 0, k * P:(k + 1) * P], ident[:, :])
                    ins.then_inc(sem("o_xT_psum"), 1)
                    pe.wait_ge(sem("o_xT"), i + 1)
                    pe.sem_inc(sem("pe_step"), 1)
                    for f in range(K):
                        for k in range(K):
                            ins = mm(bank[2][:, f * P:(f + 1) * P], W32[0][:, 0, k, f * P:(f + 1) * P], xT_ring[:, 0, k, :],
                                     start=k == 0, stop=k == K - 1)
                    ins.then_inc(sem("o_m1"), 1)
                    pe.wait_ge(sem("o_hT"), K * i + K)
                    pe.sem_inc(sem("pe_step"), 1)
                    linear(xT_ring[:, 1, :, :], lambda k: W32[0][:, 1, k, :], bank[4][:, :], "o_m2")


_INS = ['x', 'src', 'dst', 'L0_gnn_Ws', 'L0_gnn_Wb', 'L0_gnn_a_w', 'L0_gnn_a_b', 'L0_ffn_Wg', 'L0_ffn_bg',
        'L0_ffn_We', 'L0_ffn_be', 'L1_gnn_W', 'L1_gnn_b', 'L1_ffn_Wr', 'L1_ffn_br', 'L1_ffn_W1', 'L1_ffn_b1',
        'L1_ffn_W2', 'L1_ffn_b2']


def kernel(**inputs):
    import concourse.bacc as _bacc
    from concourse.bass_utils import run_bass_kernel_spmd as _run

    nc = _bacc.Bacc("TRN2", target_bir_lowering=False, num_devices=1)
    arrays, args = {}, []
    for name in _INS:
        a = np.ascontiguousarray(inputs[name])
        arrays[f"in_{name}"] = a
        args.append(nc.dram_tensor(f"in_{name}", a.shape, mybir.dt.from_np(a.dtype), kind="ExternalInput").ap())
    args.append(nc.dram_tensor("out", (NODES, D), F32, kind="ExternalOutput").ap())
    gnn_ffn_kernel(nc, *args)
    r = _run(nc, [arrays], core_ids=[0])
    return r.results[0]["out"]
```
